# Optimizing a Trainium2 kernel written in Bass

```python
import numpy as np
import jax
import jax.numpy as jnp

def _softmax(x, axis=-1):
    return jax.nn.softmax(x, axis=axis)

def _gelu(x):
    return jax.nn.gelu(x, approximate=True)

def _silu(x):
    return jax.nn.silu(x)

def _sigmoid(x):
    return jax.nn.sigmoid(x)

def _layernorm(x, axis=-1, eps=1e-05):
    m = jnp.mean(x, axis=axis, keepdims=True)
    v = jnp.var(x, axis=axis, keepdims=True)
    return (x - m) / jnp.sqrt(v + eps)

def _scatter_add(tgt, idx, src, axis=0):
    return tgt.at[idx].add(src)

def _segment_sum(src, seg, n):
    return jax.ops.segment_sum(src, seg, n)
kernel_name = 'mk_xattn_ffn_d1_seqx_r8_259e78'

def setup_inputs(seed: int=0):
    np.random.seed(seed)
    _w = jnp.asarray

    def _rec_inputs():
        import jax
        import jax.numpy as jnp
        _rk = jax.random.key(seed)
        x = -0.0002928 + 1 * jax.random.normal(jax.random.fold_in(_rk, 1), (4, 512, 128), jnp.float32)
        _lenS = 512 - jax.random.randint(jax.random.fold_in(_rk, 7), (4,), 0, max(1, 512 // 4) + 1, jnp.int32)
        _lenS2 = 32 - jax.random.randint(jax.random.fold_in(_rk, 8), (4,), 0, max(1, 32 // 4) + 1, jnp.int32)
        _ctx_1024P = jax.random.normal(jax.random.fold_in(_rk, 11), (4, 16, 128), jnp.float32)
        _ctx_1024c = jax.random.dirichlet(jax.random.fold_in(_rk, 511), 0.3 * jnp.ones((16,), jnp.float32), (4, 32))
        _ctx_1024t = jnp.einsum('bsk,bkd->bsd', _ctx_1024c, _ctx_1024P)
        _ctx_1024t = _ctx_1024t * jax.lax.rsqrt(jnp.mean(jnp.square(_ctx_1024t)) + 1e-12) * 0.953939
        ctx_1024 = 0.000227908 + 0.99994 * (_ctx_1024t + 0.3 * jax.random.normal(jax.random.fold_in(_rk, 611), (4, 32, 128), jnp.float32))
        return (x, ctx_1024)
    x, ctx_1024 = _rec_inputs()

    def _L0_xattn_setup():
        import jax, jax.numpy as jnp
        import numpy as np
        HEADS = 16
        key = jax.random.key(seed)
        ks = jax.random.split(key, 6)
        b, n, m, dim = (2, 256, 64, 128)
        s = dim ** (-0.5)
        return {'x': jax.random.normal(ks[0], (b, n, dim), jnp.float32), 'mem': jax.random.normal(ks[1], (b, m, dim), jnp.float32), 'Wq': jax.random.normal(ks[2], (dim, dim), jnp.float32) * s, 'Wkv': jax.random.normal(ks[3], (dim, 2 * dim), jnp.float32) * s, 'Wout': jax.random.normal(ks[4], (dim, dim), jnp.float32) * s, 'bout': jnp.zeros((dim,), jnp.float32)}
    _L0_xattn_all = _L0_xattn_setup()
    _L0_xattn_in = {k: v for k, v in _L0_xattn_all.items() if k in ('Wq', 'Wkv', 'Wout', 'bout')}
    del _L0_xattn_all

    def _L0_ffn_setup():
        import jax, jax.numpy as jnp
        import numpy as np
        B, L, D = (4, 256, 128)
        H = 16
        E = 16
        NS = 16
        S = NS // E
        F = 512
        EPS = 1e-05

        def _layernorm(x, g, b):
            mu = jnp.mean(x, axis=-1, keepdims=True)
            var = jnp.mean(jnp.square(x - mu), axis=-1, keepdims=True)
            return (x - mu) * jax.lax.rsqrt(var + EPS) * g + b

        def _mha(q, k, v, Wq, bq, Wk, bk, Wv, bv, Wo, bo):
            Bq, Lq, Dm = q.shape
            dh = Dm // H
            qh = (q @ Wq + bq).reshape(Bq, Lq, H, dh)
            kh = (k @ Wk + bk).reshape(Bq, -1, H, dh)
            vh = (v @ Wv + bv).reshape(Bq, -1, H, dh)
            scores = jnp.einsum('bqhd,bkhd->bhqk', qh, kh) / jnp.asarray(np.sqrt(dh), q.dtype)
            attn = jax.nn.softmax(scores, axis=-1)
            out = jnp.einsum('bhqk,bkhd->bqhd', attn, vh).reshape(Bq, Lq, Dm)
            return out @ Wo + bo
        key = jax.random.key(seed)
        ks = jax.random.split(key, 32)
        s = 0.02
        d = {}
        d['x'] = jax.random.normal(ks[0], (B, L, D), jnp.float32)
        d['slot_query'] = jax.random.normal(ks[1], (1, NS, D), jnp.float32) * 0.01
        for i, nm in enumerate(['d_Wq', 'd_Wk', 'd_Wv', 'd_Wo']):
            d[nm] = jax.random.normal(ks[2 + i], (D, D), jnp.float32) * s
        for nm in ['d_bq', 'd_bk', 'd_bv', 'd_bo']:
            d[nm] = jnp.zeros((D,), jnp.float32)
        for i, nm in enumerate(['c_Wq', 'c_Wk', 'c_Wv', 'c_Wo']):
            d[nm] = jax.random.normal(ks[6 + i], (D, D), jnp.float32) * s
        for nm in ['c_bq', 'c_bk', 'c_bv', 'c_bo']:
            d[nm] = jnp.zeros((D,), jnp.float32)
        d['e_ln_g'] = jnp.ones((E, D), jnp.float32)
        d['e_ln_b'] = jnp.zeros((E, D), jnp.float32)
        d['e_W1'] = jax.random.normal(ks[10], (E, D, F), jnp.float32) * s
        d['e_b1'] = jnp.zeros((E, F), jnp.float32)
        d['e_Wg'] = jax.random.normal(ks[11], (E, D, F), jnp.float32) * s
        d['e_bg'] = jnp.zeros((E, F), jnp.float32)
        d['e_W2'] = jax.random.normal(ks[12], (E, F, D), jnp.float32) * s
        d['e_b2'] = jnp.zeros((E, D), jnp.float32)
        return d
    _L0_ffn_all = _L0_ffn_setup()
    _L0_ffn_in = {k: v for k, v in _L0_ffn_all.items() if k in ('slot_query', 'd_Wq', 'd_Wk', 'd_Wv', 'd_Wo', 'd_bq', 'd_bk', 'd_bv', 'd_bo', 'c_Wq', 'c_Wk', 'c_Wv', 'c_Wo', 'c_bq', 'c_bk', 'c_bv', 'c_bo', 'e_ln_g', 'e_ln_b', 'e_W1', 'e_b1', 'e_Wg', 'e_bg', 'e_W2', 'e_b2')}
    del _L0_ffn_all
    return {'x': x, 'ctx_1024': ctx_1024, 'L0_xattn_Wq': _L0_xattn_in['Wq'], 'L0_xattn_Wkv': _L0_xattn_in['Wkv'], 'L0_xattn_Wout': _L0_xattn_in['Wout'], 'L0_xattn_bout': _L0_xattn_in['bout'], 'L0_ffn_slot_query': _L0_ffn_in['slot_query'], 'L0_ffn_d_Wq': _L0_ffn_in['d_Wq'], 'L0_ffn_d_Wk': _L0_ffn_in['d_Wk'], 'L0_ffn_d_Wv': _L0_ffn_in['d_Wv'], 'L0_ffn_d_Wo': _L0_ffn_in['d_Wo'], 'L0_ffn_d_bq': _L0_ffn_in['d_bq'], 'L0_ffn_d_bk': _L0_ffn_in['d_bk'], 'L0_ffn_d_bv': _L0_ffn_in['d_bv'], 'L0_ffn_d_bo': _L0_ffn_in['d_bo'], 'L0_ffn_c_Wq': _L0_ffn_in['c_Wq'], 'L0_ffn_c_Wk': _L0_ffn_in['c_Wk'], 'L0_ffn_c_Wv': _L0_ffn_in['c_Wv'], 'L0_ffn_c_Wo': _L0_ffn_in['c_Wo'], 'L0_ffn_c_bq': _L0_ffn_in['c_bq'], 'L0_ffn_c_bk': _L0_ffn_in['c_bk'], 'L0_ffn_c_bv': _L0_ffn_in['c_bv'], 'L0_ffn_c_bo': _L0_ffn_in['c_bo'], 'L0_ffn_e_ln_g': _L0_ffn_in['e_ln_g'], 'L0_ffn_e_ln_b': _L0_ffn_in['e_ln_b'], 'L0_ffn_e_W1': _L0_ffn_in['e_W1'], 'L0_ffn_e_b1': _L0_ffn_in['e_b1'], 'L0_ffn_e_Wg': _L0_ffn_in['e_Wg'], 'L0_ffn_e_bg': _L0_ffn_in['e_bg'], 'L0_ffn_e_W2': _L0_ffn_in['e_W2'], 'L0_ffn_e_b2': _L0_ffn_in['e_b2']}

def reference(x, ctx_1024, L0_xattn_Wq, L0_xattn_Wkv, L0_xattn_Wout, L0_xattn_bout, L0_ffn_slot_query, L0_ffn_d_Wq, L0_ffn_d_Wk, L0_ffn_d_Wv, L0_ffn_d_Wo, L0_ffn_d_bq, L0_ffn_d_bk, L0_ffn_d_bv, L0_ffn_d_bo, L0_ffn_c_Wq, L0_ffn_c_Wk, L0_ffn_c_Wv, L0_ffn_c_Wo, L0_ffn_c_bq, L0_ffn_c_bk, L0_ffn_c_bv, L0_ffn_c_bo, L0_ffn_e_ln_g, L0_ffn_e_ln_b, L0_ffn_e_W1, L0_ffn_e_b1, L0_ffn_e_Wg, L0_ffn_e_bg, L0_ffn_e_W2, L0_ffn_e_b2):
    import jax
    import jax.numpy as jnp

    def _L0_xattn_ref(x, mem, Wq, Wkv, Wout, bout):
        import jax, jax.numpy as jnp
        import numpy as np
        HEADS = 16
        b, n, dim = x.shape
        h = HEADS
        d = dim // h
        scale = d ** (-0.5)
        mem_len = mem.shape[1]
        q = x @ Wq
        xc = jnp.concatenate((mem, x), axis=1)
        kv = xc @ Wkv
        k, v = jnp.split(kv, 2, axis=-1)

        def to_heads(t):
            bb, nn, _ = t.shape
            return t.reshape(bb, nn, h, d).transpose(0, 2, 1, 3)
        q, k, v = (to_heads(q), to_heads(k), to_heads(v))
        dots = jnp.einsum('bhid,bhjd->bhij', q, k) * scale
        j = dots.shape[-1]
        i_idx = jnp.arange(n)[:, None]
        j_idx = jnp.arange(j)[None, :]
        mask = j_idx > i_idx + mem_len
        dots = jnp.where(mask[None, None], -jnp.inf, dots)
        attn = jax.nn.softmax(dots, axis=-1)
        out = jnp.einsum('bhij,bhjd->bhid', attn, v)
        out = out.transpose(0, 2, 1, 3).reshape(b, n, dim)
        return out @ Wout + bout

    def _L0_ffn_ref(x, slot_query, d_Wq, d_Wk, d_Wv, d_Wo, d_bq, d_bk, d_bv, d_bo, c_Wq, c_Wk, c_Wv, c_Wo, c_bq, c_bk, c_bv, c_bo, e_ln_g, e_ln_b, e_W1, e_b1, e_Wg, e_bg, e_W2, e_b2):
        import jax, jax.numpy as jnp
        import numpy as np
        B, L, D = (4, 256, 128)
        H = 16
        E = 16
        NS = 16
        S = NS // E
        F = 512
        EPS = 1e-05

        def _layernorm(x, g, b):
            mu = jnp.mean(x, axis=-1, keepdims=True)
            var = jnp.mean(jnp.square(x - mu), axis=-1, keepdims=True)
            return (x - mu) * jax.lax.rsqrt(var + EPS) * g + b

        def _mha(q, k, v, Wq, bq, Wk, bk, Wv, bv, Wo, bo):
            Bq, Lq, Dm = q.shape
            dh = Dm // H
            qh = (q @ Wq + bq).reshape(Bq, Lq, H, dh)
            kh = (k @ Wk + bk).reshape(Bq, -1, H, dh)
            vh = (v @ Wv + bv).reshape(Bq, -1, H, dh)
            scores = jnp.einsum('bqhd,bkhd->bhqk', qh, kh) / jnp.asarray(np.sqrt(dh), q.dtype)
            attn = jax.nn.softmax(scores, axis=-1)
            out = jnp.einsum('bhqk,bkhd->bqhd', attn, vh).reshape(Bq, Lq, Dm)
            return out @ Wo + bo
        Bx = x.shape[0]
        q = jnp.broadcast_to(slot_query, (Bx, NS, D))
        o = q + _mha(q, x, x, d_Wq, d_bq, d_Wk, d_bk, d_Wv, d_bv, d_Wo, d_bo)
        os = o.reshape(Bx, E, S, D)
        h = _layernorm(os, e_ln_g[None, :, None, :], e_ln_b[None, :, None, :])
        u = jax.nn.silu(jnp.einsum('besd,edf->besf', h, e_W1) + e_b1[None, :, None, :])
        g = jax.nn.silu(jnp.einsum('besd,edf->besf', h, e_Wg) + e_bg[None, :, None, :])
        y = jnp.einsum('besf,efd->besd', u * g, e_W2) + e_b2[None, :, None, :]
        o = o + y.reshape(Bx, NS, D)
        out = _mha(x, o, o, c_Wq, c_bq, c_Wk, c_bk, c_Wv, c_bv, c_Wo, c_bo)
        return out
    x = x + _L0_xattn_ref(_layernorm(x, axis=-1), ctx_1024, L0_xattn_Wq, L0_xattn_Wkv, L0_xattn_Wout, L0_xattn_bout)
    x = x + _L0_ffn_ref(_layernorm(x, axis=-1), L0_ffn_slot_query, L0_ffn_d_Wq, L0_ffn_d_Wk, L0_ffn_d_Wv, L0_ffn_d_Wo, L0_ffn_d_bq, L0_ffn_d_bk, L0_ffn_d_bv, L0_ffn_d_bo, L0_ffn_c_Wq, L0_ffn_c_Wk, L0_ffn_c_Wv, L0_ffn_c_Wo, L0_ffn_c_bq, L0_ffn_c_bk, L0_ffn_c_bv, L0_ffn_c_bo, L0_ffn_e_ln_g, L0_ffn_e_ln_b, L0_ffn_e_W1, L0_ffn_e_b1, L0_ffn_e_Wg, L0_ffn_e_bg, L0_ffn_e_W2, L0_ffn_e_b2)
    return x

_drawn_inputs = setup_inputs


def setup_inputs(seed=0):
    import zlib

    import numpy as np

    out = dict(_drawn_inputs(seed))
    spreads = {'L0_xattn_bout': (0.0, 0.1),
     'L0_ffn_d_bq': (0.0, 0.8),
     'L0_ffn_d_bk': (0.0, 2.0),
     'L0_ffn_d_bv': (0.0, 0.8),
     'L0_ffn_d_bo': (0.0, 0.8),
     'L0_ffn_c_bq': (0.0, 0.8),
     'L0_ffn_c_bk': (0.0, 2.0),
     'L0_ffn_c_bv': (0.0, 2.0),
     'L0_ffn_c_bo': (0.0, 2.0),
     'L0_ffn_e_ln_g': (1.0, 0.6),
     'L0_ffn_e_ln_b': (0.0, 0.8),
     'L0_ffn_e_b1': (0.0, 0.8),
     'L0_ffn_e_bg': (0.0, 0.8),
     'L0_ffn_e_b2': (0.0, 0.8)}
    factors = {'L0_ffn_slot_query': 8.0,
     'L0_ffn_d_Wq': 8.0,
     'L0_ffn_d_Wk': 8.0,
     'L0_ffn_d_Wv': 8.0,
     'L0_ffn_d_Wo': 8.0,
     'L0_ffn_c_Wq': 8.0,
     'L0_ffn_c_Wk': 8.0,
     'L0_ffn_c_Wv': 8.0,
     'L0_ffn_c_Wo': 2.989,
     'L0_ffn_e_W1': 8.0,
     'L0_ffn_e_Wg': 8.0,
     'L0_ffn_e_W2': 8.0}
    for name, (base, spread) in spreads.items():
        noise = np.random.default_rng([zlib.crc32(name.encode()), seed]).standard_normal(out[name].shape)
        drawn = base * np.exp(spread * noise) if base else spread * noise
        out[name] = jnp.asarray(drawn.astype(out[name].dtype))
    for name, factor in factors.items():
        out[name] = (out[name] * factor).astype(out[name].dtype)
    return out
```

```python
from contextlib import ExitStack

import concourse.bass as bass
from concourse import mybir

F32 = mybir.dt.float32
BF16 = mybir.dt.bfloat16
ALU = mybir.AluOpType
ACT = mybir.ActivationFunctionType
AX = mybir.AxisListType

P = 128
B = 4
T = 512
NT = T // P
D = 128
H = 16
DH = D // H
MEM = 32
KEYS = MEM + T
S = 16
F = 512
FC = F // P
EPS = 1e-5
SCALE = DH ** -0.5
BIG = -1.0e30

HG = 4
NGB = H // HG
NGROUPS = B * NGB
LEAD = 2
TICKS = 14
UNITS = 11
Q_TERMS = [0, 0, 1, 1, 2, 0]
K_TERMS = [0, 1, 0, 1, 0, 2]
SHIFT_ROW = DH * len(Q_TERMS)
SLOTS = NGROUPS + 2

A_STATS, A_RSTD, A_NORM, A_T, A_Q, A_SPLITQ, A_K, A_SPLITK, A_V, A_VM = 0, 4, 5, 7, 9, 10, 12, 13, 15, 17
SHIFT_TICK = 2
(P_TOK, P_ATT, P_OUT, P_STATS, P_RSTD, P_NORM, P_T, P_QC, P_KD, P_VD, P_SD, P_PT, P_PV, P_SUM) = (
    0, 4, 5, 6, 7, 8, 9, 10, 11, 12, 13, 17, 20, 23)


def projection_step(slot, tick):
    b = slot // NGB + 1
    return (b, slot % NGB * TICKS + tick) if b < B else (None, -1)


def finish_step(slot, tick):
    at = slot - NGB - 1
    return (at // NGB, at % NGB * TICKS + tick) if at >= 0 and at // NGB < B - 1 else (None, -1)


PROJ_USES = {A_T: "xnT", A_Q: "q", A_K: "k", A_V: "v", A_VM: "vmem"}


def count_uses():
    first = ["ctxT", "slotT", "kmem", "slotq"] + [(0, n) for n in PROJ_USES.values()] + [("shift", 0), ("shift", 1)]
    second = []
    for slot in range(SLOTS):
        for tick in range(TICKS):
            if tick == SHIFT_TICK and slot >= 1 and slot - 1 + LEAD < NGROUPS:
                first.append(("shift", slot - 1 + LEAD))
            b, n = projection_step(slot, tick)
            if n in PROJ_USES:
                first.append((b, PROJ_USES[n]))
            b, n = finish_step(slot, tick)
            second += finish_uses(b, n)
    for n in range(P_SUM + 1):
        second += finish_uses(B - 1, n)
    return {n: i for i, n in enumerate(first)}, {n: i for i, n in enumerate(second)}


def finish_uses(b, n):
    if P_TOK <= n < P_TOK + NT:
        return [(b, "tok", n - P_TOK)]
    if n in (P_PT, P_PT + 1):
        return [(b, "pT", n - P_PT)]
    if n in (P_PV, P_PV + 1):
        return [(b, "pv", n - P_PV)]
    if n in (P_SD, P_SD + 2):
        return [(b, "sd", (n - P_SD) // 2)]
    one = {P_ATT: "att", P_OUT: "out", P_T: "xn2T", P_QC: "qc", P_KD: "kd", P_VD: "vd", P_SUM: "sum"}
    return [(b, one[n])] if n in one else []


AREA0, AREA1 = count_uses()
CAUSAL_MADE = 6
CONSTS_MADE = CAUSAL_MADE + 7 + P // S


def program(nc, i, out):
    with ExitStack() as ctx:
        def sb(name, shape, dt=F32):
            return ctx.enter_context(nc.sbuf_tensor(name, shape, dt))

        def ps(name, shape, dt=F32):
            return ctx.enter_context(nc.psum_tensor(name, shape, dt))

        def sem(name):
            return ctx.enter_context(nc.semaphore(name))

        score_bank = [ps(f"score_bank{n}", [P, 512]) for n in range(3)]
        scoreT_bank = [ps(f"scoreT_bank{n}", [P, 512]) for n in range(2)]
        pv_bank = ps("pv_bank", [P, 512])
        area0 = ps("area0", [P, 512])
        area1 = ps("area1", [P, 512])

        x = sb("x", [P, B, NT, D])
        xn = sb("xn", [P, NT, D])
        xnT = sb("xnT", [P, T])
        ctx_in = sb("ctx_in", [P, D])
        ctxT = sb("ctxT", [P, B, HG, MEM])
        wq_cols = sb("wq_cols", [P, D])
        wk_cols = sb("wk_cols", [P, D])
        wq = sb("wq", [P, D])
        wkv = sb("wkv", [P, 2 * D])
        wout = sb("wout", [P, D])
        dw = {n: sb(f"dw_{n}", [P, D]) for n in "qkvo"}
        cw = {n: sb(f"cw_{n}", [P, D]) for n in "qkvo"}
        db = {n: sb(f"db_{n}", [P, 1]) for n in "qkv"}
        cb = {n: sb(f"cb_{n}", [P, 1]) for n in "qkv"}
        bout_row = sb("bout_row", [P, D])
        cbo_row = sb("cbo_row", [P, D])
        dbo_row = sb("dbo_row", [B * S, D])
        slot_rows = sb("slot_rows", [B * S, D])
        slots = sb("slots", [S, D])
        ln_g = sb("ln_g", [B * S, D])
        ln_b = sb("ln_b", [B * S, D])
        b2_rows = sb("b2_rows", [B * S, D])

        ident = sb("ident", [P, P])
        identb = sb("identb", [P, P], BF16)
        causal = sb("causal", [P, P], BF16)
        head_of = sb("head_of", [P, H])
        slot_head = sb("slot_head", [P, 2, H])
        slot_sel = sb("slot_sel", [P, S])
        zero_rows = sb("zero_rows", [P, T], BF16)
        one_rows = sb("one_rows", [S, KEYS], BF16)
        slotsT = sb("slotsT", [P, S])

        stats = sb("stats", [P, NT, 6])
        mv = sb("mv", [P, NT, 2])
        rstd = sb("rstd", [P, NT])
        vare = sb("vare", [P, NT])
        mhalf = sb("mhalf", [P, NT])
        stats2 = sb("stats2", [P, NT, 6])
        mv2 = sb("mv2", [P, NT, 2])
        rstd2 = sb("rstd2", [P, NT])
        vare2 = sb("vare2", [P, NT])

        qp = sb("qp", [P, 3, T], BF16)
        kp = sb("kp", [P, 3, KEYS], BF16)
        kmem = sb("kmem", [P, 3, B * MEM], BF16)
        res = sb("res", [P, T])
        resk = sb("resk", [P, T])
        q_stack = [sb(f"q_stack{n}", [P, H // 2, T], BF16) for n in range(2)]
        k_stack = [sb(f"k_stack{n}", [P, H, KEYS], BF16) for n in range(2)]
        v_aug = [sb(f"v_aug{n}", [P, NT, H, DH + 1]) for n in range(2)]
        v_mem = [sb(f"v_mem{n}", [P, NGB, P]) for n in range(2)]
        rowmax = [sb(f"rowmax{n}", [P, NT, 2, 2]) for n in range(2)]
        tailmax = [sb(f"tailmax{n}", [P, 2, 2]) for n in range(2)]
        shift = [sb(f"shift{n}", [P, NT, 2, 2, 2], BF16) for n in range(2)]
        shiftT = [sb(f"shiftT{n}", [8, T], BF16) for n in range(2)]
        probs = [sb(f"probs{n}", [P, UNITS, 512]) for n in range(2)]
        oT = sb("oT", [P, NGB, T])
        rden = sb("rden", [P, H])
        att = sb("att", [P, NT, D])
        attT = sb("attT", [P, T])
        xn2 = att
        xn2T = attT
        qcT = sb("qcT", [P, B, T])
        kdT = sb("kdT", [P, T])
        vd = sb("vd", [P, NT, D])
        qd_heads = sb("qd_heads", [P, H, S])
        qdT = sb("qdT", [P, S])
        sd_max = sb("sd_max", [P, 2])
        sd_sum = sb("sd_sum", [P, 2])
        sd_r = sb("sd_r", [P, 2])
        pd = sb("pd", [P, 2, T])
        pdT = sb("pdT", [P, 2, T])
        od = sb("od", [P, 2, D])
        adT = sb("adT", [P, B, S])
        w1_early = sb("w1_early", [P, 12, F])
        k0 = k_stack[0][:, :, :].rearrange("p h n -> p (h n)").bitcast(F32)
        k1 = k_stack[1][:, :, :].rearrange("p h n -> p (h n)").bitcast(F32)
        q0 = q_stack[0][:, :, :].rearrange("p h n -> p (h n)").bitcast(F32)
        q1 = q_stack[1][:, :, :].rearrange("p h n -> p (h n)").bitcast(F32)
        late1 = k1[:, 0:4 * F].rearrange("p (e f) -> p e f", f=F)
        lateg = k1[:, 4 * F:8 * F].rearrange("p (e f) -> p e f", f=F)
        midg0 = k0[:, 0:8 * F].rearrange("p (e f) -> p e f", f=F)
        midg1 = q0[:, 0:4 * F].rearrange("p (e f) -> p e f", f=F)
        w1 = [w1_early[:, e, :] if e < 12 else late1[:, e - 12, :] for e in range(S)]
        wg = [midg0[:, e, :] if e < 8 else midg1[:, e - 8, :] if e < 12 else lateg[:, e - 12, :] for e in range(S)]
        w2 = [probs[e // 8][:, e % 8, :].rearrange("p (c d) -> p c d", d=D) for e in range(S)]
        b1_rows = oT[:, :, :]
        bg_rows = q1.rearrange("p (g n) -> p g n", g=NGB)
        hT = probs[0][:, 8, :].rearrange("p (e c) -> p e c", c=32)
        uvT = [probs[0][:, 9, :], probs[0][:, 10, :]]
        ub = [probs[1][:, 8, :], probs[1][:, 9, :]]
        gb = [probs[1][:, 10, :], res[:, :]]
        uv = [resk[:, :], qp[:, 0:2, :].rearrange("p a n -> p (a n)").bitcast(F32)]
        ysb = xn[:, :, :].rearrange("p t d -> p (t d)")
        kc_heads = pd[:, :, :].rearrange("p c n -> p (c n)").rearrange("p (b h s) -> p b h s", b=B, h=H)
        vc_heads = pdT[:, :, :].rearrange("p c n -> p (c n)").rearrange("p (b h s) -> p b h s", b=B, h=H)
        vo = k0[:, 0:1024].rearrange("p (b c d) -> p b c d", b=B, c=2)
        o_rows = sb("o_rows", [B * S, D])
        o_T = sb("o_T", [P, B * S])
        o_stats = sb("o_stats", [B * S, 6])
        o_mv = sb("o_mv", [B * S, 2])
        h_rows = sb("h_rows", [B * S, D])
        o2T = sb("o2T", [P, B, S])
        kcT = sb("kcT", [P, B, S])
        vcT = sb("vcT", [P, B, S])
        c_max = [sb(f"c_max{n}", [P, 2 * H]) for n in range(2)]
        c_sum = [sb(f"c_sum{n}", [P, 2 * H]) for n in range(2)]
        oT_flat = oT[:, :, :]
        c_exp = [oT_flat[:, 0, :], oT_flat[:, 1, :]]
        c_prob = [oT_flat[:, 2, :], oT_flat[:, 3, :]]
        c_probT = [xnT[:, :], kdT[:, :]]
        y = vd[:, :, :].rearrange("p (a t) d -> p a t d", a=2)

        names = ("x_in0 x_in1 attn_w_in ctx_in_sem slot_w_in rows_in w1_in wg_in w2_in b1_in out_done consts pool_const "
                 "stats_done rstd_done vare_done norm_done area0_filled area0_drained area1_filled area1_drained "
                 "q_first k_first res_done q_second q_third mem_copied kmem_part v_ready scores_ready scores_reduced max_chain "
                 "scoreT_ready exp_done diag_done pv_done oT_copied shift_row slotq_done qd_done "
                 "x_plus stats2_done rstd2_done vare2_done norm2_done rden_done sd_chain sd_exp od_done sum_copied "
                 "o_chain o_pool hT_copied hT_zeroed oh_ready kzero_done x_b tile_stats tile_stats2 v_zero c_summing cols_done up_ready silu_in silu_done uv_done uvT_ready uvT_copied y_ready y_copied "
                 "yT_ready o2_done kcT_ready kcT_copied kheads_done vheads_done vo_ready vo_copied c_scored c_reduced c_shifted "
                 "c_exped c_summed c_normed c_transposed c_copied c_mixed y_done").split()
        s = {n: sem(n) for n in names}
        (x_in0, x_in1, attn_w_in, ctx_in_sem, slot_w_in, rows_in, w1_in, wg_in, w2_in, b1_in, out_done, consts, pool_const,
         stats_done, rstd_done, vare_done, norm_done, area0_filled, area0_drained, area1_filled, area1_drained,
         q_first, k_first, res_done, q_second, q_third, mem_copied, kmem_part, v_ready, scores_ready, scores_reduced,
         max_chain, scoreT_ready, exp_done, diag_done, pv_done, oT_copied, shift_row, slotq_done, qd_done,
         x_plus, stats2_done, rstd2_done, vare2_done, norm2_done, rden_done, sd_chain, sd_exp, od_done, sum_copied,
         o_chain, o_pool, hT_copied, hT_zeroed, oh_ready, kzero_done, x_b, tile_stats, tile_stats2, v_zero, c_summing, cols_done, up_ready, silu_in, silu_done, uv_done, uvT_ready, uvT_copied, y_ready, y_copied,
         yT_ready, o2_done, kcT_ready, kcT_copied, kheads_done, vheads_done, vo_ready, vo_copied, c_scored, c_reduced,
         c_shifted, c_exped, c_summed, c_normed, c_transposed, c_copied, c_mixed, y_done) = (s[n] for n in names)
        out_sent = [sem(f"out_sent{n}") for n in range(2)]
        stack_init = sem("stack_init")
        q_stacked = [sem(f"q_stacked{b}") for b in range(B)]
        k_stacked = [sem(f"k_stacked{b}") for b in range(B)]
        shift_in = [sem(f"shift_in{n}") for n in range(2)]

        NQ_DMA = 16 * (2 * len(Q_TERMS) + 2)
        NK_DMA = 16 * (2 * len(K_TERMS))

        def wait_area(eng, sem_drained, n):
            if n:
                eng.wait_ge(sem_drained, n)

        def unit_of_scores(group, k):
            if k < 2:
                return 0, [2 * k, 2 * k + 1]
            return (k - 2) // 4 + 1, [(k - 2) % 4]

        def scores_cols(tile):
            return min(MEM + P * (tile + 1), 512)

        block = ctx.enter_context(nc.Block())

        @block.sync
        def _(sp):
            for b in range(B):
                sp.dma_start(x[:, b, :, :], i["x"][b].rearrange("(t p) d -> p t d", p=P)).then_inc(
                    x_in0 if b == 0 else x_in1, 16)
                if b == 0:
                    sp.dma_start(ctx_in[:, :], i["ctx_1024"].rearrange("b m d -> (b m) d")).then_inc(ctx_in_sem, 16)
                    sp.dma_start(wq[:, :], i["L0_xattn_Wq"]).then_inc(attn_w_in, 16)
                    sp.dma_start(wkv[:, :], i["L0_xattn_Wkv"]).then_inc(attn_w_in, 16)
            sp.dma_start(slots[:, :], i["L0_ffn_slot_query"][0]).then_inc(slot_w_in, 16)
            sp.dma_start(wout[:, :], i["L0_xattn_Wout"]).then_inc(slot_w_in, 16)
            for n in "qkvo":
                sp.dma_start(dw[n][:, :], i[f"L0_ffn_d_W{n}"]).then_inc(slot_w_in, 16)
                sp.dma_start(cw[n][:, :], i[f"L0_ffn_c_W{n}"]).then_inc(slot_w_in, 16)
            for n in "qkv":
                sp.dma_start(db[n][:, :], i[f"L0_ffn_d_b{n}"].rearrange("(d o) -> d o", o=1)).then_inc(slot_w_in, 16)
                sp.dma_start(cb[n][:, :], i[f"L0_ffn_c_b{n}"].rearrange("(d o) -> d o", o=1)).then_inc(slot_w_in, 16)
            sp.dma_start(bout_row[:, :], i["L0_xattn_bout"].partition_broadcast(P)).then_inc(rows_in, 16)
            sp.dma_start(cbo_row[:, :], i["L0_ffn_c_bo"].partition_broadcast(P)).then_inc(rows_in, 16)
            sp.dma_start(dbo_row[:, :], i["L0_ffn_d_bo"].partition_broadcast(B * S)).then_inc(rows_in, 16)
            for b in range(B):
                rows = slice(S * b, S * (b + 1))
                sp.dma_start(slot_rows[rows, :], i["L0_ffn_slot_query"][0]).then_inc(rows_in, 16)
                sp.dma_start(ln_g[rows, :], i["L0_ffn_e_ln_g"]).then_inc(rows_in, 16)
                sp.dma_start(ln_b[rows, :], i["L0_ffn_e_ln_b"]).then_inc(rows_in, 16)
                sp.dma_start(b2_rows[rows, :], i["L0_ffn_e_b2"]).then_inc(rows_in, 16)

            def stack(b):
                if b >= 2:
                    sp.wait_ge(scoreT_ready, UNITS * NGB * (b - 1))
                if b == 0:
                    sp.wait_ge(consts, 2)
                for g in range(2):
                    sp.dma_start(q_stack[b % 2][64 * g + SHIFT_ROW:64 * g + 64, :, :],
                                 zero_rows[:, :]).then_inc(q_stacked[b], 16)
                if b < 2:
                    sp.wait_ge(kzero_done, b + 1)
                    for g in range(2):
                        sp.dma_start(k_stack[b][64 * g + SHIFT_ROW:64 * g + SHIFT_ROW + 2, g::2, :],
                                     one_rows[:, :]).then_inc(stack_init, 16)
                sp.wait_ge(q_first, b + 1)
                sp.wait_ge(q_third, 2 * b + 1)
                for t, part in enumerate(Q_TERMS):
                    for g in range(2):
                        sp.dma_start(q_stack[b % 2][64 * g + DH * t:64 * g + DH * (t + 1), :, :],
                                     qp[64 * g:64 * (g + 1), part, :]).then_inc(q_stacked[b], 16)
                sp.wait_ge(k_first, b + 1)
                sp.wait_ge(q_third, 2 * b + 2)
                sp.wait_ge(mem_copied, b + 1)
                for t, part in enumerate(K_TERMS):
                    for g in range(2):
                        sp.dma_start(k_stack[b % 2][64 * g + DH * t:64 * g + DH * (t + 1), g::2, :],
                                     kp[64 * g:64 * (g + 1), part, :]).then_inc(k_stacked[b], 16)

            def shift_rows(group):
                sp.wait_ge(area0_drained, AREA0[("shift", group)] + 1)
                b, gl = divmod(group, NGB)
                for g in range(2):
                    sp.dma_start(q_stack[b % 2][64 * g + SHIFT_ROW:64 * g + SHIFT_ROW + 2, 2 * gl:2 * gl + 2, :],
                                 shiftT[group % 2][4 * g:4 * g + 4, :]).then_inc(shift_in[group % 2], 16)

            stack(0)
            for group in range(LEAD):
                shift_rows(group)
            for slot in range(NGROUPS):
                if slot >= 1 and slot - 1 + LEAD < NGROUPS:
                    shift_rows(slot - 1 + LEAD)
                if slot % NGB == 1 and slot // NGB + 1 < B:
                    stack(slot // NGB + 1)
                if slot < 12:
                    sp.dma_start(w1[slot], i["L0_ffn_e_W1"][slot]).then_inc(w1_in, 16)
                else:
                    if slot == 12:
                        sp.wait_ge(scoreT_ready, UNITS * 12)
                    for e in range(3 * (slot - 12), 3 * (slot - 12) + 3):
                        sp.dma_start(wg[e], i["L0_ffn_e_Wg"][e]).then_inc(wg_in, 16)
            sp.wait_ge(scoreT_ready, UNITS * NGROUPS)
            for e in range(12, S):
                sp.dma_start(w1[e], i["L0_ffn_e_W1"][e]).then_inc(w1_in, 16)
                sp.dma_start(wg[e], i["L0_ffn_e_Wg"][e]).then_inc(wg_in, 16)
            for dst, name in ((bg_rows, "L0_ffn_e_bg"), (b1_rows, "L0_ffn_e_b1")):
                if name == "L0_ffn_e_b1":
                    sp.wait_ge(pv_done, NGROUPS)
                    for e in range(S):
                        sp.dma_start(w2[e], i["L0_ffn_e_W2"][e].rearrange("(p c) d -> p c d", c=FC)).then_inc(w2_in, 16)
                    sp.wait_ge(area1_filled, AREA1[(B - 1, "tok", NT - 1)] + 1)
                for jj in range(HG):
                    src = i[name].rearrange("(g j) f -> j g f", j=HG)[jj].partition_broadcast(32)
                    sp.dma_start(dst[32 * jj:32 * jj + 32, :, :], src).then_inc(b1_in, 16)
            for pair in range(2 * B):
                sp.wait_ge(y_done, pair + 1)
                b, half = divmod(pair, 2)
                dst = out[b].rearrange("(h t p) d -> h p t d", h=2, p=P)[half]
                sp.dma_start(dst, y[:, pair % 2, :, :]).then_inc(out_sent[pair % 2], 16)
            for n in range(2):
                sp.wait_ge(out_sent[n], 16 * B)

        @block.gpsimd
        def _(pool):
            made = [0]

            def const(ins):
                made[0] += 1
                ins.then_inc(pool_const, 1)
                pool.wait_ge(pool_const, made[0])

            const(nc.gpsimd.memset(mhalf[:, :], -0.5))
            const(nc.gpsimd.memset(ident[:, :], 0.0))
            const(nc.gpsimd.affine_select(out=ident[:, :], in_=ident[:, :], compare_op=ALU.not_equal, fill=1.0,
                                          base=0, pattern=[[-1, P]], channel_multiplier=1))

            def rstd_of(n, done_stats, v, mvs, r, s_v, s_r):
                pool.wait_ge(done_stats, n + 1)
                nc.gpsimd.tensor_scalar(v, mvs, EPS, None, ALU.add).then_inc(s_v, 1)
                pool.wait_ge(s_v, n + 1)
                nc.gpsimd.tensor_tensor(r, v, mhalf[:, :], ALU.pow).then_inc(s_r, 1)

            def cut(n, parts, left, s_stacked):
                pool.wait_ge(res_done, n + 1)
                if s_stacked is not None:
                    pool.wait_ge(s_stacked[0], s_stacked[1])
                nc.gpsimd.tensor_copy(parts[1], left).then_inc(q_second, 1)
                pool.wait_ge(q_second, n + 1)
                nc.gpsimd.tensor_tensor(parts[2], left, parts[1], ALU.subtract).then_inc(q_third, 1)

            def cut_q(b):
                cut(2 * b, (None, qp[:, 1, :], qp[:, 2, :]), res[:, :],
                    (q_stacked[b - 1], NQ_DMA) if b else None)

            def cut_k(b):
                stacked = (k_stacked[b - 1], NK_DMA) if b else None
                cut(2 * b + 1, (None, kp[:, 1, MEM:], kp[:, 2, MEM:]), resk[:, :], stacked)
                pool.wait_ge(kmem_part, 3)
                nc.gpsimd.tensor_copy(kp[:, :, 0:MEM], kmem[:, :, MEM * b:MEM * (b + 1)]).then_inc(mem_copied, 1)

            def diagonal(group, n):
                pr = probs[group % 2]
                pool.wait_ge(exp_done, UNITS * group + (4, 8, 10)[n])
                (lo, hi), cols = (((0, 4), (0,)), ((4, 8), (0, 384)), ((8, 10), (0, 256)))[n]
                for c in cols:
                    v = pr[:, lo:hi, c:c + P]
                    ins = nc.gpsimd.affine_select(out=v, in_=v, compare_op=ALU.is_ge, fill=0.0, base=0,
                                                  pattern=[[0, hi - lo], [1, P]], channel_multiplier=-1)
                ins.then_inc(diag_done, 1)

            def add_row(n, b, row, normalised):
                pool.wait_ge(normalised, b + 1)
                xb = x[:, b, :, :]
                nc.gpsimd.tensor_tensor(xb, xb, row[:, :].unsqueeze(1).broadcast_to([P, NT, D]),
                                        ALU.add).then_inc(n, 1)

            nc.gpsimd.memset(k0.bitcast(mybir.dt.uint32), 0).then_inc(kzero_done, 1)
            const(nc.gpsimd.tensor_copy(identb[:, :], ident[:, :]))
            const(nc.gpsimd.memset(causal[:, :], 0.0))
            const(nc.gpsimd.affine_select(out=causal[:, :], in_=causal[:, :], compare_op=ALU.is_ge, fill=BIG,
                                          base=0, pattern=[[-1, P]], channel_multiplier=1))
            assert made[0] == CAUSAL_MADE
            rstd_of(0, stats_done, vare[:, :], mv[:, :, 1], rstd[:, :], vare_done, rstd_done)
            cut_q(0)
            cut_k(0)
            nc.gpsimd.memset(k1.bitcast(mybir.dt.uint32), 0).then_inc(kzero_done, 1)
            const(nc.gpsimd.memset(head_of[:, :], 1.0))
            const(nc.gpsimd.affine_select(out=head_of[:, :], in_=head_of[:, :], compare_op=ALU.is_ge, fill=0.0,
                                          base=0, pattern=[[-DH, H]], channel_multiplier=1))
            const(nc.gpsimd.affine_select(out=head_of[:, :], in_=head_of[:, :], compare_op=ALU.is_ge, fill=0.0,
                                          base=DH - 1, pattern=[[DH, H]], channel_multiplier=-1))
            const(nc.gpsimd.memset(slot_head[:, :, :], 1.0))
            const(nc.gpsimd.affine_select(out=slot_head[:, :, :], in_=slot_head[:, :, :], compare_op=ALU.is_ge,
                                          fill=0.0, base=0, pattern=[[P, 2], [-S, H]], channel_multiplier=1))
            const(nc.gpsimd.affine_select(out=slot_head[:, :, :], in_=slot_head[:, :, :], compare_op=ALU.is_ge,
                                          fill=0.0, base=S - 1, pattern=[[-P, 2], [S, H]], channel_multiplier=-1))
            const(nc.gpsimd.memset(slot_sel[:, :], 0.0))
            for r in range(P // S):
                const(nc.gpsimd.affine_select(out=slot_sel[:, :], in_=slot_sel[:, :], compare_op=ALU.not_equal,
                                              fill=1.0, base=-S * r, pattern=[[-1, S]], channel_multiplier=1))
            assert made[0] == CONSTS_MADE
            pool.wait_ge(area0_drained, AREA0["slotq"] + 1)
            nc.gpsimd.tensor_tensor(qd_heads[:, :, :], qdT[:, :].unsqueeze(1).broadcast_to([P, H, S]),
                                    head_of[:, :].unsqueeze(2).broadcast_to([P, H, S]), ALU.mult).then_inc(slotq_done, 1)
            pool.wait_ge(rows_in, 16 * (3 + 4 * B))
            add_row(x_b, 0, bout_row, norm_done)
            nc.gpsimd.tensor_tensor(slot_rows[:, :], slot_rows[:, :], dbo_row[:, :], ALU.add).then_inc(o_pool, 1)
            for slot in range(SLOTS):
                for tick in range(TICKS):
                    b, n = projection_step(slot, tick)
                    if n == A_RSTD:
                        rstd_of(b, stats_done, vare[:, :], mv[:, :, 1], rstd[:, :], vare_done, rstd_done)
                    if n == A_SPLITQ:
                        cut_q(b)
                        add_row(x_b, b, bout_row, norm_done)
                    if n == A_SPLITK:
                        cut_k(b)
                    b, n = finish_step(slot, tick)
                    if n == P_RSTD:
                        rstd_of(b, stats2_done, vare2[:, :], mv2[:, :, 1], rstd2[:, :], vare2_done, rstd2_done)
                    if n == P_QC:
                        add_row(x_plus, b, cbo_row, norm2_done)
                    if slot < NGROUPS and tick in (4, 8, 11):
                        diagonal(slot, (4, 8, 11).index(tick))
            rstd_of(B - 1, stats2_done, vare2[:, :], mv2[:, :, 1], rstd2[:, :], vare2_done, rstd2_done)
            add_row(x_plus, B - 1, cbo_row, norm2_done)
            pool.wait_ge(o_chain, 3)
            nc.gpsimd.tensor_scalar(vare[0:B * S, 0:1], o_mv[:, 1:2], EPS, None, ALU.add).then_inc(o_pool, 1)
            pool.wait_ge(o_pool, 2)
            nc.gpsimd.tensor_tensor(rstd[0:B * S, 0:1], vare[0:B * S, 0:1], mhalf[0:B * S, 0:1],
                                    ALU.pow).then_inc(o_pool, 1)
            pool.wait_ge(kcT_copied, 2)
            for b in range(B):
                nc.gpsimd.tensor_tensor(vc_heads[:, b, :, :], vcT[:, b, :].unsqueeze(1).broadcast_to([P, H, S]),
                                        head_of[:, :].unsqueeze(2).broadcast_to([P, H, S]),
                                        ALU.mult).then_inc(vheads_done, 1)
            for pair in range(2 * B):
                pool.wait_ge(c_summed, pair + 1)
                if pair >= 2:
                    pool.wait_ge(c_transposed, pair - 1)
                nc.gpsimd.tensor_tensor(c_prob[pair % 2].rearrange("p (a s) -> p a s", s=S),
                                        c_exp[pair % 2].rearrange("p (a s) -> p a s", s=S),
                                        c_sum[pair % 2][:, :].unsqueeze(2).broadcast_to([P, 2 * H, S]),
                                        ALU.mult).then_inc(c_normed, 1)

        @block.scalar
        def _(act):
            act.wait_ge(attn_w_in, 32)
            for dst, src in ((wq_cols, wq[:, :]), (wk_cols, wkv[:, 0:D])):
                src = src.rearrange("k (s g d) -> k g d s", s=H // 2, g=2)
                for g in range(2):
                    nc.scalar.activation(dst[:, 64 * g:64 * (g + 1)].rearrange("k (d s) -> k d s", d=DH),
                                         src[:, g, :, :], ACT.Copy).then_inc(cols_done, 1)
            act.wait_ge(area0_filled, AREA0["ctxT"] + 1)
            nc.scalar.activation(ctxT[:, :, :, :], area0[:, 0:P].rearrange("p (b m) -> p b m", b=B).unsqueeze(2)
                                 .broadcast_to([P, B, HG, MEM]), ACT.Copy).then_inc(area0_drained, 1)
            act.wait_ge(area0_filled, AREA0["slotT"] + 1)
            nc.scalar.activation(slotsT[:, :], area0[:, 0:S], ACT.Copy).then_inc(area0_drained, 1)
            act.wait_ge(area0_filled, AREA0["kmem"] + 1)
            nc.scalar.activation(kmem[:, 0, :], area0[:, 0:P], ACT.Copy).then_inc(kmem_part, 1)
            act.wait_ge(area0_filled, AREA0["slotq"] + 1)
            nc.scalar.activation(qdT[:, :], area0[:, 0:S], ACT.Identity,
                                 bias=db["q"][:, 0:1]).then_inc(area0_drained, 1)

            def project(b, step):
                if step == A_T:
                    act.wait_ge(area0_filled, AREA0[(b, "xnT")] + 1)
                    nc.scalar.activation(xnT[:, :], area0[:, :], ACT.Copy).then_inc(area0_drained, 1)
                if step == A_Q:
                    act.wait_ge(area0_filled, AREA0[(b, "q")] + 1)
                    if b:
                        act.wait_ge(q_stacked[b - 1], NQ_DMA)
                    nc.scalar.activation(qp[:, 0, :], area0[:, :], ACT.Copy).then_inc(q_first, 1)
                if step == A_K:
                    act.wait_ge(area0_filled, AREA0[(b, "k")] + 1)
                    if b:
                        act.wait_ge(k_stacked[b - 1], NK_DMA)
                    nc.scalar.activation(kp[:, 0, MEM:], area0[:, :], ACT.Copy).then_inc(k_first, 1)
                if step == A_V:
                    act.wait_ge(area0_filled, AREA0[(b, "v")] + 1)
                    if b == 0:
                        act.wait_ge(consts, 3)
                    if b >= 2:
                        act.wait_ge(pv_done, NGB * (b - 1))
                    nc.scalar.activation(v_aug[b % 2][:, :, :, 0:DH],
                                         area0[:, :].rearrange("p (t h d) -> p t h d", t=NT, d=DH),
                                         ACT.Copy).then_inc(area0_drained, 1)

            def finish(b, n):
                uses = finish_uses(b, n)
                if uses:
                    act_waits = AREA1[uses[0]] + 1
                if n == P_ATT:
                    act.wait_ge(area1_filled, act_waits)
                    nc.scalar.activation(attT[:, :], area1[:, :], ACT.Copy).then_inc(area1_drained, 1)
                if n == P_T:
                    act.wait_ge(area1_filled, act_waits)
                    nc.scalar.activation(xn2T[:, :], area1[:, :], ACT.Copy).then_inc(area1_drained, 1)
                if n == P_QC:
                    act.wait_ge(area1_filled, act_waits)
                    nc.scalar.activation(qcT[:, b, :], area1[:, :], ACT.Identity,
                                         bias=cb["q"][:, 0:1]).then_inc(area1_drained, 1)
                if n == P_KD:
                    act.wait_ge(area1_filled, act_waits)
                    nc.scalar.activation(kdT[:, :], area1[:, :], ACT.Identity,
                                         bias=db["k"][:, 0:1]).then_inc(area1_drained, 1)
                if n == P_VD:
                    act.wait_ge(area1_filled, act_waits)
                    nc.scalar.activation(vd[:, :, :].rearrange("p t d -> p (t d)"), area1[:, :],
                                         ACT.Copy).then_inc(area1_drained, 1)
                if n in (P_SD, P_SD + 2):
                    c = (n - P_SD) // 2
                    act.wait_ge(sd_chain, 2 * (2 * b + c + 1))
                    nc.scalar.activation(pd[:, c, :], area1[:, :], ACT.Exp, bias=sd_max[:, c:c + 1], scale=SCALE,
                                         accum_out=sd_sum[:, c:c + 1]).then_inc(area1_drained, 1)
                if n in (P_PT, P_PT + 1):
                    act.wait_ge(area1_filled, act_waits)
                    nc.scalar.activation(pdT[:, n - P_PT, :], area1[:, :], ACT.Copy).then_inc(area1_drained, 1)

            def exp_unit(group, u):
                m = UNITS * group + u
                act.wait_ge(scoreT_ready, m + 1)
                if u == 0 and group >= 2:
                    act.wait_ge(pv_done, group - 1)
                nc.scalar.activation(probs[group % 2][:, u, :], scoreT_bank[m % 2][:, :], ACT.Exp,
                                     scale=SCALE).then_inc(exp_done, 1)

            def copy_oT(group):
                act.wait_ge(pv_done, group + 1)
                b, gl = divmod(group, NGB)
                if b:
                    act.wait_ge(area1_filled, AREA1[(b - 1, "tok", NT - 1)] + 1)
                nc.scalar.activation(oT[:, gl, :], pv_bank[:, :], ACT.Copy).then_inc(oT_copied, 1)

            for step in range(A_VM + 1):
                project(0, step)
            for slot in range(SLOTS):
                for tick in range(TICKS):
                    if slot < NGROUPS and tick < UNITS:
                        exp_unit(slot, tick)
                    b, n = projection_step(slot, tick)
                    if b is not None:
                        project(b, n)
                    b, n = finish_step(slot, tick)
                    if b is not None:
                        finish(b, n)
                    if tick == 11 and 1 <= slot <= NGROUPS:
                        copy_oT(slot - 1)
            for n in range(P_SUM + 1):
                finish(B - 1, n)

            act.wait_ge(oh_ready, 2)
            act.wait_ge(hT_zeroed, 1)
            nc.scalar.activation(hT[:, :, 0:B], area1[:, 0:B * S].rearrange("p (b e) -> p e b", b=B),
                                 ACT.Copy).then_inc(hT_copied, 1)
            nc.scalar.activation(o_T[:, :], area1[:, B * S:2 * B * S], ACT.Copy).then_inc(hT_copied, 1)

            def copy_uvT(g):
                act.wait_ge(uvT_ready, g + 1)
                if g >= 2:
                    act.wait_ge(y_ready, g - 1)
                nc.scalar.activation(uvT[g % 2], scoreT_bank[g % 2][:, :], ACT.Copy).then_inc(uvT_copied, 1)

            for g in range(NGB):
                for k in range(2):
                    act.wait_ge(silu_in, 2 * g + k + 1)
                    t = (ub, gb)[k][g % 2]
                    nc.scalar.activation(t, t, ACT.Silu).then_inc(silu_done, 1)
                if g >= 1:
                    copy_uvT(g - 1)
            copy_uvT(NGB - 1)
            act.wait_ge(kcT_ready, 2)
            nc.scalar.activation(kcT[:, :, :].rearrange("p b s -> p (b s)"), area0[:, 0:B * S], ACT.Identity,
                                 bias=cb["k"][:, 0:1]).then_inc(kcT_copied, 1)
            nc.scalar.activation(vcT[:, :, :].rearrange("p b s -> p (b s)"), area0[:, B * S:2 * B * S], ACT.Identity,
                                 bias=cb["v"][:, 0:1]).then_inc(kcT_copied, 1)
            for c in range(2):
                act.wait_ge(vo_ready, c + 1)
                nc.scalar.activation(vo[:, 2 * c:2 * c + 2, :, :].rearrange("p b c d -> p (b c d)"),
                                     (area1, pv_bank)[c][:, :], ACT.Copy).then_inc(vo_copied, 1)

            def c_exponentiate(pair):
                act.wait_ge(c_shifted, pair + 1)
                nc.scalar.activation(c_exp[pair % 2], c_exp[pair % 2], ACT.Exp, scale=SCALE).then_inc(c_exped, 1)

            def c_copy(pair):
                act.wait_ge(c_transposed, pair + 1)
                if pair >= 2:
                    act.wait_ge(c_mixed, pair - 1)
                nc.scalar.activation(c_probT[pair % 2], scoreT_bank[pair % 2][:, :], ACT.Copy).then_inc(c_copied, 1)

            for pair in range(2 * B):
                c_exponentiate(pair)
                if pair:
                    c_copy(pair - 1)
            c_copy(2 * B - 1)

        @block.tensor
        def _(pe):
            wv = wkv[:, D:2 * D]
            shift_bank = area0[:, :].bitcast(BF16)

            def use0(name):
                if AREA0[name]:
                    pe.wait_ge(area0_drained, AREA0[name])

            def use1(name):
                if AREA1[name]:
                    pe.wait_ge(area1_drained, AREA1[name])

            pe.wait_ge(pool_const, 3)
            pe.wait_ge(ctx_in_sem, 16)
            nc.tensor.transpose(area0[:, 0:P], ctx_in[:, :], ident[:, :]).then_inc(area0_filled, 1)
            pe.wait_ge(slot_w_in, 16 * 16)
            use0("slotT")
            nc.tensor.transpose(area0[:, 0:S], slots[:, :], ident[0:S, 0:S]).then_inc(area0_filled, 1)
            pe.wait_ge(cols_done, 4)
            use0("kmem")
            nc.tensor.matmul(area0[:, 0:P], wk_cols[:, :], ctxT[:, :, 0, :], start=True, stop=True).then_inc(area0_filled, 1)
            use0("slotq")
            nc.tensor.matmul(area0[:, 0:S], dw["q"][:, :], slotsT[:, :], start=True, stop=True).then_inc(area0_filled, 1)

            def project(b, step):
                if step in PROJ_USES:
                    use0((b, PROJ_USES[step]))
                if step == A_T:
                    pe.wait_ge(norm_done, b + 1)
                    for t in range(NT):
                        mm = nc.tensor.transpose(area0[:, P * t:P * (t + 1)], xn[:, t, :], ident[:, :])
                    mm.then_inc(area0_filled, 1)
                if step == A_Q:
                    nc.tensor.matmul(area0[:, :], wq_cols[:, :], xnT[:, :], start=True, stop=True).then_inc(area0_filled, 1)
                if step == A_K:
                    nc.tensor.matmul(area0[:, :], wk_cols[:, :], xnT[:, :], start=True, stop=True).then_inc(area0_filled, 1)
                if step == A_V:
                    for t in range(NT):
                        mm = nc.tensor.matmul(area0[:, P * t:P * (t + 1)], xnT[:, P * t:P * (t + 1)], wv,
                                              start=True, stop=True)
                    mm.then_inc(area0_filled, 1)
                if step == A_VM:
                    mem = ctxT[:, b, :, :].rearrange("p j m -> p (j m)")
                    nc.tensor.matmul(area0[:, 0:D], mem, wv, start=True, stop=True).then_inc(area0_filled, 1)

            def score_unit(group, k):
                n = TICKS * group + k
                b, gl = divmod(group, NGB)
                tile, heads = unit_of_scores(group, k)
                if k == 0 and gl == 0:
                    pe.wait_ge(q_stacked[b], NQ_DMA)
                    pe.wait_ge(k_stacked[b], NK_DMA)
                    if b < 2:
                        pe.wait_ge(stack_init, 32 * (b + 1))
                    if b == 0:
                        pe.wait_ge(pool_const, CAUSAL_MADE)
                if n >= 3:
                    pe.wait_ge(scores_reduced, n - 2)
                bank = score_bank[n % 3]
                q, keys = q_stack[b % 2], k_stack[b % 2]
                cols = scores_cols(tile)
                first = True

                def masked(h, t, at, lo, hi):
                    nonlocal first
                    nc.tensor.matmul(bank[:, at:at + hi - lo], q[:, h // 2, P * t:P * (t + 1)], keys[:, h, lo:hi],
                                     start=first, stop=False, skip_group_check=True)
                    first = False
                    d = MEM + P * t
                    a = max(lo, d)
                    return nc.tensor.matmul(bank[:, at + a - lo:at + hi - lo], identb[:, :], causal[:, a - d:hi - d],
                                            start=False, stop=True, skip_group_check=True)

                for m, hj in enumerate(heads):
                    mm = masked(HG * gl + hj, tile, cols * m, 0, cols)
                if tile == 0:
                    for m, hj in enumerate(heads):
                        mm = masked(HG * gl + hj, NT - 1, cols * len(heads) + MEM * m, 512, KEYS)
                mm.then_inc(scores_ready, 1)

            def shift_rows(group):
                use0(("shift", group))
                pe.wait_ge(max_chain, 3 * (group + 1))
                for t in range(NT):
                    mm = nc.tensor.transpose(shift_bank[0:8, P * t:P * (t + 1)],
                                             shift[group % 2][:, t].rearrange("p g a s -> p (g a s)"), identb[:, :])
                mm.then_inc(area0_filled, 1)

            def scoreT_unit(group, u):
                m = UNITS * group + u
                b, gl = divmod(group, NGB)
                if u == 0:
                    pe.wait_ge(shift_in[group % 2], 32 * (group // 2 + 1))
                if m >= 2:
                    pe.wait_ge(exp_done, m - 1)
                bank = scoreT_bank[m % 2]
                q, keys = q_stack[b % 2], k_stack[b % 2]

                def block_of(h, j, at):
                    return nc.tensor.matmul(bank[:, at:at + T - P * j], keys[:, h, MEM + P * j:MEM + P * (j + 1)],
                                            q[:, h // 2, P * j:T], start=(at == 0), stop=True, skip_group_check=True)

                if u < 4:
                    mm = block_of(HG * gl + u, 0, 0)
                elif u < 8:
                    block_of(HG * gl + u - 4, 1, 0)
                    mm = block_of(HG * gl + u - 4, 3, 384)
                elif u < 10:
                    for r in range(2):
                        mm = block_of(HG * gl + 2 * (u - 8) + r, 2, 256 * r)
                else:
                    for j in range(HG):
                        h = HG * gl + j
                        mm = nc.tensor.matmul(bank[32 * j:32 * j + MEM, :], keys[:, h, 0:MEM], q[:, h // 2, :],
                                              start=True, stop=True)
                mm.then_inc(scoreT_ready, 1)

            def pv_piece(group, piece):
                b, gl = divmod(group, NGB)
                pr, v = probs[group % 2], v_aug[b % 2]
                if piece == 0:
                    pe.wait_ge(exp_done, UNITS * (group + 1))
                    if gl == 0:
                        pe.wait_ge(area0_drained, AREA0[(b, "vmem")] + 1)
                    if group:
                        pe.wait_ge(oT_copied, group)
                    nc.tensor.matmul(pv_bank[:, :], v_mem[b % 2][:, gl, :], pr[:, 10, :], start=True, stop=False,
                                     skip_group_check=True)
                    return
                j = (0, 1, 2, 3)[piece - 1]
                pe.wait_ge(diag_done, 3 * group + (1, 2, 3, 3)[j])
                for hj in range(HG):
                    src = (pr[:, hj, :], pr[:, 4 + hj, 0:384], pr[:, 8 + hj // 2, 256 * (hj % 2):256 * (hj % 2) + 256],
                           pr[:, 4 + hj, 384:512])[j]
                    mm = nc.tensor.matmul(pv_bank[32 * hj:32 * hj + DH + 1, P * j:T], v[:, j, HG * gl + hj, :], src,
                                          start=False, stop=(j == 3), skip_group_check=True)
                if j == 3:
                    mm.then_inc(pv_done, 1)

            def finish(b, n):
                for name in finish_uses(b, n):
                    use1(name)
                if P_TOK <= n < P_TOK + NT:
                    t = n - P_TOK
                    pe.wait_ge(oT_copied, NGB * (b + 1))
                    for gl in range(NGB):
                        mm = nc.tensor.transpose(area1[:, P * gl:P * (gl + 1)], oT[:, gl, P * t:P * (t + 1)], ident[:, :])
                elif n == P_ATT or n == P_T:
                    if n == P_T:
                        pe.wait_ge(norm2_done, b + 1)
                    for t in range(NT):
                        mm = nc.tensor.transpose(area1[:, P * t:P * (t + 1)], att[:, t, :], ident[:, :])
                elif n == P_OUT:
                    for t in range(NT):
                        mm = nc.tensor.matmul(area1[:, P * t:P * (t + 1)], attT[:, P * t:P * (t + 1)], wout[:, :],
                                              start=True, stop=True)
                elif n == P_QC:
                    mm = nc.tensor.matmul(area1[:, :], cw["q"][:, :], xn2T[:, :], start=True, stop=True)
                elif n == P_KD:
                    mm = nc.tensor.matmul(area1[:, :], dw["k"][:, :], xn2T[:, :], start=True, stop=True)
                elif n == P_VD:
                    for t in range(NT):
                        mm = nc.tensor.matmul(area1[:, P * t:P * (t + 1)], xn2T[:, P * t:P * (t + 1)], dw["v"][:, :],
                                              start=True, stop=True)
                elif n in (P_SD, P_SD + 2):
                    c = (n - P_SD) // 2
                    pe.wait_ge(slotq_done, 1)
                    mm = nc.tensor.matmul(area1[:, :], qd_heads[:, 8 * c:8 * c + 8, :].rearrange("p h s -> p (h s)"),
                                          kdT[:, :], start=True, stop=True)
                elif n in (P_PT, P_PT + 1):
                    for t in range(NT):
                        mm = nc.tensor.transpose(area1[:, P * t:P * (t + 1)], pd[:, n - P_PT, P * t:P * (t + 1)],
                                                 ident[:, :])
                elif n in (P_PV, P_PV + 1):
                    for t in range(NT):
                        mm = nc.tensor.matmul(area1[:, 0:D], pdT[:, n - P_PV, P * t:P * (t + 1)], vd[:, t, :],
                                              start=(t == 0), stop=(t == NT - 1))
                elif n == P_SUM:
                    pe.wait_ge(pool_const, CONSTS_MADE)
                    for c in range(2):
                        mm = nc.tensor.matmul(area1[:, 0:S], od[:, c, :], slot_sel[:, :], start=(c == 0), stop=(c == 1))
                else:
                    return
                mm.then_inc(area1_filled, 1)

            for step in range(A_VM + 1):
                project(0, step)
            for group in range(LEAD):
                for k in range(TICKS):
                    score_unit(group, k)
                    if group and k == SHIFT_TICK:
                        shift_rows(group - 1)
            shift_rows(LEAD - 1)
            for slot in range(SLOTS):
                for tick in range(TICKS):
                    if slot + LEAD < NGROUPS:
                        score_unit(slot + LEAD, tick)
                    if slot < NGROUPS and tick < UNITS:
                        scoreT_unit(slot, tick)
                    if 1 <= slot <= NGROUPS and tick % 2 == 0 and tick < 10:
                        pv_piece(slot - 1, tick // 2)
                    if tick == SHIFT_TICK and slot >= 1 and slot - 1 + LEAD < NGROUPS:
                        shift_rows(slot - 1 + LEAD)
                    b, n = projection_step(slot, tick)
                    if b is not None:
                        project(b, n)
                    b, n = finish_step(slot, tick)
                    if b is not None:
                        finish(b, n)
            for n in range(P_SUM + 1):
                finish(B - 1, n)

            pe.wait_ge(area1_drained, len(AREA1))
            nc.tensor.matmul(area0[0:B * S, 0:D], adT[:, :, :].rearrange("p b s -> p (b s)"), dw["o"][:, :],
                             start=True, stop=True).then_inc(oh_ready, 1)
            pe.wait_ge(o_chain, 7)
            nc.tensor.transpose(area1[:, 0:B * S], h_rows[:, :], ident[0:B * S, 0:B * S])
            nc.tensor.transpose(area1[:, B * S:2 * B * S], o_rows[:, :], ident[0:B * S, 0:B * S]).then_inc(oh_ready, 1)
            pe.wait_ge(hT_copied, 1)
            up_banks = score_bank + [area0]

            def up(g, k):
                n = 2 * g + k
                if n == 0:
                    pe.wait_ge(w1_in, 16 * S)
                    pe.wait_ge(wg_in, 16 * S)
                if n >= len(up_banks):
                    pe.wait_ge(silu_in, n - len(up_banks) + 1)
                for j in range(HG):
                    mm = nc.tensor.matmul(up_banks[n % 4][32 * j:32 * j + 32, :], hT[:, HG * g + j, :],
                                          (w1, wg)[k][HG * g + j], start=True, stop=True)
                mm.then_inc(up_ready, 1)

            def turn(g):
                pe.wait_ge(uv_done, g + 1)
                if g >= 2:
                    pe.wait_ge(uvT_copied, g - 1)
                for c in range(FC):
                    mm = nc.tensor.transpose(scoreT_bank[g % 2][:, P * c:P * (c + 1)], uv[g % 2][:, c::FC], ident[:, :])
                mm.then_inc(uvT_ready, 1)

            def down(g):
                pe.wait_ge(uvT_copied, g + 1)
                if g == 0:
                    pe.wait_ge(w2_in, 16 * S)
                for c in range(FC):
                    for j in range(HG):
                        e = HG * g + j
                        mm = nc.tensor.matmul(pv_bank[32 * j:32 * j + 32, D * g:D * (g + 1)],
                                              uvT[g % 2][:, P * c + 32 * j:P * c + 32 * j + 32],
                                              w2[e][:, c, :], start=(c == 0), stop=(c == FC - 1),
                                              skip_group_check=True)
                mm.then_inc(y_ready, 1)

            for g in range(NGB):
                up(g, 0)
                up(g, 1)
                if g >= 1:
                    turn(g - 1)
                if g >= 2:
                    down(g - 2)
            turn(NGB - 1)
            down(NGB - 2)
            down(NGB - 1)
            pe.wait_ge(y_copied, 1)
            pe.wait_ge(hT_copied, 2)
            for g in range(NGB):
                mm = nc.tensor.transpose(area1[:, P * g:P * (g + 1)], ysb[:, P * g:P * (g + 1)], ident[:, :])
            mm.then_inc(yT_ready, 1)
            pe.wait_ge(o2_done, 1)
            o2 = o2T[:, :, :].rearrange("p b s -> p (b s)")
            nc.tensor.matmul(area0[:, 0:B * S], cw["k"][:, :], o2, start=True, stop=True)
            nc.tensor.matmul(area0[:, B * S:2 * B * S], cw["v"][:, :], o2, start=True, stop=True).then_inc(kcT_ready, 2)

            def c_scores(pair):
                b, half = divmod(pair, 2)
                pe.wait_ge(kheads_done, b + 1)
                if pair >= 3:
                    pe.wait_ge(c_shifted, pair - 2)
                for r in range(2):
                    t = 2 * half + r
                    mm = nc.tensor.matmul(score_bank[pair % 3][:, 256 * r:256 * (r + 1)], qcT[:, b, P * t:P * (t + 1)],
                                          kc_heads[:, b, :, :].rearrange("p h s -> p (h s)"), start=True, stop=True)
                mm.then_inc(c_scored, 1)

            def c_transpose(pair):
                pe.wait_ge(c_normed, pair + 1)
                if pair >= 2:
                    pe.wait_ge(c_copied, pair - 1)
                for c in range(4):
                    mm = nc.tensor.transpose(scoreT_bank[pair % 2][:, P * c:P * (c + 1)],
                                             c_prob[pair % 2][:, P * c:P * (c + 1)], ident[:, :])
                mm.then_inc(c_transposed, 1)

            def c_mix(pair):
                b, half = divmod(pair, 2)
                pe.wait_ge(c_copied, pair + 1)
                pe.wait_ge(vo_copied, 2)
                if pair >= 2:
                    pe.wait_ge(y_done, pair - 1)
                for r in range(2):
                    for c in range(2):
                        mm = nc.tensor.matmul((area0, area1)[pair % 2][:, D * r:D * (r + 1)],
                                              c_probT[pair % 2][:, P * (2 * r + c):P * (2 * r + c + 1)],
                                              vo[:, b, c, :], start=(c == 0), stop=(c == 1))
                mm.then_inc(c_mixed, 1)

            c_scores(0)
            c_scores(1)
            pe.wait_ge(vheads_done, B)
            for b in range(B):
                for c in range(2):
                    mm = nc.tensor.matmul((area1, pv_bank)[b // 2][:, D * (2 * (b % 2) + c):D * (2 * (b % 2) + c + 1)],
                                          vc_heads[:, b, 8 * c:8 * c + 8, :].rearrange("p h s -> p (h s)"),
                                          cw["o"][:, :], start=True, stop=True)
                if b % 2:
                    mm.then_inc(vo_ready, 1)
            for pair in range(2 * B):
                if pair + 2 < 2 * B:
                    c_scores(pair + 2)
                c_transpose(pair)
                if pair:
                    c_mix(pair - 1)
            c_mix(2 * B - 1)

        @block.vector
        def _(dve):
            nc.vector.memset(zero_rows[:, :], 0.0).then_inc(consts, 1)
            nc.vector.memset(one_rows[:, :], 1.0).then_inc(consts, 1)

            def norm_stats(n, src, st, m, done, per_tile):
                for t in range(NT):
                    nc.vector.bn_stats(st[:, t, :], src[:, t, :]).then_inc(per_tile, 1)
                dve.wait_ge(per_tile, NT * (n + 1))
                for t in range(NT):
                    ins = nc.vector.bn_aggr(m[:, t, :], st[:, t, :])
                ins.then_inc(done, 1)

            def normalise(n, src, dst, m, r, s_r, done):
                dve.wait_ge(s_r, n + 1)
                for t in range(NT):
                    ins = nc.vector.tensor_scalar(dst[:, t, :], src[:, t, :], m[:, t, 0:1], r[:, t:t + 1],
                                                  ALU.subtract, ALU.mult)
                ins.then_inc(done, 1)

            def project(b, step):
                if step == A_STATS:
                    dve.wait_ge(x_in0 if b == 0 else x_in1, 16 if b == 0 else 16 * (B - 1))
                    norm_stats(b, x[:, b, :, :], stats, mv, stats_done, tile_stats)
                if step == A_NORM:
                    if b:
                        dve.wait_ge(area0_filled, AREA0[(b - 1, "xnT")] + 1)
                    normalise(b, x[:, b, :, :], xn, mv, rstd, rstd_done, norm_done)
                if step == A_Q:
                    dve.wait_ge(q_first, b + 1)
                    if b:
                        dve.wait_ge(q_third, 2 * b - 1)
                    nc.vector.tensor_tensor(res[:, :], area0[:, :], qp[:, 0, :], ALU.subtract).then_inc(res_done, 1)
                    dve.wait_ge(res_done, 2 * b + 1)
                    dve.sem_inc(area0_drained, 1)
                if step == A_K:
                    dve.wait_ge(k_first, b + 1)
                    if b:
                        dve.wait_ge(q_third, 2 * b)
                    nc.vector.tensor_tensor(resk[:, :], area0[:, :], kp[:, 0, MEM:], ALU.subtract).then_inc(res_done, 1)
                    dve.wait_ge(res_done, 2 * b + 2)
                    dve.sem_inc(area0_drained, 1)
                if step == A_VM:
                    dve.wait_ge(area0_filled, AREA0[(b, "vmem")] + 1)
                    dve.wait_ge(consts, 3 if b == 0 else 3)
                    if b >= 2:
                        dve.wait_ge(pv_done, NGB * (b - 1))
                    for j in range(HG):
                        rows = slice(32 * j, 32 * j + 32)
                        ins = nc.vector.tensor_copy(
                            v_mem[b % 2][rows, :, 32 * j:32 * j + DH],
                            area0[rows, 0:D].rearrange("p (g j d) -> p g j d", g=NGB, j=HG)[:, :, j, :])
                    ins.then_inc(area0_drained, 1)

            def reduce_unit(group, k):
                n = TICKS * group + k
                tile, heads = unit_of_scores(group, k)
                dve.wait_ge(scores_ready, n + 1)
                bank = score_bank[n % 3]
                m, cols = rowmax[group % 2], scores_cols(tile)
                if tile == 0:
                    nc.vector.tensor_reduce(m[:, 0, :, k], bank[:, 0:2 * cols].rearrange("p (a n) -> p a n", a=2),
                                            AX.X, ALU.max)
                    nc.vector.tensor_reduce(tailmax[group % 2][:, :, k],
                                            bank[:, 2 * cols:2 * cols + 2 * MEM].rearrange("p (a n) -> p a n", a=2),
                                            AX.X, ALU.max).then_inc(scores_reduced, 1)
                else:
                    h = heads[0]
                    nc.vector.tensor_reduce(m[:, tile, h % 2, h // 2:h // 2 + 1], bank[:, 0:cols], AX.X,
                                            ALU.max).then_inc(scores_reduced, 1)

            def shift_of(group):
                m, sh = rowmax[group % 2], shift[group % 2]
                dve.wait_ge(scores_reduced, TICKS * (group + 1))
                if group >= 2:
                    dve.wait_ge(area0_filled, AREA0[("shift", group - 2)] + 1)
                last = m[:, NT - 1, :, :].rearrange("p g s -> p (g s)")
                nc.vector.tensor_tensor(last, last, tailmax[group % 2][:, :, :].rearrange("p g s -> p (g s)"),
                                        ALU.max).then_inc(max_chain, 1)
                dve.wait_ge(max_chain, 3 * group + 1)
                mm = m[:, :, :, :].rearrange("p t g s -> p (t g) s")
                hi = sh[:, :, :, 0, :].rearrange("p t g s -> p (t g) s")
                lo = sh[:, :, :, 1, :].rearrange("p t g s -> p (t g) s")
                nc.vector.tensor_scalar(hi, mm, -1.0, None, ALU.mult).then_inc(max_chain, 1)
                dve.wait_ge(max_chain, 3 * group + 2)
                nc.vector.scalar_tensor_tensor(out=lo, in0=mm, scalar=-1.0, in1=hi, op0=ALU.mult,
                                               op1=ALU.subtract).then_inc(max_chain, 1)
                dve.wait_ge(area0_filled, AREA0[("shift", group)] + 1)
                if group >= 2:
                    dve.wait_ge(shift_in[group % 2], 32 * (group // 2))
                nc.vector.tensor_copy(shiftT[group % 2][:, :], area0[:, :].bitcast(BF16)[0:8, 0:T])\
                    .then_inc(area0_drained, 1)

            def finish(b, n):
                for name in finish_uses(b, n):
                    filled = AREA1[name] + 1
                if P_TOK <= n < P_TOK + NT:
                    t = n - P_TOK
                    heads = area1[:, :].rearrange("p (h c) -> p h c", h=H)
                    dve.wait_ge(area1_filled, filled)
                    nc.vector.reciprocal(rden[:, :], heads[:, :, DH]).then_inc(rden_done, 1)
                    dve.wait_ge(rden_done, NT * b + t + 1)
                    nc.vector.tensor_tensor(att[:, t, :].rearrange("p (h d) -> p h d", h=H), heads[:, :, 0:DH],
                                            rden[:, :].unsqueeze(2).broadcast_to([P, H, DH]),
                                            ALU.mult).then_inc(area1_drained, 1)
                if n == P_OUT:
                    dve.wait_ge(area1_filled, filled)
                    dve.wait_ge(x_b, b + 1)
                    xb = x[:, b, :, :].rearrange("p t d -> p (t d)")
                    nc.vector.tensor_tensor(xb, area1[:, :], xb, ALU.add).then_inc(area1_drained, 1)
                if n == P_STATS:
                    dve.wait_ge(area1_drained, AREA1[(b, "out")] + 1)
                    norm_stats(b, x[:, b, :, :], stats2, mv2, stats2_done, tile_stats2)
                if n == P_NORM:
                    normalise(b, x[:, b, :, :], xn2, mv2, rstd2, rstd2_done, norm2_done)
                if n in (P_SD, P_SD + 2):
                    c = (n - P_SD) // 2
                    dve.wait_ge(area1_filled, filled)
                    nc.vector.tensor_reduce(sd_max[:, c:c + 1], area1[:, :], AX.X, ALU.max,
                                            negate=True).then_inc(sd_chain, 1)
                    dve.wait_ge(sd_chain, 2 * (2 * b + c) + 1)
                    nc.vector.tensor_scalar(sd_max[:, c:c + 1], sd_max[:, c:c + 1], SCALE, None,
                                            ALU.mult).then_inc(sd_chain, 1)
                if n in (P_PV, P_PV + 1):
                    c = n - P_PV
                    dve.wait_ge(area1_filled, filled)
                    dve.wait_ge(area1_drained, AREA1[(b, "sd", c)] + 1)
                    nc.vector.reciprocal(sd_r[:, c:c + 1], sd_sum[:, c:c + 1]).then_inc(od_done, 1)
                    dve.wait_ge(od_done, 2 * b + c + 1)
                    nc.vector.scalar_tensor_tensor(
                        out=od[:, c, :].rearrange("p (h d) -> p h d", h=H),
                        in0=area1[:, 0:D].rearrange("p (h d) -> p h d", h=H), scalar=sd_r[:, c:c + 1],
                        in1=slot_head[:, c, :].unsqueeze(2).broadcast_to([P, H, DH]),
                        op0=ALU.mult, op1=ALU.mult).then_inc(area1_drained, 1)
                if n == P_SUM:
                    dve.wait_ge(area1_filled, filled)
                    nc.vector.tensor_scalar(adT[:, b, :], area1[:, 0:S], db["v"][:, 0:1], None,
                                            ALU.add).then_inc(area1_drained, 1)

            project(0, A_STATS)
            for n in range(2):
                nc.vector.memset(v_mem[n][:, :, :], 0.0).then_inc(v_zero, 1)
            nc.vector.memset(v_aug[0][:, :, :, DH:DH + 1], 1.0)
            nc.vector.memset(v_aug[1][:, :, :, DH:DH + 1], 1.0)
            dve.wait_ge(v_zero, 2)
            for n in range(2):
                for j in range(HG):
                    ins = nc.vector.memset(v_mem[n][32 * j:32 * j + 32, :, 32 * j + DH:32 * j + DH + 1], 1.0)
            ins.then_inc(consts, 1)
            dve.wait_ge(kmem_part, 1)
            nc.vector.tensor_tensor(resk[:, 0:P], area0[:, 0:P], kmem[:, 0, :], ALU.subtract).then_inc(kmem_part, 1)
            dve.wait_ge(kmem_part, 2)
            nc.vector.tensor_copy(kmem[:, 1, :], resk[:, 0:P]).then_inc(area0_drained, 1)
            dve.wait_ge(area0_drained, AREA0["kmem"] + 1)
            nc.vector.tensor_tensor(kmem[:, 2, :], resk[:, 0:P], kmem[:, 1, :], ALU.subtract).then_inc(kmem_part, 1)
            for step in range(1, A_VM + 1):
                project(0, step)
            for group in range(LEAD):
                for k in range(TICKS):
                    reduce_unit(group, k)
                    if group and k == SHIFT_TICK:
                        shift_of(group - 1)
            shift_of(LEAD - 1)
            for slot in range(SLOTS):
                for tick in range(TICKS):
                    if slot + LEAD < NGROUPS:
                        reduce_unit(slot + LEAD, tick)
                    if tick == SHIFT_TICK and slot >= 1 and slot - 1 + LEAD < NGROUPS:
                        shift_of(slot - 1 + LEAD)
                    b, n = projection_step(slot, tick)
                    if b is not None:
                        project(b, n)
                    b, n = finish_step(slot, tick)
                    if b is not None:
                        finish(b, n)
            for n in range(P_SUM + 1):
                finish(B - 1, n)

            dve.wait_ge(scoreT_ready, UNITS * NGROUPS)
            nc.vector.memset(hT, 0.0).then_inc(hT_zeroed, 1)
            dve.wait_ge(oh_ready, 1)
            dve.wait_ge(o_pool, 1)
            nc.vector.tensor_tensor(o_rows[:, :], area0[0:B * S, 0:D], slot_rows[:, :], ALU.add).then_inc(o_chain, 1)
            dve.wait_ge(o_chain, 1)
            nc.vector.bn_stats(o_stats[:, :], o_rows[:, :]).then_inc(o_chain, 1)
            dve.wait_ge(o_chain, 2)
            nc.vector.bn_aggr(o_mv[:, :], o_stats[:, :]).then_inc(o_chain, 1)
            dve.wait_ge(o_pool, 3)
            nc.vector.tensor_scalar(h_rows[:, :], o_rows[:, :], o_mv[:, 0:1], rstd[0:B * S, 0:1], ALU.subtract,
                                    ALU.mult).then_inc(o_chain, 1)
            dve.wait_ge(o_chain, 4)
            nc.vector.tensor_tensor(h_rows[:, :], h_rows[:, :], ln_g[:, :], ALU.mult).then_inc(o_chain, 1)
            dve.wait_ge(o_chain, 5)
            nc.vector.tensor_tensor(h_rows[:, :], h_rows[:, :], ln_b[:, :], ALU.add).then_inc(o_chain, 1)
            nc.vector.tensor_tensor(o_rows[:, :], o_rows[:, :], b2_rows[:, :], ALU.add).then_inc(o_chain, 1)
            up_banks = score_bank + [area0]

            def add_bias(g, k):
                n = 2 * g + k
                if n == 0:
                    dve.wait_ge(b1_in, 16 * 2 * HG)
                dve.wait_ge(up_ready, n + 1)
                nc.vector.tensor_tensor((ub, gb)[k][g % 2], up_banks[n % 4][:, :], (b1_rows, bg_rows)[k][:, g, :],
                                        ALU.add).then_inc(silu_in, 1)

            def times(g):
                dve.wait_ge(silu_done, 2 * g + 2)
                if g >= 2:
                    dve.wait_ge(uvT_ready, g - 1)
                nc.vector.tensor_tensor(uv[g % 2], ub[g % 2], gb[g % 2], ALU.mult).then_inc(uv_done, 1)

            for g in range(NGB):
                if g >= 2:
                    dve.wait_ge(uv_done, g - 1)
                add_bias(g, 0)
                add_bias(g, 1)
                if g:
                    times(g - 1)
            times(NGB - 1)
            dve.wait_ge(y_ready, NGB)
            nc.vector.tensor_copy(ysb, pv_bank[:, :]).then_inc(y_copied, 1)
            dve.wait_ge(yT_ready, 1)
            nc.vector.tensor_tensor(o2T[:, :, :].rearrange("p b (g j) -> p b g j", g=NGB),
                                    area1[:, :].rearrange("p (g j r) -> p r g j", g=NGB, j=HG)[:, 0:B, :, :],
                                    o_T[:, :].rearrange("p (b g j) -> p b g j", b=B, g=NGB), ALU.add).then_inc(o2_done, 1)

            dve.wait_ge(kcT_copied, 1)
            for b in range(B):
                nc.vector.tensor_tensor(kc_heads[:, b, :, :], kcT[:, b, :].unsqueeze(1).broadcast_to([P, H, S]),
                                        head_of[:, :].unsqueeze(2).broadcast_to([P, H, S]),
                                        ALU.mult).then_inc(kheads_done, 1)

            def c_shift(pair):
                bank = score_bank[pair % 3][:, :].rearrange("p (a s) -> p a s", s=S)
                m = c_max[pair % 2]
                dve.wait_ge(c_scored, pair + 1)
                nc.vector.tensor_reduce(m[:, :], bank, AX.X, ALU.max).then_inc(c_reduced, 1)
                dve.wait_ge(c_reduced, pair + 1)
                if pair >= 2:
                    dve.wait_ge(c_normed, pair - 1)
                nc.vector.tensor_tensor(c_exp[pair % 2].rearrange("p (a s) -> p a s", s=S), bank,
                                        m[:, :].unsqueeze(2).broadcast_to([P, 2 * H, S]),
                                        ALU.subtract).then_inc(c_shifted, 1)

            def c_sums(pair):
                dve.wait_ge(c_exped, pair + 1)
                if pair >= 2:
                    dve.wait_ge(c_normed, pair - 1)
                nc.vector.tensor_reduce(c_sum[pair % 2][:, :], c_exp[pair % 2].rearrange("p (a s) -> p a s", s=S),
                                        AX.X, ALU.add).then_inc(c_summing, 1)
                dve.wait_ge(c_summing, pair + 1)
                nc.vector.reciprocal(c_sum[pair % 2][:, :], c_sum[pair % 2][:, :]).then_inc(c_summed, 1)

            def c_result(pair):
                b, half = divmod(pair, 2)
                dve.wait_ge(c_mixed, pair + 1)
                dve.wait_ge(x_plus, b + 1)
                if pair >= 2:
                    dve.wait_ge(out_sent[pair % 2], 16 * (pair // 2))
                nc.vector.tensor_tensor(y[:, pair % 2, :, :].rearrange("p t d -> p (t d)"),
                                        (area0, area1)[pair % 2][:, 0:2 * D],
                                        x[:, b, 2 * half:2 * half + 2, :].rearrange("p t d -> p (t d)"),
                                        ALU.add).then_inc(y_done, 1)

            c_shift(0)
            for pair in range(2 * B):
                if pair + 1 < 2 * B:
                    c_shift(pair + 1)
                c_sums(pair)
                if pair >= 2:
                    c_result(pair - 2)
            c_result(2 * B - 2)
            c_result(2 * B - 1)


INS = ["x", "ctx_1024", "L0_xattn_Wq", "L0_xattn_Wkv", "L0_xattn_Wout", "L0_xattn_bout", "L0_ffn_slot_query",
       "L0_ffn_d_Wq", "L0_ffn_d_Wk", "L0_ffn_d_Wv", "L0_ffn_d_Wo", "L0_ffn_d_bq", "L0_ffn_d_bk", "L0_ffn_d_bv",
       "L0_ffn_d_bo", "L0_ffn_c_Wq", "L0_ffn_c_Wk", "L0_ffn_c_Wv", "L0_ffn_c_Wo", "L0_ffn_c_bq", "L0_ffn_c_bk",
       "L0_ffn_c_bv", "L0_ffn_c_bo", "L0_ffn_e_ln_g", "L0_ffn_e_ln_b", "L0_ffn_e_W1", "L0_ffn_e_b1", "L0_ffn_e_Wg",
       "L0_ffn_e_bg", "L0_ffn_e_W2", "L0_ffn_e_b2"]


def kernel(**inputs):
    import numpy as np
    import concourse.bacc as bacc
    from concourse.bass_utils import run_bass_kernel_spmd

    nc = bacc.Bacc("TRN2", target_bir_lowering=False, num_devices=1)
    arrays, args = {}, {}
    for name in INS:
        a = np.ascontiguousarray(inputs[name])
        arrays[f"in_{name}"] = a
        args[name] = nc.dram_tensor(f"in_{name}", a.shape, mybir.dt.from_np(a.dtype), kind="ExternalInput").ap()
    out = nc.dram_tensor("out", (B, T, D), F32, kind="ExternalOutput").ap()
    program(nc, args, out)
    r = run_bass_kernel_spmd(nc, [arrays], core_ids=[0])
    return r.results[0]["out"]
```

```python
from contextlib import ExitStack

import concourse.bass as bass
from concourse import mybir

F32 = mybir.dt.float32
BF16 = mybir.dt.bfloat16
ALU = mybir.AluOpType
ACT = mybir.ActivationFunctionType
AX = mybir.AxisListType

P = 128
B = 4
T = 512
NT = T // P
D = 128
H = 16
DH = D // H
MEM = 32
KEYS = MEM + T
S = 16
F = 512
FC = F // P
EPS = 1e-5
SCALE = DH ** -0.5
BIG = -1.0e30

HG = 4
NGB = H // HG
NGROUPS = B * NGB
LEAD = 2
TICKS = 14
UNITS = 11
Q_TERMS = [0, 0, 1, 1, 2, 0]
K_TERMS = [0, 1, 0, 1, 0, 2]
SHIFT_ROW = 2 * DH * len(Q_TERMS)
SLOTS = NGROUPS + 2

A_STATS, A_RSTD, A_NORM, A_T, A_Q, A_K, A_V, A_VM = 0, 2, 4, 7, 9, 13, 28, 30
A_END = A_VM + 3
SLOT_QUERY_SLOT, SLOT_QUERY_TICK = 1, 7
MAX_TICK, SHIFT_TICK = 1, 4
PV_TICKS = (2, 5, 8, 11, 12)
P_TOK, P_ATT, P_OUT, P_STATS, P_RSTD, P_NORM, P_T = (2, 4, 6, 8), 11, 14, 15, 17, 19, 22
P_KD, P_VD, P_SD, P_QC, P_PT, P_PV, P_SUM = 25, 28, (31, 34), 37, (40, 42), (45, 47), 50
P_END = P_SUM + 2
READ = 1
SCORE_UNITS = [(3, (0,)), (0, (0, 1)), (2, (0,)), (1, (0,)), (3, (1,)), (1, (1,)), (2, (1,)),
               (3, (2,)), (1, (2,)), (0, (2, 3)), (2, (2,)), (3, (3,)), (1, (3,)), (2, (3,))]


def projection_step(slot, tick):
    slot, tick = slot + tick // TICKS, tick % TICKS
    b, step = (slot + 1) // NGB + 1, (slot + 1) % NGB * TICKS + tick
    if slot < -1 or b >= B or (b == 1 and step < A_K):
        return None, -1
    return b, step


def finish_step(slot, tick):
    slot, tick = slot + tick // TICKS, tick % TICKS
    at = slot - NGB - 1
    return (at // NGB, at % NGB * TICKS + tick) if at >= 0 and at // NGB < B - 1 else (None, -1)


PROJ_USES = {A_T: "xnT", A_Q: "q", A_K: "k", A_V: "v", A_VM: "vmem"}


def count_uses():
    first = ["ctxT", "kmem"] + [(0, n) for n in PROJ_USES.values()] + [(1, "xnT"), (1, "q")]
    second = []
    for slot in range(-LEAD, SLOTS):
        for tick in range(TICKS):
            if tick == SHIFT_TICK and -LEAD <= slot - 1 and slot - 1 + LEAD < NGROUPS:
                first.append(("shift", slot - 1 + LEAD))
            if (slot, tick) == (SLOT_QUERY_SLOT, SLOT_QUERY_TICK):
                first += ["slotT", "slotq"]
            b, n = projection_step(slot, tick)
            if n in PROJ_USES:
                first.append((b, PROJ_USES[n]))
            b, n = finish_step(slot, tick)
            second += finish_uses(b, n)
    for n in range(P_END):
        second += finish_uses(B - 1, n)
    return {n: i for i, n in enumerate(first)}, {n: i for i, n in enumerate(second)}


def finish_uses(b, n):
    for at, what in ((P_TOK, "tok"), (P_PT, "pT"), (P_PV, "pv"), (P_SD, "sd")):
        if n in at:
            return [(b, what, at.index(n))]
    one = {P_ATT: "att", P_OUT: "out", P_T: "xn2T", P_QC: "qc", P_KD: "kd", P_VD: "vd", P_SUM: "sum"}
    return [(b, one[n])] if n in one else []


AREA0, AREA1 = count_uses()
CAUSAL_MADE = 6
CONSTS_MADE = CAUSAL_MADE + 7 + P // S
POOL_PAIRS = 2 * B - 2


def program(nc, i, out):
    with ExitStack() as ctx:
        def sb(name, shape, dt=F32):
            return ctx.enter_context(nc.sbuf_tensor(name, shape, dt))

        def ps(name, shape, dt=F32):
            return ctx.enter_context(nc.psum_tensor(name, shape, dt))

        def sem(name):
            return ctx.enter_context(nc.semaphore(name))

        score_bank = [ps(f"score_bank{n}", [P, 512]) for n in range(3)]
        scoreT_bank = [ps(f"scoreT_bank{n}", [P, 512]) for n in range(2)]
        pv_bank = ps("pv_bank", [P, 512])
        area0 = ps("area0", [P, 512])
        area1 = ps("area1", [P, 512])

        x = sb("x", [P, B, NT, D])
        xn = sb("xn", [P, NT, D])
        xnT = sb("xnT", [P, T])
        ctx_in = sb("ctx_in", [P, D])
        ctxT = sb("ctxT", [P, B, HG, MEM])
        wq_cols = sb("wq_cols", [P, D])
        wk_cols = sb("wk_cols", [P, D])
        wq = sb("wq", [P, D])
        wkv = sb("wkv", [P, 2 * D])
        wout = sb("wout", [P, D])
        dw = {n: sb(f"dw_{n}", [P, D]) for n in "qkvo"}
        cw = {n: sb(f"cw_{n}", [P, D]) for n in "qkvo"}
        db = {n: sb(f"db_{n}", [P, 1]) for n in "qkv"}
        cb = {n: sb(f"cb_{n}", [P, 1]) for n in "qkv"}
        bout_row = sb("bout_row", [P, D])
        cbo_row = sb("cbo_row", [P, D])
        dbo_row = sb("dbo_row", [B * S, D])
        slot_rows = sb("slot_rows", [B * S, D])
        slots = sb("slots", [S, D])
        ln_g = sb("ln_g", [B * S, D])
        ln_b = sb("ln_b", [B * S, D])
        b2_rows = sb("b2_rows", [B * S, D])

        ident = sb("ident", [P, P])
        identb = sb("identb", [P, P], BF16)
        causal = sb("causal", [P, P], BF16)
        head_of = sb("head_of", [P, H])
        slot_head = sb("slot_head", [P, 2, H])
        slot_sel = sb("slot_sel", [P, S])
        zero_rows = sb("zero_rows", [4 * H // 2, T], BF16)
        one_rows = sb("one_rows", [S, KEYS], BF16)
        slotsT = sb("slotsT", [P, S])

        stats = sb("stats", [P, NT, 6])
        mv = sb("mv", [P, NT, 2])
        rstd = sb("rstd", [P, NT])
        vare = sb("vare", [P, NT])
        mhalf = sb("mhalf", [P, NT])
        stats2 = sb("stats2", [P, NT, 6])
        mv2 = sb("mv2", [P, NT, 2])
        rstd2 = sb("rstd2", [P, NT])
        vare2 = sb("vare2", [P, NT])

        qp = sb("qp", [P, 3, T], BF16)
        kp = sb("kp", [P, 3, KEYS], BF16)
        kmem = sb("kmem", [P, 3, B * MEM], BF16)
        res = sb("res", [P, T])
        resk = sb("resk", [P, T])
        q_stack = [sb(f"q_stack{n}", [P, H // 2, T], BF16) for n in range(2)]
        k_stack = [sb(f"k_stack{n}", [P, H, KEYS], BF16) for n in range(2)]
        v_aug = [sb(f"v_aug{n}", [P, NT, H, DH + 1]) for n in range(2)]
        v_mem = [sb(f"v_mem{n}", [P, NGB, P]) for n in range(2)]
        rowmax = [sb(f"rowmax{n}", [P, NT, 2, 2]) for n in range(2)]
        tailmax = [sb(f"tailmax{n}", [P, 2, 2]) for n in range(2)]
        shift = [sb(f"shift{n}", [P, NT, 2, 2, 2], BF16) for n in range(2)]
        shiftT = [sb(f"shiftT{n}", [8, T], BF16) for n in range(2)]
        probs = [sb(f"probs{n}", [P, UNITS, 512]) for n in range(2)]
        oT = sb("oT", [P, NGB, T])
        rden = sb("rden", [P, NT, H])
        att = sb("att", [P, NT, D])
        attT = sb("attT", [P, T])
        xn2 = att
        xn2T = attT
        qcT = sb("qcT", [P, B, T])
        kdT = sb("kdT", [P, T])
        vd = sb("vd", [P, NT, D])
        qd_heads = sb("qd_heads", [P, H, S])
        qdT = sb("qdT", [P, S])
        sd_max = sb("sd_max", [P, 2])
        sd_sum = sb("sd_sum", [P, 2])
        sd_r = sb("sd_r", [P, 2])
        pd = sb("pd", [P, 2, T])
        pdT = sb("pdT", [P, 2, T])
        od = sb("od", [P, 2, D])
        adT = sb("adT", [P, B, S])
        w1_early = sb("w1_early", [P, 12, F])
        k0 = k_stack[0][:, :, :].rearrange("p h n -> p (h n)").bitcast(F32)
        k1 = k_stack[1][:, :, :].rearrange("p h n -> p (h n)").bitcast(F32)
        q0 = q_stack[0][:, :, :].rearrange("p h n -> p (h n)").bitcast(F32)
        q1 = q_stack[1][:, :, :].rearrange("p h n -> p (h n)").bitcast(F32)
        late1 = k1[:, 0:4 * F].rearrange("p (e f) -> p e f", f=F)
        lateg = k1[:, 4 * F:8 * F].rearrange("p (e f) -> p e f", f=F)
        midg0 = k0[:, 0:8 * F].rearrange("p (e f) -> p e f", f=F)
        midg1 = q0[:, 0:4 * F].rearrange("p (e f) -> p e f", f=F)
        w1 = [w1_early[:, e, :] if e < 12 else late1[:, e - 12, :] for e in range(S)]
        wg = [midg0[:, e, :] if e < 8 else midg1[:, e - 8, :] if e < 12 else lateg[:, e - 12, :] for e in range(S)]
        w2 = [probs[e // 8][:, e % 8, :].rearrange("p (c d) -> p c d", d=D) for e in range(S)]
        b1_rows = oT[:, :, :]
        bg_rows = q1.rearrange("p (g n) -> p g n", g=NGB)
        hT = probs[0][:, 8, :].rearrange("p (e c) -> p e c", c=32)
        uvT = [probs[0][:, 9, :], probs[0][:, 10, :]]
        ub = [probs[1][:, 8, :], probs[1][:, 9, :]]
        gb = [probs[1][:, 10, :], res[:, :]]
        uv = [resk[:, :], qp[:, 0:2, :].rearrange("p a n -> p (a n)").bitcast(F32)]
        ysb = xn[:, :, :].rearrange("p t d -> p (t d)")
        kc_heads = pd[:, :, :].rearrange("p c n -> p (c n)").rearrange("p (b h s) -> p b h s", b=B, h=H)
        vc_heads = pdT[:, :, :].rearrange("p c n -> p (c n)").rearrange("p (b h s) -> p b h s", b=B, h=H)
        vo = k0[:, 0:1024].rearrange("p (b c d) -> p b c d", b=B, c=2)
        table_probe = sb("table_probe", [P, 1])
        o_rows = sb("o_rows", [B * S, D])
        o_T = sb("o_T", [P, B * S])
        o_stats = sb("o_stats", [B * S, 6])
        o_mv = sb("o_mv", [B * S, 2])
        h_rows = sb("h_rows", [B * S, D])
        o2T = sb("o2T", [P, B, S])
        kcT = sb("kcT", [P, B, S])
        vcT = sb("vcT", [P, B, S])
        c_max = [sb(f"c_max{n}", [P, 2 * H]) for n in range(2)]
        c_sum = [sb(f"c_sum{n}", [P, 2 * H]) for n in range(2)]
        oT_flat = oT[:, :, :]
        c_exp = [oT_flat[:, 0, :], oT_flat[:, 1, :], k0[:, 1024:1536]]
        c_prob = [oT_flat[:, 2, :], oT_flat[:, 3, :]]
        c_probT = [xnT[:, :], kdT[:, :]]
        y = vd[:, :, :].rearrange("p (a t) d -> p a t d", a=2)

        names = ("x_in0 x_in1 attn_w_in ctx_in_sem slot_w_in late_w_in bout_in rows_in w1_in wg_in w2_in b1_in out_done consts pool_const "
                 "stats_done rstd_done vare_done norm_done area0_filled area0_drained area1_filled "
                 "q_first k_first res_done q_second q_third mem_copied kmem_part v_ready scores_ready scores_reduced max_chain "
                 "scoreT_ready exp_done diag_done pv_done oT_copied shift_row slotq_done qd_done "
                 "x_plus stats2_done rstd2_done vare2_done norm2_done rden_done sd_chain sd_exp od_done sum_copied "
                 "o_chain o_pool hT_copied hT_zeroed oh_ready kzero_done x_b tile_stats tile_stats2 v_zero ones_set q_zeroed sd_recip att_done attT_done x_added xn2T_done qc_done kdT_done vd_done pdT_done ad_done c_summing cols_done up_ready silu_in silu_done uv_done uvT_ready uvT_copied y_ready y_copied "
                 "yT_ready o2_done kcT_ready kcT_copied kheads_done vheads_done vo_ready vo_copied c_scored c_reduced c_shifted "
                 "c_exped c_summed c_normed c_transposed c_copied c_mixed mix_copied last_y_done y_done").split()
        s = {n: sem(n) for n in names}
        (x_in0, x_in1, attn_w_in, ctx_in_sem, slot_w_in, late_w_in, bout_in, rows_in, w1_in, wg_in, w2_in, b1_in, out_done, consts, pool_const,
         stats_done, rstd_done, vare_done, norm_done, area0_filled, area0_drained, area1_filled,
         q_first, k_first, res_done, q_second, q_third, mem_copied, kmem_part, v_ready, scores_ready, scores_reduced,
         max_chain, scoreT_ready, exp_done, diag_done, pv_done, oT_copied, shift_row, slotq_done, qd_done,
         x_plus, stats2_done, rstd2_done, vare2_done, norm2_done, rden_done, sd_chain, sd_exp, od_done, sum_copied,
         o_chain, o_pool, hT_copied, hT_zeroed, oh_ready, kzero_done, x_b, tile_stats, tile_stats2, v_zero, ones_set, q_zeroed, sd_recip, att_done, attT_done, x_added, xn2T_done, qc_done, kdT_done, vd_done, pdT_done, ad_done, c_summing, cols_done, up_ready, silu_in, silu_done, uv_done, uvT_ready, uvT_copied, y_ready, y_copied,
         yT_ready, o2_done, kcT_ready, kcT_copied, kheads_done, vheads_done, vo_ready, vo_copied, c_scored, c_reduced,
         c_shifted, c_exped, c_summed, c_normed, c_transposed, c_copied, c_mixed, mix_copied, last_y_done, y_done) = (s[n] for n in names)
        out_sent = [sem(f"out_sent{n}") for n in range(2)]
        stack_init = sem("stack_init")
        q_stacked = [sem(f"q_stacked{b}") for b in range(B)]
        k_stacked = [sem(f"k_stacked{b}") for b in range(B)]
        shift_in = [sem(f"shift_in{n}") for n in range(2)]

        NQ_DMA = [16 * (len(Q_TERMS) + (b >= 2)) for b in range(B)]
        ROWS_DMA = 16 * 6
        LATE_DMA = 16 * 12
        NK_DMA = 16 * (2 * len(K_TERMS))

        def wait_area(eng, sem_drained, n):
            if n:
                eng.wait_ge(sem_drained, n)

        def unit_of_scores(group, k):
            return SCORE_UNITS[k]

        def scores_cols(tile):
            return min(MEM + P * (tile + 1), 512)

        def projection_bank(b, name):
            first = {"xnT": scoreT_bank[0], "k": score_bank[0], "v": score_bank[1], "vmem": score_bank[2]}
            return first.get(name, area0) if b == 0 else area0

        finish_banks = [area1, *score_bank, *scoreT_bank]
        bank_of, previous, last_in = {}, {}, {}
        for name, n in AREA1.items():
            k = 0 if name[0] < B - 1 else (n - AREA1[(B - 1, "tok", 0)]) % len(finish_banks)
            bank_of[name], previous[name] = finish_banks[k], last_in.get(k)
            last_in[k] = name

        def read(name):
            b, what = name[0], name[1]
            if what == "tok":
                return att_done, NT * b + name[2] + 1
            if what in ("sd", "pT", "pv"):
                return {"sd": sd_exp, "pT": pdT_done, "pv": od_done}[what], 2 * b + name[2] + 1
            return {"att": attT_done, "out": x_added, "xn2T": xn2T_done, "qc": qc_done, "kd": kdT_done,
                    "vd": vd_done, "sum": ad_done}[what], b + 1

        block = ctx.enter_context(nc.Block())

        @block.sync
        def _(sp):
            sp.dma_start(x[:, 0, :, :], i["x"][0].rearrange("(t p) d -> p t d", p=P)).then_inc(x_in0, 16)
            sp.dma_start(ctx_in[:, :], i["ctx_1024"].rearrange("b m d -> (b m) d")).then_inc(ctx_in_sem, 16)
            sp.dma_start(wq[:, :], i["L0_xattn_Wq"]).then_inc(attn_w_in, 16)
            sp.dma_start(wkv[:, :], i["L0_xattn_Wkv"]).then_inc(attn_w_in, 16)

            def stack_q(b, part):
                for t in range(len(Q_TERMS)):
                    if Q_TERMS[t] == part:
                        sp.dma_start(q_stack[b % 2][2 * DH * t:2 * DH * (t + 1), :, :],
                                     qp[:, part, :]).then_inc(q_stacked[b], 16)

            def stack_k(b, part):
                for t in range(len(K_TERMS)):
                    if K_TERMS[t] == part:
                        for g in range(2):
                            row = 2 * DH * t + DH * g
                            sp.dma_start(k_stack[b % 2][row:row + DH, g::2, :],
                                         kp[64 * g:64 * (g + 1), part, :]).then_inc(k_stacked[b], 16)

            def stack_sequence(b):
                if b < 2:
                    sp.wait_ge(kzero_done, 2 * (b + 1))
                    sp.wait_ge(consts, 1)
                    for g in range(2):
                        sp.dma_start(k_stack[b][SHIFT_ROW + 2 * g:SHIFT_ROW + 2 * g + 2, g::2, :],
                                     one_rows[:, :]).then_inc(stack_init, 16)
                else:
                    sp.wait_ge(scoreT_ready, UNITS * NGB * (b - 1))
                    sp.wait_ge(consts, 4)
                    sp.dma_start(q_stack[b % 2][SHIFT_ROW:SHIFT_ROW + 4, :, :], zero_rows[:, :]).then_inc(q_stacked[b], 16)
                for part, (s_q, n_q, s_k, n_k) in enumerate((
                        (q_first, b + 1, k_first, b + 1),
                        (q_second, 2 * b + 1, q_second, 2 * b + 2),
                        (q_third, 2 * b + 1, q_third, 2 * b + 2))):
                    sp.wait_ge(s_q, n_q)
                    stack_q(b, part)
                    if part == 0:
                        sp.wait_ge(mem_copied, b + 1)
                    sp.wait_ge(s_k, n_k)
                    stack_k(b, part)

            def shift_rows(group):
                sp.wait_ge(area0_drained, AREA0[("shift", group)] + 1)
                b, gl = divmod(group, NGB)
                sp.dma_start(q_stack[b % 2][SHIFT_ROW:SHIFT_ROW + 4, 2 * gl:2 * gl + 2, :],
                             shiftT[group % 2][:, :]).then_inc(shift_in[group % 2], 16)

            for b in range(1, B):
                sp.dma_start(x[:, b, :, :], i["x"][b].rearrange("(t p) d -> p t d", p=P)).then_inc(x_in1, 16)
            stack_sequence(0)
            for slot in range(-LEAD, NGROUPS):
                if slot == -1:
                    sp.dma_start(bout_row[:, :], i["L0_xattn_bout"].partition_broadcast(P)).then_inc(bout_in, 16)
                    sp.dma_start(slots[:, :], i["L0_ffn_slot_query"][0]).then_inc(slot_w_in, 16)
                    sp.dma_start(wout[:, :], i["L0_xattn_Wout"]).then_inc(slot_w_in, 16)
                    sp.dma_start(dw["q"][:, :], i["L0_ffn_d_Wq"]).then_inc(slot_w_in, 16)
                    sp.dma_start(db["q"][:, :], i["L0_ffn_d_bq"].rearrange("(d o) -> d o", o=1)).then_inc(slot_w_in, 16)
                if slot > -LEAD and slot - 1 + LEAD < NGROUPS:
                    shift_rows(slot - 1 + LEAD)
                if slot % NGB == 0 and slot // NGB + 1 < B:
                    stack_sequence(slot // NGB + 1)
                if slot == 2:
                    for n in "qkvo":
                        if n != "q":
                            sp.dma_start(dw[n][:, :], i[f"L0_ffn_d_W{n}"]).then_inc(late_w_in, 16)
                        sp.dma_start(cw[n][:, :], i[f"L0_ffn_c_W{n}"]).then_inc(late_w_in, 16)
                    for n in "qkv":
                        if n != "q":
                            sp.dma_start(db[n][:, :], i[f"L0_ffn_d_b{n}"].rearrange("(d o) -> d o", o=1)).then_inc(late_w_in, 16)
                        sp.dma_start(cb[n][:, :], i[f"L0_ffn_c_b{n}"].rearrange("(d o) -> d o", o=1)).then_inc(late_w_in, 16)
                if slot == 3:
                    sp.dma_start(cbo_row[:, :], i["L0_ffn_c_bo"].partition_broadcast(P)).then_inc(rows_in, 16)
                    sp.dma_start(dbo_row[:, :], i["L0_ffn_d_bo"].partition_broadcast(B * S)).then_inc(rows_in, 16)
                    for dst, src in ((slot_rows, i["L0_ffn_slot_query"][0]), (ln_g, i["L0_ffn_e_ln_g"]),
                                     (ln_b, i["L0_ffn_e_ln_b"]), (b2_rows, i["L0_ffn_e_b2"])):
                        sp.dma_start(dst[:, :], src.partition_broadcast(B)).then_inc(rows_in, 16)
                if 4 <= slot < 12:
                    for e in (range(2) if slot < 8 else range(1)):
                        e += 2 * (slot - 4) if slot < 8 else slot
                        sp.dma_start(w1[e], i["L0_ffn_e_W1"][e]).then_inc(w1_in, 16)
                elif slot >= 12:
                    if slot == 12:
                        sp.wait_ge(scoreT_ready, UNITS * 12)
                    for e in range(3 * (slot - 12), 3 * (slot - 12) + 3):
                        sp.dma_start(wg[e], i["L0_ffn_e_Wg"][e]).then_inc(wg_in, 16)
            sp.wait_ge(scoreT_ready, UNITS * NGROUPS)
            for e in range(12, S):
                sp.dma_start(w1[e], i["L0_ffn_e_W1"][e]).then_inc(w1_in, 16)
                sp.dma_start(wg[e], i["L0_ffn_e_Wg"][e]).then_inc(wg_in, 16)
            for dst, name in ((bg_rows, "L0_ffn_e_bg"), (b1_rows, "L0_ffn_e_b1")):
                if name == "L0_ffn_e_b1":
                    sp.wait_ge(pv_done, NGROUPS)
                    for e in range(S):
                        sp.dma_start(w2[e], i["L0_ffn_e_W2"][e].rearrange("(p c) d -> p c d", c=FC)).then_inc(w2_in, 16)
                    sp.wait_ge(area1_filled, AREA1[(B - 1, "tok", NT - 1)] + 1)
                for jj in range(HG):
                    src = i[name].rearrange("(g j) f -> j g f", j=HG)[jj].partition_broadcast(32)
                    sp.dma_start(dst[32 * jj:32 * jj + 32, :, :], src).then_inc(b1_in, 16)
            for pair in range(2 * B):
                if pair < POOL_PAIRS:
                    sp.wait_ge(y_done, pair + 1)
                else:
                    sp.wait_ge(last_y_done, pair - POOL_PAIRS + 1)
                b, half = divmod(pair, 2)
                dst = out[b].rearrange("(h t p) d -> h p t d", h=2, p=P)[half]
                sp.dma_start(dst, y[:, pair % 2, :, :]).then_inc(out_sent[pair % 2], 16)
            for n in range(2):
                sp.wait_ge(out_sent[n], 16 * B)

        @block.gpsimd
        def _(pool):
            made = [0]

            def const(ins):
                made[0] += 1
                ins.then_inc(pool_const, 1)
                pool.wait_ge(pool_const, made[0])

            const(nc.gpsimd.memset(mhalf[:, :], -0.5))
            const(nc.gpsimd.memset(ident[:, :], 0.0))
            const(nc.gpsimd.affine_select(out=ident[:, :], in_=ident[:, :], compare_op=ALU.not_equal, fill=1.0,
                                          base=0, pattern=[[-1, P]], channel_multiplier=1))

            def rstd_of(n, done_stats, v, mvs, r, s_v, s_r):
                pool.wait_ge(done_stats, n + 1)
                nc.gpsimd.tensor_scalar(v, mvs, EPS, None, ALU.add).then_inc(s_v, 1)
                pool.wait_ge(s_v, n + 1)
                nc.gpsimd.tensor_tensor(r, v, mhalf[:, :], ALU.pow).then_inc(s_r, 1)

            def cut(n, parts, left, s_stacked):
                if s_stacked is not None:
                    pool.wait_ge(s_stacked[0], s_stacked[1])
                pool.wait_ge(q_second, n + 1)
                nc.gpsimd.tensor_tensor(parts[2], left, parts[1], ALU.subtract).then_inc(q_third, 1)

            def cut_q(b):
                cut(2 * b, (None, qp[:, 1, :], qp[:, 2, :]), res[:, :],
                    (q_stacked[b - 1], NQ_DMA[b - 1]) if b else None)

            def cut_k(b):
                if b:
                    copy_memory(b)
                stacked = (k_stacked[b - 1], NK_DMA) if b else None
                cut(2 * b + 1, (None, kp[:, 1, MEM:], kp[:, 2, MEM:]), resk[:, :], stacked)

            def copy_memory(b):
                pool.wait_ge(kmem_part, 4)
                if b:
                    pool.wait_ge(k_stacked[b - 1], NK_DMA)
                nc.gpsimd.tensor_copy(kp[:, :, 0:MEM], kmem[:, :, MEM * b:MEM * (b + 1)]).then_inc(mem_copied, 1)

            def diagonal(group, n):
                pr = probs[group % 2]
                pool.wait_ge(exp_done, UNITS * group + (4, 8, 10)[n])
                (lo, hi), cols = (((0, 4), (0,)), ((4, 8), (0, 384)), ((8, 10), (0, 256)))[n]
                for c in cols:
                    v = pr[:, lo:hi, c:c + P]
                    ins = nc.gpsimd.affine_select(out=v, in_=v, compare_op=ALU.is_ge, fill=0.0, base=0,
                                                  pattern=[[0, hi - lo], [1, P]], channel_multiplier=-1)
                ins.then_inc(diag_done, 1)

            def add_row(n, b, row, normalised):
                pool.wait_ge(normalised, b + 1)
                xb = x[:, b, :, :]
                nc.gpsimd.tensor_tensor(xb, xb, row[:, :].unsqueeze(1).broadcast_to([P, NT, D]),
                                        ALU.add).then_inc(n, 1)

            zeros = k0.bitcast(mybir.dt.uint32)
            nc.gpsimd.memset(zeros[:, zeros.shape[1] // 2:], 0).then_inc(kzero_done, 1)
            rstd_of(0, stats_done, vare[:, :], mv[:, :, 1], rstd[:, :], vare_done, rstd_done)
            const(nc.gpsimd.tensor_copy(identb[:, :], ident[:, :]))
            const(nc.gpsimd.memset(causal[:, :], 0.0))
            const(nc.gpsimd.affine_select(out=causal[:, :], in_=causal[:, :], compare_op=ALU.is_ge, fill=BIG,
                                          base=0, pattern=[[-1, P]], channel_multiplier=1))
            assert made[0] == CAUSAL_MADE
            copy_memory(0)
            nc.gpsimd.memset(k1.bitcast(mybir.dt.uint32), 0).then_inc(kzero_done, 2)
            cut_q(0)
            cut_k(0)
            rstd_of(1, stats_done, vare[:, :], mv[:, :, 1], rstd[:, :], vare_done, rstd_done)
            const(nc.gpsimd.memset(head_of[:, :], 1.0))
            const(nc.gpsimd.affine_select(out=head_of[:, :], in_=head_of[:, :], compare_op=ALU.is_ge, fill=0.0,
                                          base=0, pattern=[[-DH, H]], channel_multiplier=1))
            const(nc.gpsimd.affine_select(out=head_of[:, :], in_=head_of[:, :], compare_op=ALU.is_ge, fill=0.0,
                                          base=DH - 1, pattern=[[DH, H]], channel_multiplier=-1))
            const(nc.gpsimd.memset(slot_head[:, :, :], 1.0))
            const(nc.gpsimd.affine_select(out=slot_head[:, :, :], in_=slot_head[:, :, :], compare_op=ALU.is_ge,
                                          fill=0.0, base=0, pattern=[[P, 2], [-S, H]], channel_multiplier=1))
            const(nc.gpsimd.affine_select(out=slot_head[:, :, :], in_=slot_head[:, :, :], compare_op=ALU.is_ge,
                                          fill=0.0, base=S - 1, pattern=[[-P, 2], [S, H]], channel_multiplier=-1))
            const(nc.gpsimd.memset(slot_sel[:, :], 0.0))
            for r in range(P // S):
                const(nc.gpsimd.affine_select(out=slot_sel[:, :], in_=slot_sel[:, :], compare_op=ALU.not_equal,
                                              fill=1.0, base=-S * r, pattern=[[-1, S]], channel_multiplier=1))
            assert made[0] == CONSTS_MADE

            cut_q(1)

            def slot_queries():
                pool.wait_ge(area0_drained, AREA0["slotq"] + 1)
                nc.gpsimd.tensor_tensor(qd_heads[:, :, :], qdT[:, :].unsqueeze(1).broadcast_to([P, H, S]),
                                    head_of[:, :].unsqueeze(2).broadcast_to([P, H, S]), ALU.mult).then_inc(slotq_done, 1)

            for slot in range(-LEAD, SLOTS):
                for tick in range(TICKS):
                    if (slot, tick) == (-1, 0):
                        pool.wait_ge(bout_in, 16)
                        add_row(x_b, 0, bout_row, norm_done)
                    if (slot, tick) == (SLOT_QUERY_SLOT, SLOT_QUERY_TICK + 2):
                        slot_queries()
                    if (slot, tick) == (NGB, 0):
                        pool.wait_ge(rows_in, ROWS_DMA)
                        nc.gpsimd.tensor_tensor(slot_rows[:, :], slot_rows[:, :], dbo_row[:, :],
                                                ALU.add).then_inc(o_pool, 1)
                    b, n = projection_step(slot, tick)
                    if n == A_RSTD:
                        rstd_of(b, stats_done, vare[:, :], mv[:, :, 1], rstd[:, :], vare_done, rstd_done)
                    if n == A_Q + 3:
                        cut_q(b)
                    if n == A_K + 3:
                        cut_k(b)
                    if n == A_K + 6:
                        add_row(x_b, b, bout_row, norm_done)
                    b, n = finish_step(slot, tick)
                    if n == P_RSTD:
                        rstd_of(b, stats2_done, vare2[:, :], mv2[:, :, 1], rstd2[:, :], vare2_done, rstd2_done)
                    if n == P_QC:
                        add_row(x_plus, b, cbo_row, norm2_done)
                    if 0 <= slot < NGROUPS and tick in (4, 8, 11):
                        diagonal(slot, (4, 8, 11).index(tick))
            rstd_of(B - 1, stats2_done, vare2[:, :], mv2[:, :, 1], rstd2[:, :], vare2_done, rstd2_done)
            add_row(x_plus, B - 1, cbo_row, norm2_done)
            pool.wait_ge(o_chain, 3)
            nc.gpsimd.tensor_scalar(vare[0:B * S, 0:1], o_mv[:, 1:2], EPS, None, ALU.add).then_inc(o_pool, 1)
            pool.wait_ge(o_pool, 2)
            nc.gpsimd.tensor_tensor(rstd[0:B * S, 0:1], vare[0:B * S, 0:1], mhalf[0:B * S, 0:1],
                                    ALU.pow).then_inc(o_pool, 1)
            pool.wait_ge(kcT_copied, 2)
            for b in range(B):
                nc.gpsimd.tensor_tensor(vc_heads[:, b, :, :], vcT[:, b, :].unsqueeze(1).broadcast_to([P, H, S]),
                                        head_of[:, :].unsqueeze(2).broadcast_to([P, H, S]),
                                        ALU.mult).then_inc(vheads_done, 1)
            def add_residual(pair):
                b, half = divmod(pair, 2)
                pool.wait_ge(mix_copied, pair + 1)
                yp = y[:, pair % 2, :, :]
                nc.gpsimd.tensor_tensor(yp, yp, x[:, b, 2 * half:2 * half + 2, :], ALU.add).then_inc(y_done, 1)

            for pair in range(2 * B):
                if 0 <= pair - 3 < POOL_PAIRS:
                    add_residual(pair - 3)
                pool.wait_ge(c_summed, pair + 1)
                if pair >= 2:
                    pool.wait_ge(c_transposed, pair - 1)
                nc.gpsimd.tensor_tensor(c_prob[pair % 2].rearrange("p (a s) -> p a s", s=S),
                                        c_exp[pair % 3].rearrange("p (a s) -> p a s", s=S),
                                        c_sum[pair % 2][:, :].unsqueeze(2).broadcast_to([P, 2 * H, S]),
                                        ALU.mult).then_inc(c_normed, 1)
            for pair in range(2 * B - 3, POOL_PAIRS):
                add_residual(pair)

        @block.scalar
        def _(act):
            act.wait_ge(attn_w_in, 32)
            for dst, src in ((wq_cols, wq[:, :]), (wk_cols, wkv[:, 0:D])):
                src = src.rearrange("k (s g d) -> k g d s", s=H // 2, g=2)
                for g in range(2):
                    nc.scalar.activation(dst[:, 64 * g:64 * (g + 1)].rearrange("k (d s) -> k d s", d=DH),
                                         src[:, g, :, :], ACT.Copy).then_inc(cols_done, 1)
            act.wait_ge(area0_filled, AREA0["ctxT"] + 1)
            nc.scalar.activation(ctxT[:, :, :, :], area0[:, 0:P].rearrange("p (b m) -> p b m", b=B).unsqueeze(2)
                                 .broadcast_to([P, B, HG, MEM]), ACT.Copy).then_inc(area0_drained, 1)
            act.wait_ge(area0_filled, AREA0["kmem"] + 1)
            nc.scalar.activation(kmem[:, 0, :], area0[:, 0:P], ACT.Copy).then_inc(kmem_part, 1)

            def slot_queries():
                act.wait_ge(area0_filled, AREA0["slotT"] + 1)
                nc.scalar.activation(slotsT[:, :], area0[:, 0:S], ACT.Copy).then_inc(area0_drained, 1)
                act.wait_ge(area0_filled, AREA0["slotq"] + 1)
                nc.scalar.activation(qdT[:, :], area0[:, 0:S], ACT.Identity,
                                     bias=db["q"][:, 0:1]).then_inc(area0_drained, 1)

            def project(b, step):
                if step == A_T + READ:
                    act.wait_ge(area0_filled, AREA0[(b, "xnT")] + 1)
                    nc.scalar.activation(xnT[:, :], projection_bank(b, "xnT")[:, :], ACT.Copy).then_inc(area0_drained, 1)
                if step == A_Q + READ:
                    act.wait_ge(area0_filled, AREA0[(b, "q")] + 1)
                    if b:
                        act.wait_ge(q_stacked[b - 1], NQ_DMA[b - 1])
                    nc.scalar.activation(qp[:, 0, :], area0[:, :], ACT.Copy).then_inc(q_first, 1)
                if step == A_Q + 3:
                    act.wait_ge(res_done, 2 * b + 1)
                    nc.scalar.activation(qp[:, 1, :], res[:, :], ACT.Copy).then_inc(q_second, 1)
                if step == A_K + READ:
                    act.wait_ge(area0_filled, AREA0[(b, "k")] + 1)
                    if b:
                        act.wait_ge(k_stacked[b - 1], NK_DMA)
                    nc.scalar.activation(kp[:, 0, MEM:], projection_bank(b, "k")[:, :], ACT.Copy).then_inc(k_first, 1)
                if step == A_K + 3:
                    act.wait_ge(res_done, 2 * b + 2)
                    nc.scalar.activation(kp[:, 1, MEM:], resk[:, :], ACT.Copy).then_inc(q_second, 1)
                if step == A_V + READ:
                    act.wait_ge(area0_filled, AREA0[(b, "v")] + 1)
                    if b < 2:
                        act.wait_ge(consts, (2, 4)[b])
                    if b >= 2:
                        act.wait_ge(pv_done, NGB * (b - 1))
                    nc.scalar.activation(v_aug[b % 2][:, :, :, 0:DH],
                                         projection_bank(b, "v")[:, :].rearrange("p (t h d) -> p t h d", t=NT, d=DH),
                                         ACT.Copy).then_inc(area0_drained, 1)

            def finish(b, n):
                uses = finish_uses(b, n)
                if uses:
                    act_waits, bank = AREA1[uses[0]] + 1, bank_of[uses[0]]
                if n == P_ATT:
                    act.wait_ge(area1_filled, act_waits)
                    nc.scalar.activation(attT[:, :], bank[:, :], ACT.Copy).then_inc(attT_done, 1)
                if n == P_T:
                    act.wait_ge(area1_filled, act_waits)
                    nc.scalar.activation(xn2T[:, :], bank[:, :], ACT.Copy).then_inc(xn2T_done, 1)
                if n == P_QC:
                    act.wait_ge(area1_filled, act_waits)
                    nc.scalar.activation(qcT[:, b, :], bank[:, :], ACT.Identity,
                                         bias=cb["q"][:, 0:1]).then_inc(qc_done, 1)
                if n == P_KD:
                    act.wait_ge(area1_filled, act_waits)
                    nc.scalar.activation(kdT[:, :], bank[:, :], ACT.Identity,
                                         bias=db["k"][:, 0:1]).then_inc(kdT_done, 1)
                if n == P_VD:
                    act.wait_ge(area1_filled, act_waits)
                    nc.scalar.activation(vd[:, :, :].rearrange("p t d -> p (t d)"), bank[:, :],
                                         ACT.Copy).then_inc(vd_done, 1)
                if n - 1 in P_SD:
                    c = P_SD.index(n - 1)
                    bank = bank_of[(b, "sd", c)]
                    act.wait_ge(sd_chain, 2 * (2 * b + c + 1))
                    nc.scalar.activation(pd[:, c, :], bank[:, :], ACT.Exp, bias=sd_max[:, c:c + 1], scale=SCALE,
                                         accum_out=sd_sum[:, c:c + 1]).then_inc(sd_exp, 1)
                if n in P_PT:
                    act.wait_ge(area1_filled, act_waits)
                    nc.scalar.activation(pdT[:, P_PT.index(n), :], bank[:, :], ACT.Copy).then_inc(pdT_done, 1)

            def exp_unit(group, u):
                m = UNITS * group + u
                act.wait_ge(scoreT_ready, m + 1)
                if u == 0 and group >= 2:
                    act.wait_ge(pv_done, group - 1)
                nc.scalar.activation(probs[group % 2][:, u, :], scoreT_bank[m % 2][:, :], ACT.Exp,
                                     scale=SCALE).then_inc(exp_done, 1)

            def copy_oT(group):
                act.wait_ge(pv_done, group + 1)
                b, gl = divmod(group, NGB)
                if b:
                    act.wait_ge(area1_filled, AREA1[(b - 1, "tok", NT - 1)] + 1)
                nc.scalar.activation(oT[:, gl, :], pv_bank[:, :], ACT.Copy).then_inc(oT_copied, 1)

            for step in range(A_END):
                project(0, step)
            for step in range(A_K):
                project(1, step)
            for slot in range(-LEAD, SLOTS):
                for tick in range(TICKS):
                    if tick == 0 and 2 <= slot:
                        copy_oT(slot - 2)
                    if 0 <= slot < NGROUPS and tick < UNITS:
                        exp_unit(slot, tick)
                    if (slot, tick) == (SLOT_QUERY_SLOT, SLOT_QUERY_TICK):
                        slot_queries()
                    b, n = projection_step(slot, tick)
                    if b is not None:
                        project(b, n)
                    b, n = finish_step(slot, tick - READ)
                    if b is not None:
                        finish(b, n)
            for n in range(P_END):
                finish(B - 1, n)

            act.wait_ge(pool_const, 1)
            nc.scalar.activation(table_probe[:, :], mhalf[:, 0:1], ACT.Silu)
            act.wait_ge(oh_ready, 2)
            act.wait_ge(hT_zeroed, 1)
            nc.scalar.activation(hT[:, :, 0:B], area1[:, 0:B * S].rearrange("p (b e) -> p e b", b=B),
                                 ACT.Copy).then_inc(hT_copied, 1)
            nc.scalar.activation(o_T[:, :], area1[:, B * S:2 * B * S], ACT.Copy).then_inc(hT_copied, 1)

            def copy_uvT(g):
                act.wait_ge(uvT_ready, g + 1)
                if g >= 2:
                    act.wait_ge(y_ready, g - 1)
                nc.scalar.activation(uvT[g % 2], scoreT_bank[g % 2][:, :], ACT.Copy).then_inc(uvT_copied, 1)

            def silu(n):
                act.wait_ge(silu_in, n + 1)
                t = (ub, gb)[n % 2][n // 2 % 2]
                nc.scalar.activation(t, t, ACT.Silu).then_inc(silu_done, 1)

            for n in range(2 * NGB):
                silu(n)
                if n >= 3 and n % 2:
                    copy_uvT((n - 3) // 2)
            copy_uvT(NGB - 1)
            nc.scalar.activation(table_probe[:, :], mhalf[:, 0:1], ACT.Exp)
            act.wait_ge(kcT_ready, 1)
            nc.scalar.activation(kcT[:, :, :].rearrange("p b s -> p (b s)"), area0[:, 0:B * S], ACT.Identity,
                                 bias=cb["k"][:, 0:1]).then_inc(kcT_copied, 1)
            nc.scalar.activation(vcT[:, :, :].rearrange("p b s -> p (b s)"), area0[:, B * S:2 * B * S], ACT.Identity,
                                 bias=cb["v"][:, 0:1]).then_inc(kcT_copied, 1)
            for c in range(2):
                act.wait_ge(vo_ready, c + 1)
                nc.scalar.activation(vo[:, 2 * c:2 * c + 2, :, :].rearrange("p b c d -> p (b c d)"),
                                     (area1, pv_bank)[c][:, :], ACT.Copy).then_inc(vo_copied, 1)

            def c_exponentiate(pair):
                act.wait_ge(c_shifted, pair + 1)
                nc.scalar.activation(c_exp[pair % 3], c_exp[pair % 3], ACT.Exp, scale=SCALE).then_inc(c_exped, 1)

            def c_copy(pair):
                act.wait_ge(c_transposed, pair + 1)
                if pair >= 2:
                    act.wait_ge(c_mixed, pair - 1)
                nc.scalar.activation(c_probT[pair % 2], scoreT_bank[pair % 2][:, :], ACT.Copy).then_inc(c_copied, 1)

            def mix_copy(pair):
                act.wait_ge(c_mixed, pair + 1)
                if pair >= 2:
                    act.wait_ge(out_sent[pair % 2], 16 * (pair // 2))
                nc.scalar.activation(y[:, pair % 2, :, :].rearrange("p t d -> p (t d)"),
                                     (area0, area1)[pair % 2][:, 0:2 * D], ACT.Copy).then_inc(mix_copied, 1)

            for pair in range(2 * B):
                c_exponentiate(pair)
                if 0 <= pair - 3 < POOL_PAIRS:
                    mix_copy(pair - 3)
                if pair:
                    c_copy(pair - 1)
            c_copy(2 * B - 1)
            for pair in range(2 * B - 3, POOL_PAIRS):
                mix_copy(pair)

        @block.tensor
        def _(pe):
            wv = wkv[:, D:2 * D]
            shift_bank = area0[:, :].bitcast(BF16)

            def use0(name):
                if AREA0[name]:
                    pe.wait_ge(area0_drained, AREA0[name])

            def use1(name):
                if previous[name] is not None:
                    pe.wait_ge(*read(previous[name]))

            pe.wait_ge(pool_const, 3)
            pe.wait_ge(ctx_in_sem, 16)
            nc.tensor.transpose(area0[:, 0:P], ctx_in[:, :], ident[:, :]).then_inc(area0_filled, 1)
            pe.wait_ge(cols_done, 4)
            use0("kmem")
            nc.tensor.matmul(area0[:, 0:P], wk_cols[:, :], ctxT[:, :, 0, :], start=True, stop=True).then_inc(area0_filled, 1)

            def slot_queries():
                pe.wait_ge(slot_w_in, 16 * 4)
                use0("slotT")
                nc.tensor.transpose(area0[:, 0:S], slots[:, :], ident[0:S, 0:S]).then_inc(area0_filled, 1)
                use0("slotq")
                nc.tensor.matmul(area0[:, 0:S], dw["q"][:, :], slotsT[:, :], start=True,
                                 stop=True).then_inc(area0_filled, 1)

            def project(b, step):
                if step in PROJ_USES:
                    bank = projection_bank(b, PROJ_USES[step])
                    if bank is area0:
                        use0((b, PROJ_USES[step]))
                if step == A_T:
                    pe.wait_ge(norm_done, b + 1)
                    for t in range(NT):
                        mm = nc.tensor.transpose(bank[:, P * t:P * (t + 1)], xn[:, t, :], ident[:, :])
                    mm.then_inc(area0_filled, 1)
                if step == A_Q:
                    nc.tensor.matmul(bank[:, :], wq_cols[:, :], xnT[:, :], start=True, stop=True).then_inc(area0_filled, 1)
                if step == A_K:
                    nc.tensor.matmul(bank[:, :], wk_cols[:, :], xnT[:, :], start=True, stop=True).then_inc(area0_filled, 1)
                if step == A_V:
                    for t in range(NT):
                        mm = nc.tensor.matmul(bank[:, P * t:P * (t + 1)], xnT[:, P * t:P * (t + 1)], wv,
                                              start=True, stop=True)
                    mm.then_inc(area0_filled, 1)
                if step == A_VM:
                    mem = ctxT[:, b, :, :].rearrange("p j m -> p (j m)")
                    nc.tensor.matmul(bank[:, 0:D], mem, wv, start=True, stop=True).then_inc(area0_filled, 1)

            def score_unit(group, k):
                n = TICKS * group + k
                b, gl = divmod(group, NGB)
                tile, heads = unit_of_scores(group, k)
                if k == 0 and gl == 0:
                    pe.wait_ge(q_stacked[b], NQ_DMA[b])
                    pe.wait_ge(k_stacked[b], NK_DMA)
                    if b < 2:
                        pe.wait_ge(stack_init, 32 * (b + 1))
                        pe.wait_ge(q_zeroed, b + 1)
                    if b == 0:
                        pe.wait_ge(pool_const, CAUSAL_MADE)
                        pe.wait_ge(area0_drained, AREA0[(0, "vmem")] + 1)
                if n >= 3:
                    pe.wait_ge(scores_reduced, n - 2)
                bank = score_bank[n % 3]
                q, keys = q_stack[b % 2], k_stack[b % 2]
                cols = scores_cols(tile)
                first = True

                def masked(h, t, at, lo, hi):
                    nonlocal first
                    nc.tensor.matmul(bank[:, at:at + hi - lo], q[:, h // 2, P * t:P * (t + 1)], keys[:, h, lo:hi],
                                     start=first, stop=False, skip_group_check=True)
                    first = False
                    d = MEM + P * t
                    a = max(lo, d)
                    return nc.tensor.matmul(bank[:, at + a - lo:at + hi - lo], identb[:, :], causal[:, a - d:hi - d],
                                            start=False, stop=True, skip_group_check=True)

                for m, hj in enumerate(heads):
                    mm = masked(HG * gl + hj, tile, cols * m, 0, cols)
                if tile == 0:
                    for m, hj in enumerate(heads):
                        mm = masked(HG * gl + hj, NT - 1, cols * len(heads) + MEM * m, 512, KEYS)
                mm.then_inc(scores_ready, 1)

            def shift_rows(group):
                use0(("shift", group))
                pe.wait_ge(max_chain, 3 * (group + 1))
                for t in range(NT):
                    mm = nc.tensor.transpose(shift_bank[0:8, P * t:P * (t + 1)],
                                             shift[group % 2][:, t].rearrange("p g a s -> p (g a s)"), identb[:, :])
                mm.then_inc(area0_filled, 1)

            def scoreT_unit(group, u):
                m = UNITS * group + u
                b, gl = divmod(group, NGB)
                if u == 0:
                    pe.wait_ge(shift_in[group % 2], 16 * (group // 2 + 1))
                if m >= 2:
                    pe.wait_ge(exp_done, m - 1)
                bank = scoreT_bank[m % 2]
                q, keys = q_stack[b % 2], k_stack[b % 2]

                def block_of(h, j, at):
                    return nc.tensor.matmul(bank[:, at:at + T - P * j], keys[:, h, MEM + P * j:MEM + P * (j + 1)],
                                            q[:, h // 2, P * j:T], start=(at == 0), stop=True, skip_group_check=True)

                if u < 4:
                    mm = block_of(HG * gl + u, 0, 0)
                elif u < 8:
                    block_of(HG * gl + u - 4, 1, 0)
                    mm = block_of(HG * gl + u - 4, 3, 384)
                elif u < 10:
                    for r in range(2):
                        mm = block_of(HG * gl + 2 * (u - 8) + r, 2, 256 * r)
                else:
                    for j in range(HG):
                        h = HG * gl + j
                        mm = nc.tensor.matmul(bank[32 * j:32 * j + MEM, :], keys[:, h, 0:MEM], q[:, h // 2, :],
                                              start=True, stop=True)
                mm.then_inc(scoreT_ready, 1)

            def pv_piece(group, piece):
                b, gl = divmod(group, NGB)
                pr, v = probs[group % 2], v_aug[b % 2]
                if piece == 0:
                    pe.wait_ge(exp_done, UNITS * (group + 1))
                    if gl == 0:
                        pe.wait_ge(area0_drained, AREA0[(b, "vmem")] + 1)
                    if group:
                        pe.wait_ge(oT_copied, group)
                    nc.tensor.matmul(pv_bank[:, :], v_mem[b % 2][:, gl, :], pr[:, 10, :], start=True, stop=False,
                                     skip_group_check=True)
                    return
                j = (0, 1, 2, 3)[piece - 1]
                pe.wait_ge(diag_done, 3 * group + (1, 2, 3, 3)[j])
                for hj in range(HG):
                    src = (pr[:, hj, :], pr[:, 4 + hj, 0:384], pr[:, 8 + hj // 2, 256 * (hj % 2):256 * (hj % 2) + 256],
                           pr[:, 4 + hj, 384:512])[j]
                    mm = nc.tensor.matmul(pv_bank[32 * hj:32 * hj + DH + 1, P * j:T], v[:, j, HG * gl + hj, :], src,
                                          start=False, stop=(j == 3), skip_group_check=True)
                if j == 3:
                    mm.then_inc(pv_done, 1)

            def finish(b, n):
                for name in finish_uses(b, n):
                    use1(name)
                    bank = bank_of[name]
                if n in P_TOK:
                    t = P_TOK.index(n)
                    pe.wait_ge(oT_copied, NGB * (b + 1))
                    for gl in range(NGB):
                        mm = nc.tensor.transpose(bank[:, P * gl:P * (gl + 1)], oT[:, gl, P * t:P * (t + 1)], ident[:, :])
                elif n == P_ATT or n == P_T:
                    if n == P_T:
                        pe.wait_ge(norm2_done, b + 1)
                    else:
                        pe.wait_ge(*read((b, "tok", NT - 1)))
                        if b == 0:
                            pe.wait_ge(slot_w_in, 16 * 4)
                    for t in range(NT):
                        mm = nc.tensor.transpose(bank[:, P * t:P * (t + 1)], att[:, t, :], ident[:, :])
                elif n == P_OUT:
                    pe.wait_ge(attT_done, b + 1)
                    for t in range(NT):
                        mm = nc.tensor.matmul(bank[:, P * t:P * (t + 1)], attT[:, P * t:P * (t + 1)], wout[:, :],
                                              start=True, stop=True)
                elif n == P_QC:
                    pe.wait_ge(xn2T_done, b + 1)
                    mm = nc.tensor.matmul(bank[:, :], cw["q"][:, :], xn2T[:, :], start=True, stop=True)
                elif n == P_KD:
                    pe.wait_ge(xn2T_done, b + 1)
                    pe.wait_ge(late_w_in, LATE_DMA)
                    mm = nc.tensor.matmul(bank[:, :], dw["k"][:, :], xn2T[:, :], start=True, stop=True)
                elif n == P_VD:
                    for t in range(NT):
                        mm = nc.tensor.matmul(bank[:, P * t:P * (t + 1)], xn2T[:, P * t:P * (t + 1)], dw["v"][:, :],
                                              start=True, stop=True)
                elif n in P_SD:
                    c = P_SD.index(n)
                    pe.wait_ge(slotq_done, 1)
                    pe.wait_ge(kdT_done, b + 1)
                    mm = nc.tensor.matmul(bank[:, :], qd_heads[:, 8 * c:8 * c + 8, :].rearrange("p h s -> p (h s)"),
                                          kdT[:, :], start=True, stop=True)
                elif n in P_PT:
                    c = P_PT.index(n)
                    pe.wait_ge(sd_exp, 2 * b + c + 1)
                    for t in range(NT):
                        mm = nc.tensor.transpose(bank[:, P * t:P * (t + 1)], pd[:, c, P * t:P * (t + 1)],
                                                 ident[:, :])
                elif n in P_PV:
                    c = P_PV.index(n)
                    pe.wait_ge(pdT_done, 2 * b + c + 1)
                    pe.wait_ge(vd_done, b + 1)
                    for t in range(NT):
                        mm = nc.tensor.matmul(bank[:, 0:D], pdT[:, c, P * t:P * (t + 1)], vd[:, t, :],
                                              start=(t == 0), stop=(t == NT - 1))
                elif n == P_SUM:
                    pe.wait_ge(od_done, 2 * b + 2)
                    pe.wait_ge(pool_const, CONSTS_MADE)
                    for c in range(2):
                        mm = nc.tensor.matmul(bank[:, 0:S], od[:, c, :], slot_sel[:, :], start=(c == 0), stop=(c == 1))
                else:
                    return
                mm.then_inc(area1_filled, 1)

            for step in range(A_END):
                project(0, step)
            for step in range(A_K):
                project(1, step)
            for slot in range(-LEAD, SLOTS):
                for tick in range(TICKS):
                    if slot + LEAD < NGROUPS:
                        score_unit(slot + LEAD, tick)
                    if 0 <= slot < NGROUPS and tick < UNITS:
                        scoreT_unit(slot, tick)
                    if 1 <= slot <= NGROUPS and tick in PV_TICKS:
                        pv_piece(slot - 1, PV_TICKS.index(tick))
                    if tick == SHIFT_TICK and slot > -LEAD and slot - 1 + LEAD < NGROUPS:
                        shift_rows(slot - 1 + LEAD)
                    if (slot, tick) == (SLOT_QUERY_SLOT, SLOT_QUERY_TICK):
                        slot_queries()
                    b, n = projection_step(slot, tick)
                    if b is not None:
                        project(b, n)
                    b, n = finish_step(slot, tick)
                    if b is not None:
                        finish(b, n)
            for n in range(P_END):
                finish(B - 1, n)

            pe.wait_ge(ad_done, B)
            nc.tensor.matmul(area0[0:B * S, 0:D], adT[:, :, :].rearrange("p b s -> p (b s)"), dw["o"][:, :],
                             start=True, stop=True).then_inc(oh_ready, 1)
            pe.wait_ge(o_chain, 7)
            nc.tensor.transpose(area1[:, 0:B * S], h_rows[:, :], ident[0:B * S, 0:B * S])
            nc.tensor.transpose(area1[:, B * S:2 * B * S], o_rows[:, :], ident[0:B * S, 0:B * S]).then_inc(oh_ready, 1)
            pe.wait_ge(hT_copied, 1)
            up_banks = [*score_bank, area0, area1]

            def up(g, k):
                n = 2 * g + k
                if n == 0:
                    pe.wait_ge(w1_in, 16 * S)
                    pe.wait_ge(wg_in, 16 * S)
                if n == 4:
                    pe.wait_ge(hT_copied, 2)
                if n >= len(up_banks):
                    pe.wait_ge(silu_in, n - len(up_banks) + 1)
                for j in range(HG):
                    mm = nc.tensor.matmul(up_banks[n % len(up_banks)][32 * j:32 * j + 32, :], hT[:, HG * g + j, :],
                                          (w1, wg)[k][HG * g + j], start=True, stop=True)
                mm.then_inc(up_ready, 1)

            def turn(g):
                pe.wait_ge(uv_done, g + 1)
                if g >= 2:
                    pe.wait_ge(uvT_copied, g - 1)
                for c in range(FC):
                    mm = nc.tensor.transpose(scoreT_bank[g % 2][:, P * c:P * (c + 1)], uv[g % 2][:, c::FC], ident[:, :])
                mm.then_inc(uvT_ready, 1)

            def down(g):
                pe.wait_ge(uvT_copied, g + 1)
                if g == 0:
                    pe.wait_ge(w2_in, 16 * S)
                if g == 1:
                    pe.wait_ge(silu_in, 4)
                if g >= 2:
                    pe.wait_ge(y_copied, g - 1)
                for c in range(FC):
                    for j in range(HG):
                        e = HG * g + j
                        mm = nc.tensor.matmul((pv_bank, area0)[g % 2][32 * j:32 * j + 32, 0:D],
                                              uvT[g % 2][:, P * c + 32 * j:P * c + 32 * j + 32],
                                              w2[e][:, c, :], start=(c == 0), stop=(c == FC - 1),
                                              skip_group_check=True)
                mm.then_inc(y_ready, 1)

            def turn_y(g):
                pe.wait_ge(y_copied, g + 1)
                if g == 0:
                    pe.wait_ge(silu_in, 5)
                nc.tensor.transpose(area1[:, P * g:P * (g + 1)], ysb[:, P * g:P * (g + 1)],
                                    ident[:, :]).then_inc(yT_ready, 1)

            for g, k in ((0, 0), (0, 1), (1, 0), (1, 1), (2, 0)):
                up(g, k)
            turn(0)
            up(2, 1)
            down(0)
            turn(1)
            up(3, 0)
            down(1)
            up(3, 1)
            turn(2)
            turn_y(0)
            down(2)
            turn_y(1)
            turn(3)
            turn_y(2)
            down(3)
            turn_y(3)
            pe.wait_ge(o2_done, 1)
            o2 = o2T[:, :, :].rearrange("p b s -> p (b s)")
            nc.tensor.matmul(area0[:, 0:B * S], cw["k"][:, :], o2, start=True, stop=True)
            nc.tensor.matmul(area0[:, B * S:2 * B * S], cw["v"][:, :], o2, start=True, stop=True).then_inc(kcT_ready, 1)

            def c_scores(pair):
                b, half = divmod(pair, 2)
                pe.wait_ge(kheads_done, b + 1)
                if pair >= 3:
                    pe.wait_ge(c_shifted, pair - 2)
                for r in range(2):
                    t = 2 * half + r
                    mm = nc.tensor.matmul(score_bank[pair % 3][:, 256 * r:256 * (r + 1)], qcT[:, b, P * t:P * (t + 1)],
                                          kc_heads[:, b, :, :].rearrange("p h s -> p (h s)"), start=True, stop=True)
                mm.then_inc(c_scored, 1)

            def c_transpose(pair):
                pe.wait_ge(c_normed, pair + 1)
                if pair >= 2:
                    pe.wait_ge(c_copied, pair - 1)
                for c in range(4):
                    mm = nc.tensor.transpose(scoreT_bank[pair % 2][:, P * c:P * (c + 1)],
                                             c_prob[pair % 2][:, P * c:P * (c + 1)], ident[:, :])
                mm.then_inc(c_transposed, 1)

            def c_mix(pair):
                b, half = divmod(pair, 2)
                pe.wait_ge(c_copied, pair + 1)
                pe.wait_ge(vo_copied, 2)
                if pair >= 2:
                    pe.wait_ge(mix_copied, pair - 1)
                for r in range(2):
                    for c in range(2):
                        mm = nc.tensor.matmul((area0, area1)[pair % 2][:, D * r:D * (r + 1)],
                                              c_probT[pair % 2][:, P * (2 * r + c):P * (2 * r + c + 1)],
                                              vo[:, b, c, :], start=(c == 0), stop=(c == 1))
                mm.then_inc(c_mixed, 1)

            c_scores(0)
            c_scores(1)
            pe.wait_ge(vheads_done, B)
            for b in range(B):
                for c in range(2):
                    mm = nc.tensor.matmul((area1, pv_bank)[b // 2][:, D * (2 * (b % 2) + c):D * (2 * (b % 2) + c + 1)],
                                          vc_heads[:, b, 8 * c:8 * c + 8, :].rearrange("p h s -> p (h s)"),
                                          cw["o"][:, :], start=True, stop=True)
                if b % 2:
                    mm.then_inc(vo_ready, 1)
            for pair in range(2 * B):
                if pair + 2 < 2 * B:
                    c_scores(pair + 2)
                c_transpose(pair)
                if pair:
                    c_mix(pair - 1)
            c_mix(2 * B - 1)

        @block.vector
        def _(dve):
            U32 = mybir.dt.uint32
            zeros = k0.bitcast(U32)
            nc.vector.memset(zeros[:, 0:zeros.shape[1] // 2], 0).then_inc(kzero_done, 1)
            nc.vector.memset(one_rows[:, :], 1.0).then_inc(consts, 1)

            def norm_stats(n, src, st, m, done, per_tile):
                for t in range(NT):
                    nc.vector.bn_stats(st[:, t, :], src[:, t, :]).then_inc(per_tile, 1)
                dve.wait_ge(per_tile, NT * (n + 1))
                for t in range(NT):
                    ins = nc.vector.bn_aggr(m[:, t, :], st[:, t, :])
                ins.then_inc(done, 1)

            def normalise(n, src, dst, m, r, s_r, done):
                dve.wait_ge(s_r, n + 1)
                for t in range(NT):
                    ins = nc.vector.tensor_scalar(dst[:, t, :], src[:, t, :], m[:, t, 0:1], r[:, t:t + 1],
                                                  ALU.subtract, ALU.mult)
                ins.then_inc(done, 1)

            def values_ones(n):
                for j in range(HG):
                    nc.vector.memset(v_mem[n][32 * j:32 * j + 32, :, 32 * j + DH:32 * j + DH + 1], 1.0).then_inc(ones_set, 1)
                nc.vector.memset(v_aug[n][:, :, :, DH:DH + 1], 1.0).then_inc(consts, 1)

            def project(b, step):
                if step == A_STATS:
                    dve.wait_ge(x_in0 if b == 0 else x_in1, 16 if b == 0 else 16 * (B - 1))
                    norm_stats(b, x[:, b, :, :], stats, mv, stats_done, tile_stats)
                if step == A_NORM:
                    if b:
                        dve.wait_ge(area0_filled, AREA0[(b - 1, "xnT")] + 1)
                    normalise(b, x[:, b, :, :], xn, mv, rstd, rstd_done, norm_done)
                if step == A_Q + 2:
                    dve.wait_ge(q_first, b + 1)
                    if b:
                        dve.wait_ge(q_third, 2 * b - 1)
                    nc.vector.tensor_tensor(res[:, :], area0[:, :], qp[:, 0, :], ALU.subtract).then_inc(res_done, 1)
                    dve.wait_ge(res_done, 2 * b + 1)
                    dve.sem_inc(area0_drained, 1)
                if step == A_K + 2:
                    dve.wait_ge(k_first, b + 1)
                    if b:
                        dve.wait_ge(q_third, 2 * b)
                    nc.vector.tensor_tensor(resk[:, :], projection_bank(b, "k")[:, :], kp[:, 0, MEM:], ALU.subtract).then_inc(res_done, 1)
                    dve.wait_ge(res_done, 2 * b + 2)
                    dve.sem_inc(area0_drained, 1)
                if step == A_VM + READ:
                    dve.wait_ge(area0_filled, AREA0[(b, "vmem")] + 1)
                    dve.wait_ge(ones_set, HG * (1 + (b > 0)))
                    if b >= 2:
                        dve.wait_ge(pv_done, NGB * (b - 1))
                    for j in range(HG):
                        rows = slice(32 * j, 32 * j + 32)
                        ins = nc.vector.tensor_copy(
                            v_mem[b % 2][rows, :, 32 * j:32 * j + DH],
                            projection_bank(b, "vmem")[rows, 0:D].rearrange("p (g j d) -> p g j d", g=NGB, j=HG)[:, :, j, :])
                    ins.then_inc(area0_drained, 1)

            def reduce_unit(group, k):
                n = TICKS * group + k
                tile, heads = unit_of_scores(group, k)
                dve.wait_ge(scores_ready, n + 1)
                bank = score_bank[n % 3]
                m, cols = rowmax[group % 2], scores_cols(tile)
                if tile == 0:
                    nc.vector.tensor_reduce(m[:, 0, :, heads[0] // 2], bank[:, 0:2 * cols].rearrange("p (a n) -> p a n", a=2),
                                            AX.X, ALU.max)
                    nc.vector.tensor_reduce(tailmax[group % 2][:, :, heads[0] // 2],
                                            bank[:, 2 * cols:2 * cols + 2 * MEM].rearrange("p (a n) -> p a n", a=2),
                                            AX.X, ALU.max).then_inc(scores_reduced, 1)
                else:
                    h = heads[0]
                    nc.vector.tensor_reduce(m[:, tile, h % 2, h // 2:h // 2 + 1], bank[:, 0:cols], AX.X,
                                            ALU.max).then_inc(scores_reduced, 1)

            def shift_of(group):
                m, sh = rowmax[group % 2], shift[group % 2]
                dve.wait_ge(scores_reduced, TICKS * (group + 1))
                if group >= 2:
                    dve.wait_ge(area0_filled, AREA0[("shift", group - 2)] + 1)
                last = m[:, NT - 1, :, :].rearrange("p g s -> p (g s)")
                nc.vector.tensor_tensor(last, last, tailmax[group % 2][:, :, :].rearrange("p g s -> p (g s)"),
                                        ALU.max).then_inc(max_chain, 1)
                dve.wait_ge(max_chain, 3 * group + 1)
                mm = m[:, :, :, :].rearrange("p t g s -> p (t g) s")
                hi = sh[:, :, :, 0, :].rearrange("p t g s -> p (t g) s")
                lo = sh[:, :, :, 1, :].rearrange("p t g s -> p (t g) s")
                nc.vector.tensor_scalar(hi, mm, -1.0, None, ALU.mult).then_inc(max_chain, 1)
                dve.wait_ge(max_chain, 3 * group + 2)
                nc.vector.scalar_tensor_tensor(out=lo, in0=mm, scalar=-1.0, in1=hi, op0=ALU.mult,
                                               op1=ALU.subtract).then_inc(max_chain, 1)

            def shift_copy(group):
                dve.wait_ge(area0_filled, AREA0[("shift", group)] + 1)
                if group >= 2:
                    dve.wait_ge(shift_in[group % 2], 16 * (group // 2))
                nc.vector.tensor_copy(shiftT[group % 2][:, :], area0[:, :].bitcast(BF16)[0:8, 0:T])\
                    .then_inc(area0_drained, 1)

            def finish(b, n):
                for name in finish_uses(b, n):
                    filled, bank = AREA1[name] + 1, bank_of[name]
                if n in P_TOK:
                    t = P_TOK.index(n)
                    if t == 0 and b:
                        dve.wait_ge(att_done, NT * b)
                    heads = bank[:, :].rearrange("p (h c) -> p h c", h=H)
                    dve.wait_ge(area1_filled, filled)
                    nc.vector.reciprocal(rden[:, t, :], heads[:, :, DH]).then_inc(rden_done, 1)
                    dve.wait_ge(rden_done, NT * b + t + 1)
                    nc.vector.tensor_tensor(att[:, t, :].rearrange("p (h d) -> p h d", h=H), heads[:, :, 0:DH],
                                            rden[:, t, :].unsqueeze(2).broadcast_to([P, H, DH]),
                                            ALU.mult).then_inc(att_done, 1)
                if n == P_OUT:
                    dve.wait_ge(area1_filled, filled)
                    dve.wait_ge(x_b, b + 1)
                    xb = x[:, b, :, :].rearrange("p t d -> p (t d)")
                    nc.vector.tensor_tensor(xb, bank[:, :], xb, ALU.add).then_inc(x_added, 1)
                if n == P_STATS:
                    dve.wait_ge(x_added, b + 1)
                    norm_stats(b, x[:, b, :, :], stats2, mv2, stats2_done, tile_stats2)
                if n == P_NORM:
                    normalise(b, x[:, b, :, :], xn2, mv2, rstd2, rstd2_done, norm2_done)
                if n in P_SD:
                    c = P_SD.index(n)
                    dve.wait_ge(area1_filled, filled)
                    nc.vector.tensor_reduce(sd_max[:, c:c + 1], bank[:, :], AX.X, ALU.max,
                                            negate=True).then_inc(sd_chain, 1)
                    dve.wait_ge(sd_chain, 2 * (2 * b + c) + 1)
                    nc.vector.tensor_scalar(sd_max[:, c:c + 1], sd_max[:, c:c + 1], SCALE, None,
                                            ALU.mult).then_inc(sd_chain, 1)
                if n in P_PV:
                    c = P_PV.index(n)
                    dve.wait_ge(area1_filled, filled)
                    dve.wait_ge(sd_exp, 2 * b + c + 1)
                    nc.vector.reciprocal(sd_r[:, c:c + 1], sd_sum[:, c:c + 1]).then_inc(sd_recip, 1)
                    dve.wait_ge(sd_recip, 2 * b + c + 1)
                    nc.vector.scalar_tensor_tensor(
                        out=od[:, c, :].rearrange("p (h d) -> p h d", h=H),
                        in0=bank[:, 0:D].rearrange("p (h d) -> p h d", h=H), scalar=sd_r[:, c:c + 1],
                        in1=slot_head[:, c, :].unsqueeze(2).broadcast_to([P, H, DH]),
                        op0=ALU.mult, op1=ALU.mult).then_inc(od_done, 1)
                if n == P_SUM:
                    dve.wait_ge(area1_filled, filled)
                    nc.vector.tensor_scalar(adT[:, b, :], bank[:, 0:S], db["v"][:, 0:1], None,
                                            ALU.add).then_inc(ad_done, 1)

            project(0, A_STATS)
            nc.vector.memset(v_mem[0][:, :, :], 0.0).then_inc(v_zero, 1)
            project(0, A_NORM)
            dve.wait_ge(kmem_part, 1)
            nc.vector.tensor_tensor(resk[:, 0:P], area0[:, 0:P], kmem[:, 0, :], ALU.subtract).then_inc(kmem_part, 1)
            dve.wait_ge(kmem_part, 2)
            dve.sem_inc(area0_drained, 1)
            nc.vector.tensor_copy(kmem[:, 1, :], resk[:, 0:P]).then_inc(kmem_part, 1)
            dve.wait_ge(kmem_part, 3)
            nc.vector.tensor_tensor(kmem[:, 2, :], resk[:, 0:P], kmem[:, 1, :], ALU.subtract).then_inc(kmem_part, 1)
            nc.vector.memset(q0[SHIFT_ROW:P, :].bitcast(U32), 0).then_inc(q_zeroed, 1)
            dve.wait_ge(v_zero, 1)
            values_ones(0)
            dve.wait_ge(kmem_part, 4)
            for step in range(A_NORM + 1, A_END):
                project(0, step)
            project(1, A_STATS)
            nc.vector.memset(v_mem[1][:, :, :], 0.0).then_inc(v_zero, 1)
            nc.vector.memset(zero_rows[:, :], 0.0).then_inc(consts, 1)
            for step in range(A_STATS + 1, A_K):
                project(1, step)
            nc.vector.memset(q1[SHIFT_ROW:P, :].bitcast(U32), 0).then_inc(q_zeroed, 1)
            dve.wait_ge(v_zero, 2)
            values_ones(1)
            for slot in range(-LEAD, SLOTS):
                for tick in range(TICKS):
                    if slot + LEAD < NGROUPS:
                        reduce_unit(slot + LEAD, tick)
                    if tick == MAX_TICK and slot > -LEAD and slot - 1 + LEAD < NGROUPS:
                        shift_of(slot - 1 + LEAD)
                    if tick == SHIFT_TICK + READ and slot > -LEAD and slot - 1 + LEAD < NGROUPS:
                        shift_copy(slot - 1 + LEAD)
                    b, n = projection_step(slot, tick)
                    if b is not None:
                        project(b, n)
                    b, n = finish_step(slot, tick - READ)
                    if b is not None:
                        finish(b, n)
            dve.wait_ge(pv_done, NGROUPS - 1)
            nc.vector.memset(hT, 0.0).then_inc(hT_zeroed, 1)
            for n in range(P_END):
                finish(B - 1, n)

            dve.wait_ge(oh_ready, 1)
            dve.wait_ge(o_pool, 1)
            nc.vector.tensor_tensor(o_rows[:, :], area0[0:B * S, 0:D], slot_rows[:, :], ALU.add).then_inc(o_chain, 1)
            dve.wait_ge(o_chain, 1)
            nc.vector.bn_stats(o_stats[:, :], o_rows[:, :]).then_inc(o_chain, 1)
            dve.wait_ge(o_chain, 2)
            nc.vector.bn_aggr(o_mv[:, :], o_stats[:, :]).then_inc(o_chain, 1)
            dve.wait_ge(o_pool, 3)
            nc.vector.tensor_scalar(h_rows[:, :], o_rows[:, :], o_mv[:, 0:1], rstd[0:B * S, 0:1], ALU.subtract,
                                    ALU.mult).then_inc(o_chain, 1)
            dve.wait_ge(o_chain, 4)
            nc.vector.tensor_tensor(h_rows[:, :], h_rows[:, :], ln_g[:, :], ALU.mult).then_inc(o_chain, 1)
            dve.wait_ge(o_chain, 5)
            nc.vector.tensor_tensor(h_rows[:, :], h_rows[:, :], ln_b[:, :], ALU.add).then_inc(o_chain, 1)
            nc.vector.tensor_tensor(o_rows[:, :], o_rows[:, :], b2_rows[:, :], ALU.add).then_inc(o_chain, 1)
            up_banks = [*score_bank, area0, area1]

            def add_bias(g, k):
                n = 2 * g + k
                if n == 0:
                    dve.wait_ge(b1_in, 16 * 2 * HG)
                dve.wait_ge(up_ready, n + 1)
                nc.vector.tensor_tensor((ub, gb)[k][g % 2], up_banks[n % len(up_banks)][:, :], (b1_rows, bg_rows)[k][:, g, :],
                                        ALU.add).then_inc(silu_in, 1)

            def times(g):
                dve.wait_ge(silu_done, 2 * g + 2)
                if g >= 2:
                    dve.wait_ge(uvT_ready, g - 1)
                nc.vector.tensor_tensor(uv[g % 2], ub[g % 2], gb[g % 2], ALU.mult).then_inc(uv_done, 1)

            for g in range(NGB):
                if g >= 2:
                    dve.wait_ge(uv_done, g - 1)
                add_bias(g, 0)
                if g:
                    times(g - 1)
                add_bias(g, 1)
            times(NGB - 1)
            for g in range(NGB):
                dve.wait_ge(y_ready, g + 1)
                nc.vector.tensor_copy(ysb[:, P * g:P * (g + 1)], (pv_bank, area0)[g % 2][:, 0:P]).then_inc(y_copied, 1)
            dve.wait_ge(yT_ready, NGB)
            nc.vector.tensor_tensor(o2T[:, :, :].rearrange("p b (g j) -> p b g j", g=NGB),
                                    area1[:, :].rearrange("p (g j r) -> p r g j", g=NGB, j=HG)[:, 0:B, :, :],
                                    o_T[:, :].rearrange("p (b g j) -> p b g j", b=B, g=NGB), ALU.add).then_inc(o2_done, 1)

            dve.wait_ge(kcT_copied, 1)
            for b in range(B):
                nc.vector.tensor_tensor(kc_heads[:, b, :, :], kcT[:, b, :].unsqueeze(1).broadcast_to([P, H, S]),
                                        head_of[:, :].unsqueeze(2).broadcast_to([P, H, S]),
                                        ALU.mult).then_inc(kheads_done, 1)

            def c_shift(pair):
                bank = score_bank[pair % 3][:, :].rearrange("p (a s) -> p a s", s=S)
                m = c_max[pair % 2]
                dve.wait_ge(c_scored, pair + 1)
                nc.vector.tensor_reduce(m[:, :], bank, AX.X, ALU.max).then_inc(c_reduced, 1)
                dve.wait_ge(c_reduced, pair + 1)
                if pair >= 3:
                    dve.wait_ge(c_normed, pair - 2)
                nc.vector.tensor_tensor(c_exp[pair % 3].rearrange("p (a s) -> p a s", s=S), bank,
                                        m[:, :].unsqueeze(2).broadcast_to([P, 2 * H, S]),
                                        ALU.subtract).then_inc(c_shifted, 1)

            def c_sums(pair):
                dve.wait_ge(c_exped, pair + 1)
                if pair >= 2:
                    dve.wait_ge(c_normed, pair - 1)
                nc.vector.tensor_reduce(c_sum[pair % 2][:, :], c_exp[pair % 3].rearrange("p (a s) -> p a s", s=S),
                                        AX.X, ALU.add).then_inc(c_summing, 1)
                dve.wait_ge(c_summing, pair + 1)
                nc.vector.reciprocal(c_sum[pair % 2][:, :], c_sum[pair % 2][:, :]).then_inc(c_summed, 1)

            def c_result(pair):
                b, half = divmod(pair, 2)
                dve.wait_ge(c_mixed, pair + 1)
                dve.wait_ge(x_plus, b + 1)
                dve.wait_ge(out_sent[pair % 2], 16 * (pair // 2))
                nc.vector.tensor_tensor(y[:, pair % 2, :, :].rearrange("p t d -> p (t d)"),
                                        (area0, area1)[pair % 2][:, 0:2 * D],
                                        x[:, b, 2 * half:2 * half + 2, :].rearrange("p t d -> p (t d)"),
                                        ALU.add).then_inc(last_y_done, 1)

            c_shift(0)
            for pair in range(2 * B):
                if pair + 1 < 2 * B:
                    c_shift(pair + 1)
                c_sums(pair)
            for pair in range(POOL_PAIRS, 2 * B):
                c_result(pair)


INS = ["x", "ctx_1024", "L0_xattn_Wq", "L0_xattn_Wkv", "L0_xattn_Wout", "L0_xattn_bout", "L0_ffn_slot_query",
       "L0_ffn_d_Wq", "L0_ffn_d_Wk", "L0_ffn_d_Wv", "L0_ffn_d_Wo", "L0_ffn_d_bq", "L0_ffn_d_bk", "L0_ffn_d_bv",
       "L0_ffn_d_bo", "L0_ffn_c_Wq", "L0_ffn_c_Wk", "L0_ffn_c_Wv", "L0_ffn_c_Wo", "L0_ffn_c_bq", "L0_ffn_c_bk",
       "L0_ffn_c_bv", "L0_ffn_c_bo", "L0_ffn_e_ln_g", "L0_ffn_e_ln_b", "L0_ffn_e_W1", "L0_ffn_e_b1", "L0_ffn_e_Wg",
       "L0_ffn_e_bg", "L0_ffn_e_W2", "L0_ffn_e_b2"]


def kernel(**inputs):
    import numpy as np
    import concourse.bacc as bacc
    from concourse.bass_utils import run_bass_kernel_spmd

    nc = bacc.Bacc("TRN2", target_bir_lowering=False, num_devices=1)
    arrays, args = {}, {}
    for name in INS:
        a = np.ascontiguousarray(inputs[name])
        arrays[f"in_{name}"] = a
        args[name] = nc.dram_tensor(f"in_{name}", a.shape, mybir.dt.from_np(a.dtype), kind="ExternalInput").ap()
    out = nc.dram_tensor("out", (B, T, D), F32, kind="ExternalOutput").ap()
    program(nc, args, out)
    r = run_bass_kernel_spmd(nc, [arrays], core_ids=[0])
    return r.results[0]["out"]
```

```python
from contextlib import ExitStack

import concourse.bass as bass
from concourse import mybir

F32 = mybir.dt.float32
BF16 = mybir.dt.bfloat16
ALU = mybir.AluOpType
ACT = mybir.ActivationFunctionType
AX = mybir.AxisListType

P = 128
B = 4
T = 512
NT = T // P
D = 128
H = 16
DH = D // H
MEM = 32
KEYS = MEM + T
S = 16
F = 512
FC = F // P
EPS = 1e-5
SCALE = DH ** -0.5
BIG = -1.0e30

HG = 4
NGB = H // HG
NGROUPS = B * NGB
LEAD = 2
TICKS = 14
UNITS = 12
Q_TERMS = [0, 0, 1, 1, 2, 0]
K_TERMS = [0, 1, 0, 1, 0, 2]
SHIFT_ROW = 2 * DH * len(Q_TERMS)
SLOTS = NGROUPS + 2

A_STATS, A_RSTD, A_NORM, A_T, A_Q, A_K, A_V, A_VLAST = 0, 2, 4, 8, 10, 14, 28, 30
A_END = A_VLAST + 3
SLOT_QUERY_USES = {(1, 6): "slotT", (1, 9): "slotq", (4, 7): "wkT", (4, 10): "fold"}
MAX_TICK, SHIFT_TICK = 1, 4
PROBS_TICK = TICKS - UNITS
DIAGONAL_TICKS = (6, 10, 13)
PV_TICKS = (3, 6, 10, 12, 13)
P_TOK, P_ATT, P_OUT, P_STATS, P_RSTD, P_NORM, P_T = (2, 5, 8, 11), 14, 17, 18, 20, 22, 26
P_SD, P_VD, P_QC, P_PT, P_PV, P_SUM = (29, 33), 37, 39, (41, 44), (46, 49), 52
P_END = P_SUM + 2
READ = 1
KEY_TILES = [(P * j, max(0, P * j - MEM)) for j in range(NT)] + [(KEYS - P, T - MEM)]
KT = len(KEY_TILES)
COLS = [T - q for _, q in KEY_TILES]
AT = [0, 0, 0, COLS[2], COLS[2] + COLS[3]]
SCORE_UNITS = [(3, (0,)), (0, (0, 1)), (2, (0,)), (1, (0,)), (3, (1,)), (1, (1,)), (2, (1,)),
               (3, (2,)), (1, (2,)), (0, (2, 3)), (2, (2,)), (3, (3,)), (1, (3,)), (2, (3,))]


def projection_step(slot, tick):
    slot, tick = slot + tick // TICKS, tick % TICKS
    b, step = (slot + 1) // NGB + 1, (slot + 1) % NGB * TICKS + tick
    if slot < -1 or b >= B or (b == 1 and step < A_K):
        return None, -1
    return b, step


def finish_step(slot, tick):
    slot, tick = slot + tick // TICKS, tick % TICKS
    at = slot - NGB - 1
    return (at // NGB, at % NGB * TICKS + tick) if at >= 0 and at // NGB < B - 1 else (None, -1)


PROJ_USES = {A_T: "xnT", A_Q: "q", A_K: "k", A_V: "v", A_VLAST: "vlast"}


def count_uses():
    first = ["ctxT", "kmem"] + [(0, n) for n in PROJ_USES.values()] + [(1, "xnT"), (1, "q")]
    second = []
    for slot in range(-LEAD, SLOTS):
        for tick in range(TICKS):
            if tick == SHIFT_TICK and -LEAD <= slot - 1 and slot - 1 + LEAD < NGROUPS:
                first.append(("shift", slot - 1 + LEAD))
            if (slot, tick) in SLOT_QUERY_USES:
                first.append(SLOT_QUERY_USES[slot, tick])
            b, n = projection_step(slot, tick)
            if n in PROJ_USES:
                first.append((b, PROJ_USES[n]))
            b, n = finish_step(slot, tick)
            second += finish_uses(b, n)
    for n in range(P_END):
        second += finish_uses(B - 1, n)
    return {n: i for i, n in enumerate(first)}, {n: i for i, n in enumerate(second)}


def finish_uses(b, n):
    for at, what in ((P_TOK, "tok"), (P_PT, "pT"), (P_PV, "pv"), (P_SD, "sd")):
        if n in at:
            return [(b, what, at.index(n))]
    one = {P_ATT: "att", P_OUT: "out", P_T: "xn2T", P_QC: "qc", P_VD: "vd", P_SUM: "sum"}
    return [(b, one[n])] if n in one else []


AREA0, AREA1 = count_uses()
CAUSAL_MADE = 6
CONSTS_MADE = CAUSAL_MADE + 7 + P // S
FILL = {P_ATT: 5, P_OUT: 2, P_STATS: 3, P_T: 16}
POOL_PAIRS = 2 * B - 2


def program(nc, i, out):
    with ExitStack() as ctx:
        def sb(name, shape, dt=F32):
            return ctx.enter_context(nc.sbuf_tensor(name, shape, dt))

        def ps(name, shape, dt=F32):
            return ctx.enter_context(nc.psum_tensor(name, shape, dt))

        def sem(name):
            return ctx.enter_context(nc.semaphore(name))

        score_bank = [ps(f"score_bank{n}", [P, 512]) for n in range(3)]
        scoreT_bank = [ps(f"scoreT_bank{n}", [P, 512]) for n in range(2)]
        pv_bank = ps("pv_bank", [P, 512])
        area0 = ps("area0", [P, 512])
        area1 = ps("area1", [P, 512])

        x = sb("x", [P, B, NT, D])
        xn = sb("xn", [P, NT, D])
        xnT = sb("xnT", [P, KEYS])
        ctx_in = sb("ctx_in", [P, D])
        ctxT = sb("ctxT", [P, B, MEM])
        wq_cols = sb("wq_cols", [P, D])
        wk_cols = sb("wk_cols", [P, D])
        wq = sb("wq", [P, D])
        wkv = sb("wkv", [P, 2 * D])
        wout = sb("wout", [P, D])
        dw = {n: sb(f"dw_{n}", [P, D]) for n in "qkvo"}
        cw = {n: sb(f"cw_{n}", [P, D]) for n in "qkvo"}
        db = {n: sb(f"db_{n}", [P, 1]) for n in "qkv"}
        cb = {n: sb(f"cb_{n}", [P, 1]) for n in "qkv"}
        bout_row = sb("bout_row", [P, D])
        cbo_row = sb("cbo_row", [P, D])
        dbo_row = sb("dbo_row", [B * S, D])
        slot_rows = sb("slot_rows", [B * S, D])
        slots = sb("slots", [S, D])
        ln_g = sb("ln_g", [B * S, D])
        ln_b = sb("ln_b", [B * S, D])
        b2_rows = sb("b2_rows", [B * S, D])

        ident = sb("ident", [P, P])
        identb = sb("identb", [P, P], BF16)
        causal = sb("causal", [P, P], BF16)
        head_of = sb("head_of", [P, H])
        slot_head = sb("slot_head", [P, 2, H])
        slot_sel = sb("slot_sel", [P, S])
        zero_rows = sb("zero_rows", [4 * H // 2, T], BF16)
        one_rows = sb("one_rows", [S, KEYS], BF16)
        slotsT = sb("slotsT", [P, S])

        stats = sb("stats", [P, NT, 6])
        mv = sb("mv", [P, NT, 2])
        rstd = sb("rstd", [P, NT])
        vare = sb("vare", [P, NT])
        mhalf = sb("mhalf", [P, NT])
        stats2 = sb("stats2", [P, NT, 6])
        mv2 = sb("mv2", [P, NT, 2])
        rstd2 = sb("rstd2", [P, NT])
        vare2 = sb("vare2", [P, NT])

        qp = sb("qp", [P, 3, T], BF16)
        kp = sb("kp", [P, 3, KEYS], BF16)
        kmem = sb("kmem", [P, 3, B * MEM], BF16)
        res = sb("res", [P, T])
        resk = sb("resk", [P, T])
        q_stack = [sb(f"q_stack{n}", [P, H // 2, T], BF16) for n in range(2)]
        k_stack = [sb(f"k_stack{n}", [P, H, KEYS], BF16) for n in range(2)]
        v_aug = [sb(f"v_aug{n}", [P, KT, H, DH + 1]) for n in range(2)]
        rowmax = [sb(f"rowmax{n}", [P, NT, 2, 2]) for n in range(2)]
        tailmax = [sb(f"tailmax{n}", [P, 2, 2]) for n in range(2)]
        shift = [sb(f"shift{n}", [P, NT, 2, 2, 2], BF16) for n in range(2)]
        shiftT = [sb(f"shiftT{n}", [8, T], BF16) for n in range(2)]
        probs = [sb(f"probs{n}", [P, UNITS, 512]) for n in range(2)]
        oT = sb("oT", [P, NGB, T])
        rden = sb("rden", [P, NT, H])
        att = sb("att", [P, NT, D])
        attT = sb("attT", [P, T])
        xn2 = att
        xn2T = attT
        qcT = sb("qcT", [P, B, T])
        kdT = sb("kdT", [P, T])
        wkT = kdT[:, 0:D]
        vd = sb("vd", [P, NT, D])
        qd_heads = sb("qd_heads", [P, H, S])
        qdT = sb("qdT", [P, S])
        qd_fold = sb("qd_fold", [P, 2 * P])
        key_bias = sb("key_bias", [P, 2])
        sd_max = sb("sd_max", [P, 2])
        sd_sum = sb("sd_sum", [P, 2])
        sd_r = sb("sd_r", [P, 2])
        pd = sb("pd", [P, 2, T])
        pdT = sb("pdT", [P, 2, T])
        od = sb("od", [P, 2, D])
        adT = sb("adT", [P, B, S])
        w1_early = sb("w1_early", [P, 12, F])
        k0 = k_stack[0][:, :, :].rearrange("p h n -> p (h n)").bitcast(F32)
        k1 = k_stack[1][:, :, :].rearrange("p h n -> p (h n)").bitcast(F32)
        q0 = q_stack[0][:, :, :].rearrange("p h n -> p (h n)").bitcast(F32)
        q1 = q_stack[1][:, :, :].rearrange("p h n -> p (h n)").bitcast(F32)
        late1 = k1[:, 0:4 * F].rearrange("p (e f) -> p e f", f=F)
        lateg = k1[:, 4 * F:8 * F].rearrange("p (e f) -> p e f", f=F)
        midg0 = k0[:, 0:8 * F].rearrange("p (e f) -> p e f", f=F)
        midg1 = q0[:, 0:4 * F].rearrange("p (e f) -> p e f", f=F)
        w1 = [w1_early[:, e, :] if e < 12 else late1[:, e - 12, :] for e in range(S)]
        wg = [midg0[:, e, :] if e < 8 else midg1[:, e - 8, :] if e < 12 else lateg[:, e - 12, :] for e in range(S)]
        w2 = [probs[e // 8][:, e % 8, :].rearrange("p (c d) -> p c d", d=D) for e in range(S)]
        b1_rows = oT[:, :, :]
        bg_rows = q1.rearrange("p (g n) -> p g n", g=NGB)
        hT = probs[0][:, 8, :].rearrange("p (e c) -> p e c", c=32)
        uvT = [probs[0][:, 9, :], probs[0][:, 10, :]]
        ub = [probs[1][:, 8, :], probs[1][:, 9, :]]
        gb = [probs[1][:, 10, :], res[:, :]]
        uv = [resk[:, :], qp[:, 0:2, :].rearrange("p a n -> p (a n)").bitcast(F32)]
        ysb = xn[:, :, :].rearrange("p t d -> p (t d)")
        kc_heads = pd[:, :, :].rearrange("p c n -> p (c n)").rearrange("p (b h s) -> p b h s", b=B, h=H)
        vc_heads = pdT[:, :, :].rearrange("p c n -> p (c n)").rearrange("p (b h s) -> p b h s", b=B, h=H)
        vo = k0[:, 0:1024].rearrange("p (b c d) -> p b c d", b=B, c=2)
        table_probe = sb("table_probe", [P, 1])
        o_rows = sb("o_rows", [B * S, D])
        o_T = sb("o_T", [P, B * S])
        o_stats = sb("o_stats", [B * S, 6])
        o_mv = sb("o_mv", [B * S, 2])
        h_rows = sb("h_rows", [B * S, D])
        o2T = sb("o2T", [P, B, S])
        kcT = sb("kcT", [P, B, S])
        vcT = sb("vcT", [P, B, S])
        c_max = [sb(f"c_max{n}", [P, 2 * H]) for n in range(2)]
        c_sum = [sb(f"c_sum{n}", [P, 2 * H]) for n in range(2)]
        oT_flat = oT[:, :, :]
        c_exp = [oT_flat[:, 0, :], oT_flat[:, 1, :], k0[:, 1024:1536]]
        c_prob = [oT_flat[:, 2, :], oT_flat[:, 3, :]]
        c_probT = [xnT[:, 0:T], kdT[:, :]]
        y = vd[:, :, :].rearrange("p (a t) d -> p a t d", a=2)

        x_in0 = sem("x_in0")
        x_in1 = sem("x_in1")
        attn_w_in = sem("attn_w_in")
        ctx_in_sem = sem("ctx_in_sem")
        slot_w_in = sem("slot_w_in")
        late_w_in = sem("late_w_in")
        bout_in = sem("bout_in")
        rows_in = sem("rows_in")
        w1_in = sem("w1_in")
        wg_in = sem("wg_in")
        w2_in = sem("w2_in")
        b1_in = sem("b1_in")
        consts = sem("consts")
        pool_const = sem("pool_const")
        fold_copied = sem("fold_copied")
        ctx_placed = sem("ctx_placed")
        pv_cleared = sem("pv_cleared")
        stats_done = sem("stats_done")
        rstd_done = sem("rstd_done")
        vare_done = sem("vare_done")
        norm_done = sem("norm_done")
        area0_filled = sem("area0_filled")
        area0_drained = sem("area0_drained")
        area1_filled = sem("area1_filled")
        q_first = sem("q_first")
        k_first = sem("k_first")
        res_done = sem("res_done")
        q_second = sem("q_second")
        q_third = sem("q_third")
        mem_copied = sem("mem_copied")
        kmem_part = sem("kmem_part")
        scores_ready = sem("scores_ready")
        scores_reduced = sem("scores_reduced")
        max_chain = sem("max_chain")
        scoreT_ready = sem("scoreT_ready")
        exp_done = sem("exp_done")
        diag_done = sem("diag_done")
        pv_done = sem("pv_done")
        oT_copied = sem("oT_copied")
        slotq_done = sem("slotq_done")
        x_plus = sem("x_plus")
        stats2_done = sem("stats2_done")
        rstd2_done = sem("rstd2_done")
        vare2_done = sem("vare2_done")
        norm2_done = sem("norm2_done")
        rden_done = sem("rden_done")
        sd_chain = sem("sd_chain")
        sd_exp = sem("sd_exp")
        od_done = sem("od_done")
        o_chain = sem("o_chain")
        o_pool = sem("o_pool")
        hT_copied = sem("hT_copied")
        hT_zeroed = sem("hT_zeroed")
        oh_ready = sem("oh_ready")
        kzero_done = sem("kzero_done")
        x_b = sem("x_b")
        tile_stats = sem("tile_stats")
        tile_stats2 = sem("tile_stats2")
        v_zero = sem("v_zero")
        q_zeroed = sem("q_zeroed")
        sd_recip = sem("sd_recip")
        att_done = sem("att_done")
        attT_done = sem("attT_done")
        x_added = sem("x_added")
        xn2T_done = sem("xn2T_done")
        qc_done = sem("qc_done")
        vd_done = sem("vd_done")
        pdT_done = sem("pdT_done")
        ad_done = sem("ad_done")
        c_summing = sem("c_summing")
        cols_done = sem("cols_done")
        up_ready = sem("up_ready")
        silu_in = sem("silu_in")
        silu_done = sem("silu_done")
        uv_done = sem("uv_done")
        uvT_ready = sem("uvT_ready")
        uvT_copied = sem("uvT_copied")
        y_ready = sem("y_ready")
        y_copied = sem("y_copied")
        yT_ready = sem("yT_ready")
        o2_done = sem("o2_done")
        kcT_ready = sem("kcT_ready")
        kcT_copied = sem("kcT_copied")
        kheads_done = sem("kheads_done")
        vheads_done = sem("vheads_done")
        vo_ready = sem("vo_ready")
        vo_copied = sem("vo_copied")
        c_scored = sem("c_scored")
        c_reduced = sem("c_reduced")
        c_shifted = sem("c_shifted")
        c_exped = sem("c_exped")
        c_summed = sem("c_summed")
        c_normed = sem("c_normed")
        c_transposed = sem("c_transposed")
        c_copied = sem("c_copied")
        c_mixed = sem("c_mixed")
        mix_copied = sem("mix_copied")
        last_y_done = sem("last_y_done")
        y_done = sem("y_done")
        out_sent = [sem(f"out_sent{n}") for n in range(2)]
        stack_init = sem("stack_init")
        q_stacked = [sem(f"q_stacked{b}") for b in range(B)]
        k_stacked = [sem(f"k_stacked{b}") for b in range(B)]
        shift_in = [sem(f"shift_in{n}") for n in range(2)]

        NQ_DMA = [16 * (len(Q_TERMS) + (b >= 2)) for b in range(B)]
        ROWS_DMA = 16 * 6
        LATE_DMA = 16 * 12
        NK_DMA = 16 * (2 * len(K_TERMS))

        def unit_of_scores(group, k):
            return SCORE_UNITS[k]

        def scores_cols(tile):
            return min(MEM + P * (tile + 1), 512)

        def projection_bank(b, name):
            first = {"xnT": scoreT_bank[0], "k": score_bank[0], "v": score_bank[1], "vlast": score_bank[2]}
            return first.get(name, area0) if b == 0 else area0

        finish_banks = [area1, *score_bank, *scoreT_bank]
        bank_of, previous, last_in = {}, {}, {}
        for name, n in AREA1.items():
            k = 0
            if name[0] == B - 1:
                k = (n - AREA1[(B - 1, "tok", 0)]) % len(finish_banks)
            elif name[0] == B - 2 and n > AREA1[(B - 2, "xn2T")]:
                k = (n - AREA1[(B - 2, "xn2T")]) % 4
            bank_of[name], previous[name] = finish_banks[k], last_in.get(k)
            last_in[k] = name

        def read(name):
            b, what = name[0], name[1]
            if what == "tok":
                return att_done, NT * b + name[2] + 1
            if what in ("sd", "pT", "pv"):
                return {"sd": sd_exp, "pT": pdT_done, "pv": od_done}[what], 2 * b + name[2] + 1
            return {"att": attT_done, "out": x_added, "xn2T": xn2T_done, "qc": qc_done,
                    "vd": vd_done, "sum": ad_done}[what], b + 1

        c_banks = [*score_bank, pv_bank]

        block = ctx.enter_context(nc.Block())

        @block.sync
        def _(sp):
            sp.dma_start(x[:, 0, :, :], i["x"][0].rearrange("(t p) d -> p t d", p=P)).then_inc(x_in0, 16)
            sp.dma_start(ctx_in[:, :], i["ctx_1024"].rearrange("b m d -> (b m) d")).then_inc(ctx_in_sem, 16)
            sp.dma_start(wq[:, :], i["L0_xattn_Wq"]).then_inc(attn_w_in, 16)
            sp.dma_start(wkv[:, :], i["L0_xattn_Wkv"]).then_inc(attn_w_in, 16)

            def stack_q(b, part):
                if part == 0:
                    sp.wait_ge(q_first, b + 1)
                else:
                    sp.wait_ge((q_second, q_third)[part - 1], 2 * b + 1)
                for t in range(len(Q_TERMS)):
                    if Q_TERMS[t] == part:
                        sp.dma_start(q_stack[b % 2][2 * DH * t:2 * DH * (t + 1), :, :],
                                     qp[:, part, :]).then_inc(q_stacked[b], 16)

            def stack_k(b, part):
                for t in range(len(K_TERMS)):
                    if K_TERMS[t] == part:
                        for g in range(2):
                            row = 2 * DH * t + DH * g
                            sp.dma_start(k_stack[b % 2][row:row + DH, g::2, :],
                                         kp[64 * g:64 * (g + 1), part, :]).then_inc(k_stacked[b], 16)

            def stack_sequence(b):
                if b < 2:
                    sp.wait_ge(kzero_done, 2 * (b + 1))
                    sp.wait_ge(consts, 1)
                    for g in range(2):
                        sp.dma_start(k_stack[b][SHIFT_ROW + 2 * g:SHIFT_ROW + 2 * g + 2, g::2, :],
                                     one_rows[:, :]).then_inc(stack_init, 16)
                else:
                    sp.wait_ge(scoreT_ready, UNITS * NGB * (b - 1))
                    sp.wait_ge(consts, 4)
                    sp.dma_start(q_stack[b % 2][SHIFT_ROW:SHIFT_ROW + 4, :, :], zero_rows[:, :]).then_inc(q_stacked[b], 16)
                for part in range(3):
                    if b != 1:
                        stack_q(b, part)
                    if part == 0:
                        sp.wait_ge(mem_copied, b + 1)
                        sp.wait_ge(k_first, b + 1)
                    else:
                        sp.wait_ge((q_second, q_third)[part - 1], 2 * b + 2)
                    stack_k(b, part)

            def shift_rows(group):
                sp.wait_ge(area0_drained, AREA0[("shift", group)] + 1)
                b, gl = divmod(group, NGB)
                sp.dma_start(q_stack[b % 2][SHIFT_ROW:SHIFT_ROW + 4, 2 * gl:2 * gl + 2, :],
                             shiftT[group % 2][:, :]).then_inc(shift_in[group % 2], 16)

            for b in range(1, B):
                sp.dma_start(x[:, b, :, :], i["x"][b].rearrange("(t p) d -> p t d", p=P)).then_inc(x_in1, 16)
            stack_sequence(0)
            for slot in range(-LEAD, NGROUPS):
                if slot == -1:
                    sp.dma_start(bout_row[:, :], i["L0_xattn_bout"].partition_broadcast(P)).then_inc(bout_in, 16)
                    sp.dma_start(slots[:, :], i["L0_ffn_slot_query"][0]).then_inc(slot_w_in, 16)
                    sp.dma_start(wout[:, :], i["L0_xattn_Wout"]).then_inc(slot_w_in, 16)
                    sp.dma_start(dw["q"][:, :], i["L0_ffn_d_Wq"]).then_inc(slot_w_in, 16)
                    sp.dma_start(db["q"][:, :], i["L0_ffn_d_bq"].rearrange("(d o) -> d o", o=1)).then_inc(slot_w_in, 16)
                if slot > -LEAD and slot - 1 + LEAD < NGROUPS:
                    shift_rows(slot - 1 + LEAD)
                if slot == -1:
                    for part in range(3):
                        stack_q(1, part)
                if slot % NGB == 0 and slot // NGB + 1 < B:
                    stack_sequence(slot // NGB + 1)
                if slot == 2:
                    for n in "qkvo":
                        if n != "q":
                            sp.dma_start(dw[n][:, :], i[f"L0_ffn_d_W{n}"]).then_inc(late_w_in, 16)
                        sp.dma_start(cw[n][:, :], i[f"L0_ffn_c_W{n}"]).then_inc(late_w_in, 16)
                    for n in "qkv":
                        if n != "q":
                            sp.dma_start(db[n][:, :],
                                         i[f"L0_ffn_d_b{n}"].rearrange("(d o) -> d o", o=1)).then_inc(late_w_in, 16)
                        sp.dma_start(cb[n][:, :], i[f"L0_ffn_c_b{n}"].rearrange("(d o) -> d o", o=1)).then_inc(late_w_in, 16)
                if slot == 3:
                    sp.dma_start(cbo_row[:, :], i["L0_ffn_c_bo"].partition_broadcast(P)).then_inc(rows_in, 16)
                    sp.dma_start(dbo_row[:, :], i["L0_ffn_d_bo"].partition_broadcast(B * S)).then_inc(rows_in, 16)
                    for dst, src in ((slot_rows, i["L0_ffn_slot_query"][0]), (ln_g, i["L0_ffn_e_ln_g"]),
                                     (ln_b, i["L0_ffn_e_ln_b"]), (b2_rows, i["L0_ffn_e_b2"])):
                        sp.dma_start(dst[:, :], src.partition_broadcast(B)).then_inc(rows_in, 16)
                if 4 <= slot < 12:
                    for e in (range(2) if slot < 8 else range(1)):
                        e += 2 * (slot - 4) if slot < 8 else slot
                        sp.dma_start(w1[e], i["L0_ffn_e_W1"][e]).then_inc(w1_in, 16)
                elif slot >= 12:
                    if slot == 12:
                        sp.wait_ge(scoreT_ready, UNITS * 12)
                    for e in range(3 * (slot - 12), 3 * (slot - 12) + 3):
                        sp.dma_start(wg[e], i["L0_ffn_e_Wg"][e]).then_inc(wg_in, 16)
            sp.wait_ge(scoreT_ready, UNITS * NGROUPS)
            for e in range(12, S):
                sp.dma_start(w1[e], i["L0_ffn_e_W1"][e]).then_inc(w1_in, 16)
                sp.dma_start(wg[e], i["L0_ffn_e_Wg"][e]).then_inc(wg_in, 16)
            for dst, name in ((bg_rows, "L0_ffn_e_bg"), (b1_rows, "L0_ffn_e_b1")):
                if name == "L0_ffn_e_b1":
                    sp.wait_ge(pv_done, NGROUPS)
                    for e in range(S):
                        sp.dma_start(w2[e], i["L0_ffn_e_W2"][e].rearrange("(p c) d -> p c d", c=FC)).then_inc(w2_in, 16)
                    sp.wait_ge(area1_filled, AREA1[(B - 1, "tok", NT - 1)] + 1)
                for jj in range(HG):
                    src = i[name].rearrange("(g j) f -> j g f", j=HG)[jj].partition_broadcast(32)
                    sp.dma_start(dst[32 * jj:32 * jj + 32, :, :], src).then_inc(b1_in, 16)
            for pair in range(2 * B):
                if pair < POOL_PAIRS:
                    sp.wait_ge(y_done, pair + 1)
                else:
                    sp.wait_ge(last_y_done, pair - POOL_PAIRS + 1)
                b, half = divmod(pair, 2)
                dst = out[b].rearrange("(h t p) d -> h p t d", h=2, p=P)[half]
                sp.dma_start(dst, y[:, pair % 2, :, :]).then_inc(out_sent[pair % 2], 16)
            for n in range(2):
                sp.wait_ge(out_sent[n], 16 * B)

        @block.gpsimd
        def _(pool):
            made = [0]

            def const(ins):
                made[0] += 1
                ins.then_inc(pool_const, 1)
                pool.wait_ge(pool_const, made[0])

            const(nc.gpsimd.memset(mhalf[:, :], -0.5))
            const(nc.gpsimd.memset(ident[:, :], 0.0))
            const(nc.gpsimd.affine_select(out=ident[:, :], in_=ident[:, :], compare_op=ALU.not_equal, fill=1.0,
                                          base=0, pattern=[[-1, P]], channel_multiplier=1))

            def rstd_of(n, done_stats, v, mvs, r, s_v, s_r):
                pool.wait_ge(done_stats, n + 1)
                nc.gpsimd.tensor_scalar(v, mvs, EPS, None, ALU.add).then_inc(s_v, 1)
                pool.wait_ge(s_v, n + 1)
                nc.gpsimd.tensor_tensor(r, v, mhalf[:, :], ALU.pow).then_inc(s_r, 1)

            def third_part(n, second, third, left):
                pool.wait_ge(q_second, n + 1)
                nc.gpsimd.tensor_tensor(third, left, second, ALU.subtract).then_inc(q_third, 1)

            def cut_q(b):
                if b:
                    pool.wait_ge(q_stacked[b - 1], NQ_DMA[b - 1])
                third_part(2 * b, qp[:, 1, :], qp[:, 2, :], res[:, :])

            def cut_k(b):
                if b:
                    copy_memory(b)
                third_part(2 * b + 1, kp[:, 1, MEM:], kp[:, 2, MEM:], resk[:, :])

            def copy_memory(b):
                pool.wait_ge(kmem_part, 4)
                if b:
                    pool.wait_ge(k_stacked[b - 1], NK_DMA)
                nc.gpsimd.tensor_copy(kp[:, :, 0:MEM], kmem[:, :, MEM * b:MEM * (b + 1)]).then_inc(mem_copied, 1)

            def diagonal(group, n):
                pr = probs[group % 2]
                pool.wait_ge(exp_done, UNITS * group + HG * (n + 1))
                for j in ((0,), (1,), (2, 3, 4))[n]:
                    first_key, first_query = KEY_TILES[j]
                    ahead = first_query - (first_key - MEM)
                    v = pr[:, HG * n:HG * (n + 1), AT[j]:AT[j] + P - ahead]
                    ins = nc.gpsimd.affine_select(out=v, in_=v, compare_op=ALU.is_ge, fill=0.0, base=ahead,
                                                  pattern=[[0, HG], [1, P - ahead]], channel_multiplier=-1)
                ins.then_inc(diag_done, 1)

            def add_row(n, b, row, normalised):
                pool.wait_ge(normalised, b + 1)
                xb = x[:, b, :, :]
                nc.gpsimd.tensor_tensor(xb, xb, row[:, :].unsqueeze(1).broadcast_to([P, NT, D]),
                                        ALU.add).then_inc(n, 1)

            zeros = k0.bitcast(mybir.dt.uint32)
            nc.gpsimd.memset(zeros[:, zeros.shape[1] // 2:], 0).then_inc(kzero_done, 1)
            rstd_of(0, stats_done, vare[:, :], mv[:, :, 1], rstd[:, :], vare_done, rstd_done)
            const(nc.gpsimd.tensor_copy(identb[:, :], ident[:, :]))
            const(nc.gpsimd.memset(causal[:, :], 0.0))
            const(nc.gpsimd.affine_select(out=causal[:, :], in_=causal[:, :], compare_op=ALU.is_ge, fill=BIG,
                                          base=0, pattern=[[-1, P]], channel_multiplier=1))
            assert made[0] == CAUSAL_MADE
            copy_memory(0)
            nc.gpsimd.memset(k1.bitcast(mybir.dt.uint32), 0).then_inc(kzero_done, 2)
            cut_q(0)
            cut_k(0)
            rstd_of(1, stats_done, vare[:, :], mv[:, :, 1], rstd[:, :], vare_done, rstd_done)
            const(nc.gpsimd.memset(head_of[:, :], 1.0))
            const(nc.gpsimd.affine_select(out=head_of[:, :], in_=head_of[:, :], compare_op=ALU.is_ge, fill=0.0,
                                          base=0, pattern=[[-DH, H]], channel_multiplier=1))
            const(nc.gpsimd.affine_select(out=head_of[:, :], in_=head_of[:, :], compare_op=ALU.is_ge, fill=0.0,
                                          base=DH - 1, pattern=[[DH, H]], channel_multiplier=-1))
            const(nc.gpsimd.memset(slot_head[:, :, :], 1.0))
            const(nc.gpsimd.affine_select(out=slot_head[:, :, :], in_=slot_head[:, :, :], compare_op=ALU.is_ge,
                                          fill=0.0, base=0, pattern=[[P, 2], [-S, H]], channel_multiplier=1))
            const(nc.gpsimd.affine_select(out=slot_head[:, :, :], in_=slot_head[:, :, :], compare_op=ALU.is_ge,
                                          fill=0.0, base=S - 1, pattern=[[-P, 2], [S, H]], channel_multiplier=-1))
            const(nc.gpsimd.memset(slot_sel[:, :], 0.0))
            for r in range(P // S):
                const(nc.gpsimd.affine_select(out=slot_sel[:, :], in_=slot_sel[:, :], compare_op=ALU.not_equal,
                                              fill=1.0, base=-S * r, pattern=[[-1, S]], channel_multiplier=1))
            assert made[0] == CONSTS_MADE

            cut_q(1)

            def slot_queries():
                pool.wait_ge(area0_drained, AREA0["slotq"] + 1)
                nc.gpsimd.tensor_tensor(qd_heads[:, :, :], qdT[:, :].unsqueeze(1).broadcast_to([P, H, S]),
                                    head_of[:, :].unsqueeze(2).broadcast_to([P, H, S]), ALU.mult).then_inc(slotq_done, 1)

            for slot in range(-LEAD, SLOTS):
                for tick in range(TICKS):
                    if (slot, tick) == (-1, 0):
                        pool.wait_ge(bout_in, 16)
                        add_row(x_b, 0, bout_row, norm_done)
                    if SLOT_QUERY_USES.get((slot, tick - 2)) == "slotq":
                        slot_queries()
                    if (slot, tick) == (NGB, 0):
                        pool.wait_ge(rows_in, ROWS_DMA)
                        nc.gpsimd.tensor_tensor(slot_rows[:, :], slot_rows[:, :], dbo_row[:, :],
                                                ALU.add).then_inc(o_pool, 1)
                    b, n = projection_step(slot, tick)
                    if n == A_RSTD:
                        rstd_of(b, stats_done, vare[:, :], mv[:, :, 1], rstd[:, :], vare_done, rstd_done)
                    if n == A_Q + 3:
                        cut_q(b)
                    if n == A_K + 3:
                        cut_k(b)
                    if n == A_K + 6:
                        add_row(x_b, b, bout_row, norm_done)
                    b, n = finish_step(slot, tick)
                    if n == P_RSTD:
                        rstd_of(b, stats2_done, vare2[:, :], mv2[:, :, 1], rstd2[:, :], vare2_done, rstd2_done)
                    if n == P_QC:
                        add_row(x_plus, b, cbo_row, norm2_done)
                    if 0 <= slot < NGROUPS and tick in DIAGONAL_TICKS:
                        diagonal(slot, DIAGONAL_TICKS.index(tick))
            rstd_of(B - 1, stats2_done, vare2[:, :], mv2[:, :, 1], rstd2[:, :], vare2_done, rstd2_done)
            add_row(x_plus, B - 1, cbo_row, norm2_done)
            pool.wait_ge(o_chain, 3)
            nc.gpsimd.tensor_scalar(vare[0:B * S, 0:1], o_mv[:, 1:2], EPS, None, ALU.add).then_inc(o_pool, 1)
            pool.wait_ge(o_pool, 2)
            nc.gpsimd.tensor_tensor(rstd[0:B * S, 0:1], vare[0:B * S, 0:1], mhalf[0:B * S, 0:1],
                                    ALU.pow).then_inc(o_pool, 1)
            pool.wait_ge(kcT_copied, 2)
            for b in range(B):
                nc.gpsimd.tensor_tensor(vc_heads[:, b, :, :], vcT[:, b, :].unsqueeze(1).broadcast_to([P, H, S]),
                                        head_of[:, :].unsqueeze(2).broadcast_to([P, H, S]),
                                        ALU.mult).then_inc(vheads_done, 1)
            def add_residual(pair):
                b, half = divmod(pair, 2)
                pool.wait_ge(mix_copied, pair + 1)
                yp = y[:, pair % 2, :, :]
                nc.gpsimd.tensor_tensor(yp, yp, x[:, b, 2 * half:2 * half + 2, :], ALU.add).then_inc(y_done, 1)

            for pair in range(2 * B):
                pool.wait_ge(c_summed, pair + 1)
                if pair >= 2:
                    pool.wait_ge(c_transposed, pair - 1)
                nc.gpsimd.tensor_tensor(c_prob[pair % 2].rearrange("p (a s) -> p a s", s=S),
                                        c_exp[pair % 3].rearrange("p (a s) -> p a s", s=S),
                                        c_sum[pair % 2][:, :].unsqueeze(2).broadcast_to([P, 2 * H, S]),
                                        ALU.mult).then_inc(c_normed, 1)
                if 0 <= pair - 3 < POOL_PAIRS:
                    add_residual(pair - 3)
            for pair in range(2 * B - 3, POOL_PAIRS):
                add_residual(pair)

        @block.scalar
        def _(act):
            act.wait_ge(attn_w_in, 32)
            for dst, src in ((wq_cols, wq[:, :]), (wk_cols, wkv[:, 0:D])):
                src = src.rearrange("k (s g d) -> k g d s", s=H // 2, g=2)
                for g in range(2):
                    nc.scalar.activation(dst[:, 64 * g:64 * (g + 1)].rearrange("k (d s) -> k d s", d=DH),
                                         src[:, g, :, :], ACT.Copy).then_inc(cols_done, 1)
            act.wait_ge(area0_filled, AREA0["ctxT"] + 1)
            nc.scalar.activation(ctxT[:, :, :].rearrange("p b m -> p (b m)"), area0[:, 0:P],
                                 ACT.Copy).then_inc(area0_drained, 1)
            act.wait_ge(area0_filled, AREA0["kmem"] + 1)
            nc.scalar.activation(kmem[:, 0, :], area0[:, 0:P], ACT.Copy).then_inc(kmem_part, 1)

            def slot_queries(name):
                act.wait_ge(area0_filled, AREA0[name] + 1)
                if name == "slotT":
                    nc.scalar.activation(slotsT[:, :], area0[:, 0:S], ACT.Copy).then_inc(area0_drained, 1)
                elif name == "slotq":
                    nc.scalar.activation(qdT[:, :], area0[:, 0:S], ACT.Identity,
                                         bias=db["q"][:, 0:1]).then_inc(area0_drained, 1)
                elif name == "wkT":
                    nc.scalar.activation(wkT, area0[:, 0:D], ACT.Copy).then_inc(area0_drained, 1)
                else:
                    nc.scalar.activation(key_bias[:, :], area0[:, 2 * P:2 * P + 2], ACT.Copy).then_inc(fold_copied, 1)
                    nc.scalar.activation(qd_fold[:, :], area0[:, 0:2 * P], ACT.Copy).then_inc(area0_drained, 1)

            def project(b, step):
                if step == A_T + READ:
                    act.wait_ge(area0_filled, AREA0[(b, "xnT")] + 1)
                    nc.scalar.activation(xnT[:, 0:MEM], ctxT[:, b, :], ACT.Copy).then_inc(ctx_placed, 1)
                    nc.scalar.activation(xnT[:, MEM:], projection_bank(b, "xnT")[:, :], ACT.Copy).then_inc(area0_drained, 1)
                if step == A_Q + READ:
                    act.wait_ge(area0_filled, AREA0[(b, "q")] + 1)
                    if b:
                        act.wait_ge(q_stacked[b - 1], NQ_DMA[b - 1])
                    nc.scalar.activation(qp[:, 0, :], area0[:, :], ACT.Copy).then_inc(q_first, 1)
                if step == A_Q + 3:
                    act.wait_ge(res_done, 2 * b + 1)
                    nc.scalar.activation(qp[:, 1, :], res[:, :], ACT.Copy).then_inc(q_second, 1)
                if step == A_K + READ:
                    act.wait_ge(area0_filled, AREA0[(b, "k")] + 1)
                    if b:
                        act.wait_ge(k_stacked[b - 1], NK_DMA)
                    nc.scalar.activation(kp[:, 0, MEM:], projection_bank(b, "k")[:, :], ACT.Copy).then_inc(k_first, 1)
                if step == A_K + 3:
                    act.wait_ge(res_done, 2 * b + 2)
                    nc.scalar.activation(kp[:, 1, MEM:], resk[:, :], ACT.Copy).then_inc(q_second, 1)
                if step == A_V + READ:
                    act.wait_ge(area0_filled, AREA0[(b, "v")] + 1)
                    if b < 2:
                        act.wait_ge(consts, (2, 4)[b])
                    if b >= 2:
                        act.wait_ge(pv_done, NGB * (b - 1))
                    nc.scalar.activation(v_aug[b % 2][:, 0:NT, :, 0:DH],
                                         projection_bank(b, "v")[:, :].rearrange("p (t h d) -> p t h d", t=NT, d=DH),
                                         ACT.Copy).then_inc(area0_drained, 1)

            def finish(b, n):
                uses = finish_uses(b, n)
                if uses:
                    act_waits, bank = AREA1[uses[0]] + 1, bank_of[uses[0]]
                if n == P_ATT:
                    act.wait_ge(area1_filled, act_waits)
                    nc.scalar.activation(attT[:, :], bank[:, :], ACT.Copy).then_inc(attT_done, 1)
                if n == P_T:
                    act.wait_ge(area1_filled, act_waits)
                    nc.scalar.activation(xn2T[:, :], bank[:, :], ACT.Copy).then_inc(xn2T_done, 1)
                if n == P_QC:
                    act.wait_ge(area1_filled, act_waits)
                    nc.scalar.activation(qcT[:, b, :], bank[:, :], ACT.Identity,
                                         bias=cb["q"][:, 0:1]).then_inc(qc_done, 1)
                if n == P_VD:
                    act.wait_ge(area1_filled, act_waits)
                    nc.scalar.activation(vd[:, :, :].rearrange("p t d -> p (t d)"), bank[:, :],
                                         ACT.Copy).then_inc(vd_done, 1)
                if n - 2 in P_SD:
                    c = P_SD.index(n - 2)
                    bank = bank_of[(b, "sd", c)]
                    act.wait_ge(sd_chain, 3 * (2 * b + c + 1))
                    nc.scalar.activation(pd[:, c, :], bank[:, :], ACT.Exp, bias=sd_max[:, c:c + 1], scale=SCALE,
                                         accum_out=sd_sum[:, c:c + 1]).then_inc(sd_exp, 1)
                if n in P_PT:
                    act.wait_ge(area1_filled, act_waits)
                    nc.scalar.activation(pdT[:, P_PT.index(n), :], bank[:, :], ACT.Copy).then_inc(pdT_done, 1)

            def exp_unit(group, u):
                m = UNITS * group + u
                act.wait_ge(scoreT_ready, m + 1)
                if u == 0 and group >= 2:
                    act.wait_ge(pv_done, group - 1)
                cols = (COLS[0], COLS[1], AT[4] + COLS[4])[u // HG]
                nc.scalar.activation(probs[group % 2][:, u, 0:cols], scoreT_bank[m % 2][:, 0:cols], ACT.Exp,
                                     scale=SCALE).then_inc(exp_done, 1)

            def copy_oT(group):
                act.wait_ge(pv_done, group + 1)
                b, gl = divmod(group, NGB)
                if b:
                    act.wait_ge(area1_filled, AREA1[(b - 1, "tok", NT - 1)] + 1)
                nc.scalar.activation(oT[:, gl, :], pv_bank[:, :], ACT.Copy).then_inc(oT_copied, 1)

            for step in range(A_END):
                project(0, step)
            for step in range(A_K):
                project(1, step)
            for slot in range(-LEAD, SLOTS):
                for tick in range(TICKS):
                    if tick == 0 and 2 <= slot:
                        copy_oT(slot - 2)
                    if 0 <= slot < NGROUPS and tick >= PROBS_TICK:
                        exp_unit(slot, tick - PROBS_TICK)
                    if (slot, tick - READ) in SLOT_QUERY_USES:
                        slot_queries(SLOT_QUERY_USES[slot, tick - READ])
                    b, n = projection_step(slot, tick)
                    if b is not None:
                        project(b, n)
                    b, n = finish_step(slot, tick - READ)
                    if b is not None:
                        finish(b, n)
            for n in range(P_END):
                finish(B - 1, n)

            act.wait_ge(pool_const, 1)
            nc.scalar.activation(table_probe[:, :], mhalf[:, 0:1], ACT.Silu)
            act.wait_ge(oh_ready, 2)
            act.wait_ge(hT_zeroed, 1)
            nc.scalar.activation(hT[:, :, 0:B], area1[:, 0:B * S].rearrange("p (b e) -> p e b", b=B),
                                 ACT.Copy).then_inc(hT_copied, 1)
            nc.scalar.activation(o_T[:, :], area1[:, B * S:2 * B * S], ACT.Copy).then_inc(hT_copied, 1)

            def copy_uvT(g):
                act.wait_ge(uvT_ready, g + 1)
                if g >= 2:
                    act.wait_ge(y_ready, g - 1)
                nc.scalar.activation(uvT[g % 2], scoreT_bank[g % 2][:, :], ACT.Copy).then_inc(uvT_copied, 1)

            def silu(n):
                act.wait_ge(silu_in, n + 1)
                t = (ub, gb)[n % 2][n // 2 % 2]
                nc.scalar.activation(t, t, ACT.Silu).then_inc(silu_done, 1)

            for n in range(2 * NGB):
                silu(n)
                if n >= 3 and n % 2:
                    copy_uvT((n - 3) // 2)
            copy_uvT(NGB - 1)
            nc.scalar.activation(table_probe[:, :], mhalf[:, 0:1], ACT.Exp)
            act.wait_ge(kcT_ready, 1)
            nc.scalar.activation(kcT[:, :, :].rearrange("p b s -> p (b s)"), area0[:, 0:B * S], ACT.Identity,
                                 bias=cb["k"][:, 0:1]).then_inc(kcT_copied, 1)
            nc.scalar.activation(vcT[:, :, :].rearrange("p b s -> p (b s)"), area0[:, B * S:2 * B * S], ACT.Identity,
                                 bias=cb["v"][:, 0:1]).then_inc(kcT_copied, 1)
            def c_exponentiate(pair):
                act.wait_ge(c_shifted, pair + 1)
                nc.scalar.activation(c_exp[pair % 3], c_exp[pair % 3], ACT.Exp, scale=SCALE).then_inc(c_exped, 1)

            def c_copy(pair):
                act.wait_ge(c_transposed, pair + 1)
                if pair >= 2:
                    act.wait_ge(c_mixed, pair - 1)
                nc.scalar.activation(c_probT[pair % 2], scoreT_bank[pair % 2][:, :], ACT.Copy).then_inc(c_copied, 1)

            def mix_copy(pair):
                act.wait_ge(c_mixed, pair + 1)
                if pair >= 2:
                    act.wait_ge(out_sent[pair % 2], 16 * (pair // 2))
                nc.scalar.activation(y[:, pair % 2, :, :].rearrange("p t d -> p (t d)"),
                                     (area0, area1)[pair % 2][:, 0:2 * D], ACT.Copy).then_inc(mix_copied, 1)

            c_exponentiate(0)
            c_exponentiate(1)
            for c in range(2):
                act.wait_ge(vo_ready, c + 1)
                nc.scalar.activation(vo[:, 2 * c:2 * c + 2, :, :].rearrange("p b c d -> p (b c d)"),
                                     (area1, pv_bank)[c][:, :], ACT.Copy).then_inc(vo_copied, 1)
            for pair in range(2 * B):
                if pair >= 2:
                    c_exponentiate(pair)
                if 0 <= pair - 3 < POOL_PAIRS:
                    mix_copy(pair - 3)
                if pair:
                    c_copy(pair - 1)
            c_copy(2 * B - 1)
            for pair in range(2 * B - 3, POOL_PAIRS):
                mix_copy(pair)

        @block.tensor
        def _(pe):
            wv = wkv[:, D:2 * D]
            shift_bank = area0[:, :].bitcast(BF16)

            def use0(name):
                if AREA0[name]:
                    pe.wait_ge(area0_drained, AREA0[name])

            def use1(name):
                if previous[name] is not None:
                    pe.wait_ge(*read(previous[name]))

            pe.wait_ge(pool_const, 3)
            pe.wait_ge(ctx_in_sem, 16)
            nc.tensor.transpose(area0[:, 0:P], ctx_in[:, :], ident[:, :]).then_inc(area0_filled, 1)
            pe.wait_ge(cols_done, 4)
            use0("kmem")
            nc.tensor.matmul(area0[:, 0:P], wk_cols[:, :], ctxT[:, :, :].rearrange("p b m -> p (b m)"),
                             start=True, stop=True).then_inc(area0_filled, 1)

            def slot_queries(name):
                use0(name)
                queries = qd_heads[:, :, :].rearrange("p h s -> p (h s)")
                if name == "slotT":
                    pe.wait_ge(slot_w_in, 16 * 4)
                    mm = nc.tensor.transpose(area0[:, 0:S], slots[:, :], ident[0:S, 0:S])
                elif name == "slotq":
                    mm = nc.tensor.matmul(area0[:, 0:S], dw["q"][:, :], slotsT[:, :], start=True, stop=True)
                elif name == "wkT":
                    pe.wait_ge(late_w_in, LATE_DMA)
                    mm = nc.tensor.transpose(area0[:, 0:D], dw["k"][:, :], ident[:, :])
                else:
                    pe.wait_ge(slotq_done, 1)
                    nc.tensor.matmul(area0[:, 0:2 * P], wkT, queries, start=True, stop=True)
                    for c in range(2):
                        mm = nc.tensor.matmul(area0[:, 2 * P + c:2 * P + c + 1], queries[:, P * c:P * (c + 1)],
                                              db["k"][:, 0:1], start=True, stop=True)
                mm.then_inc(area0_filled, 1)

            def project(b, step):
                if step in PROJ_USES:
                    bank = projection_bank(b, PROJ_USES[step])
                    if bank is area0:
                        use0((b, PROJ_USES[step]))
                if step == A_T:
                    pe.wait_ge(norm_done, b + 1)
                    for t in range(NT):
                        mm = nc.tensor.transpose(bank[:, P * t:P * (t + 1)], xn[:, t, :], ident[:, :])
                    mm.then_inc(area0_filled, 1)
                if step == A_Q:
                    nc.tensor.matmul(bank[:, :], wq_cols[:, :], xnT[:, MEM:], start=True, stop=True).then_inc(area0_filled, 1)
                if step == A_K:
                    nc.tensor.matmul(bank[:, :], wk_cols[:, :], xnT[:, MEM:], start=True, stop=True).then_inc(area0_filled, 1)
                if step == A_V:
                    for t in range(NT):
                        mm = nc.tensor.matmul(bank[:, P * t:P * (t + 1)], xnT[:, P * t:P * (t + 1)], wv,
                                              start=True, stop=True)
                    mm.then_inc(area0_filled, 1)
                if step == A_VLAST:
                    nc.tensor.matmul(bank[:, 0:D], xnT[:, KEYS - P:KEYS], wv, start=True, stop=True).then_inc(area0_filled, 1)

            def score_unit(group, k):
                n = TICKS * group + k
                b, gl = divmod(group, NGB)
                tile, heads = unit_of_scores(group, k)
                if k == 0 and gl == 0:
                    pe.wait_ge(q_stacked[b], NQ_DMA[b])
                    pe.wait_ge(k_stacked[b], NK_DMA)
                    if b < 2:
                        pe.wait_ge(stack_init, 32 * (b + 1))
                        pe.wait_ge(q_zeroed, b + 1)
                    if b == 0:
                        pe.wait_ge(pool_const, CAUSAL_MADE)
                        pe.wait_ge(area0_drained, AREA0[(0, "vlast")] + 1)
                if n >= 3:
                    pe.wait_ge(scores_reduced, n - 2)
                bank = score_bank[n % 3]
                q, keys = q_stack[b % 2], k_stack[b % 2]
                cols = scores_cols(tile)
                first = True

                def masked(h, t, at, lo, hi):
                    nonlocal first
                    nc.tensor.matmul(bank[:, at:at + hi - lo], q[:, h // 2, P * t:P * (t + 1)], keys[:, h, lo:hi],
                                     start=first, stop=False, skip_group_check=True)
                    first = False
                    d = MEM + P * t
                    a = max(lo, d)
                    return nc.tensor.matmul(bank[:, at + a - lo:at + hi - lo], identb[:, :], causal[:, a - d:hi - d],
                                            start=False, stop=True, skip_group_check=True)

                for m, hj in enumerate(heads):
                    mm = masked(HG * gl + hj, tile, cols * m, 0, cols)
                if tile == 0:
                    for m, hj in enumerate(heads):
                        mm = masked(HG * gl + hj, NT - 1, cols * len(heads) + MEM * m, 512, KEYS)
                mm.then_inc(scores_ready, 1)

            def shift_rows(group):
                use0(("shift", group))
                pe.wait_ge(max_chain, 3 * (group + 1))
                for t in range(NT):
                    mm = nc.tensor.transpose(shift_bank[0:8, P * t:P * (t + 1)],
                                             shift[group % 2][:, t].rearrange("p g a s -> p (g a s)"), identb[:, :])
                mm.then_inc(area0_filled, 1)

            def scoreT_unit(group, u):
                m = UNITS * group + u
                b, gl = divmod(group, NGB)
                if u == 0:
                    pe.wait_ge(shift_in[group % 2], 16 * (group // 2 + 1))
                if m >= 2:
                    pe.wait_ge(exp_done, m - 1)
                bank = scoreT_bank[m % 2]
                q, keys = q_stack[b % 2], k_stack[b % 2]

                h = HG * gl + u % HG
                for j in ((0,), (1,), (2, 3, 4))[u // HG]:
                    first_key, first_query = KEY_TILES[j]
                    mm = nc.tensor.matmul(bank[:, AT[j]:AT[j] + COLS[j]], keys[:, h, first_key:first_key + P],
                                          q[:, h // 2, first_query:T], start=(AT[j] == 0), stop=True,
                                          skip_group_check=True)
                mm.then_inc(scoreT_ready, 1)

            def pv_piece(group, piece):
                b, gl = divmod(group, NGB)
                pr, v = probs[group % 2], v_aug[b % 2]
                if piece == 0:
                    pe.wait_ge(exp_done, UNITS * (group + 1))
                    if gl == 0:
                        pe.wait_ge(area0_drained, AREA0[(b, "vlast")] + 1)
                    if group:
                        pe.wait_ge(oT_copied, group)
                    else:
                        pe.wait_ge(pv_cleared, 1)
                j = piece
                pe.wait_ge(diag_done, 3 * group + (1, 2, 3, 3, 3)[j])
                for hj in range(HG):
                    mm = nc.tensor.matmul(pv_bank[32 * hj:32 * hj + DH + 1, KEY_TILES[j][1]:T],
                                          v[:, j, HG * gl + hj, :],
                                          pr[:, HG * min(j, 2) + hj, AT[j]:AT[j] + COLS[j]],
                                          start=(j == 0), stop=(j == KT - 1), skip_group_check=True)
                if j == KT - 1:
                    mm.then_inc(pv_done, 1)

            def keep_clock(products):
                for _ in range(products):
                    nc.tensor.matmul(pv_bank[:, :], identb[:, :], kp[:, 0, 0:T], start=True, stop=True)

            def finish(b, n):
                if b == B - 1:
                    keep_clock(FILL.get(n, 0))
                for name in finish_uses(b, n):
                    use1(name)
                    bank = bank_of[name]
                    if b == B - 2 and bank is not area1:
                        pe.wait_ge(scores_reduced, TICKS * NGROUPS)
                if n in P_TOK:
                    t = P_TOK.index(n)
                    pe.wait_ge(oT_copied, NGB * (b + 1))
                    for gl in range(NGB):
                        mm = nc.tensor.transpose(bank[:, P * gl:P * (gl + 1)], oT[:, gl, P * t:P * (t + 1)], ident[:, :])
                elif n == P_ATT or n == P_T:
                    if n == P_T:
                        pe.wait_ge(norm2_done, b + 1)
                    else:
                        pe.wait_ge(*read((b, "tok", NT - 1)))
                        if b == 0:
                            pe.wait_ge(slot_w_in, 16 * 4)
                    for t in range(NT):
                        mm = nc.tensor.transpose(bank[:, P * t:P * (t + 1)], att[:, t, :], ident[:, :])
                elif n == P_OUT:
                    pe.wait_ge(attT_done, b + 1)
                    for t in range(NT):
                        mm = nc.tensor.matmul(bank[:, P * t:P * (t + 1)], attT[:, P * t:P * (t + 1)], wout[:, :],
                                              start=True, stop=True)
                elif n == P_QC:
                    pe.wait_ge(xn2T_done, b + 1)
                    mm = nc.tensor.matmul(bank[:, :], cw["q"][:, :], xn2T[:, :], start=True, stop=True)
                elif n == P_VD:
                    for t in range(NT):
                        mm = nc.tensor.matmul(bank[:, P * t:P * (t + 1)], xn2T[:, P * t:P * (t + 1)], dw["v"][:, :],
                                              start=True, stop=True)
                elif n in P_SD:
                    c = P_SD.index(n)
                    pe.wait_ge(area0_drained, AREA0["fold"] + 1)
                    pe.wait_ge(xn2T_done, b + 1)
                    mm = nc.tensor.matmul(bank[:, :], qd_fold[:, P * c:P * (c + 1)], xn2T[:, :], start=True, stop=True)
                elif n in P_PT:
                    c = P_PT.index(n)
                    pe.wait_ge(sd_exp, 2 * b + c + 1)
                    for t in range(NT):
                        mm = nc.tensor.transpose(bank[:, P * t:P * (t + 1)], pd[:, c, P * t:P * (t + 1)],
                                                 ident[:, :])
                elif n in P_PV:
                    c = P_PV.index(n)
                    pe.wait_ge(pdT_done, 2 * b + c + 1)
                    pe.wait_ge(vd_done, b + 1)
                    for t in range(NT):
                        mm = nc.tensor.matmul(bank[:, 0:D], pdT[:, c, P * t:P * (t + 1)], vd[:, t, :],
                                              start=(t == 0), stop=(t == NT - 1))
                elif n == P_SUM:
                    pe.wait_ge(od_done, 2 * b + 2)
                    pe.wait_ge(pool_const, CONSTS_MADE)
                    for c in range(2):
                        mm = nc.tensor.matmul(bank[:, 0:S], od[:, c, :], slot_sel[:, :], start=(c == 0), stop=(c == 1))
                else:
                    return
                mm.then_inc(area1_filled, 1)

            for step in range(A_END):
                project(0, step)
            for step in range(A_K):
                project(1, step)
            for slot in range(-LEAD, SLOTS):
                for tick in range(TICKS):
                    if slot + LEAD < NGROUPS:
                        score_unit(slot + LEAD, tick)
                    if 0 <= slot < NGROUPS and tick >= PROBS_TICK:
                        scoreT_unit(slot, tick - PROBS_TICK)
                    if 1 <= slot <= NGROUPS and tick in PV_TICKS:
                        pv_piece(slot - 1, PV_TICKS.index(tick))
                    if tick == SHIFT_TICK and slot > -LEAD and slot - 1 + LEAD < NGROUPS:
                        shift_rows(slot - 1 + LEAD)
                    if (slot, tick) in SLOT_QUERY_USES:
                        slot_queries(SLOT_QUERY_USES[slot, tick])
                    b, n = projection_step(slot, tick)
                    if b is not None:
                        project(b, n)
                    b, n = finish_step(slot, tick)
                    if b is not None:
                        finish(b, n)
            for n in range(P_END):
                finish(B - 1, n)

            pe.wait_ge(ad_done, B)
            nc.tensor.matmul(area0[0:B * S, 0:D], adT[:, :, :].rearrange("p b s -> p (b s)"), dw["o"][:, :],
                             start=True, stop=True).then_inc(oh_ready, 1)
            keep_clock(8)
            pe.wait_ge(o_chain, 7)
            nc.tensor.transpose(area1[:, 0:B * S], h_rows[:, :], ident[0:B * S, 0:B * S])
            nc.tensor.transpose(area1[:, B * S:2 * B * S], o_rows[:, :], ident[0:B * S, 0:B * S]).then_inc(oh_ready, 1)
            pe.wait_ge(hT_copied, 1)
            up_banks = [*score_bank, area0, area1]

            def up(g, k):
                n = 2 * g + k
                if n == 0:
                    pe.wait_ge(w1_in, 16 * S)
                    pe.wait_ge(wg_in, 16 * S)
                if n == 4:
                    pe.wait_ge(hT_copied, 2)
                if n >= len(up_banks):
                    pe.wait_ge(silu_in, n - len(up_banks) + 1)
                for j in range(HG):
                    mm = nc.tensor.matmul(up_banks[n % len(up_banks)][32 * j:32 * j + 32, :], hT[:, HG * g + j, :],
                                          (w1, wg)[k][HG * g + j], start=True, stop=True)
                mm.then_inc(up_ready, 1)

            def turn(g):
                pe.wait_ge(uv_done, g + 1)
                if g >= 2:
                    pe.wait_ge(uvT_copied, g - 1)
                for c in range(FC):
                    mm = nc.tensor.transpose(scoreT_bank[g % 2][:, P * c:P * (c + 1)], uv[g % 2][:, c::FC], ident[:, :])
                mm.then_inc(uvT_ready, 1)

            def down(g):
                pe.wait_ge(uvT_copied, g + 1)
                if g == 0:
                    pe.wait_ge(w2_in, 16 * S)
                if g == 1:
                    pe.wait_ge(silu_in, 4)
                if g >= 2:
                    pe.wait_ge(y_copied, g - 1)
                for c in range(FC):
                    for j in range(HG):
                        e = HG * g + j
                        mm = nc.tensor.matmul((pv_bank, area0)[g % 2][32 * j:32 * j + 32, 0:D],
                                              uvT[g % 2][:, P * c + 32 * j:P * c + 32 * j + 32],
                                              w2[e][:, c, :], start=(c == 0), stop=(c == FC - 1),
                                              skip_group_check=True)
                mm.then_inc(y_ready, 1)

            def turn_y(g):
                pe.wait_ge(y_copied, g + 1)
                if g == 0:
                    pe.wait_ge(silu_in, 5)
                nc.tensor.transpose(area1[:, P * g:P * (g + 1)], ysb[:, P * g:P * (g + 1)],
                                    ident[:, :]).then_inc(yT_ready, 1)

            for g, k in ((0, 0), (0, 1), (1, 0), (1, 1), (2, 0)):
                up(g, k)
            turn(0)
            up(2, 1)
            down(0)
            turn(1)
            up(3, 0)
            down(1)
            up(3, 1)
            turn(2)
            turn_y(0)
            turn_y(1)
            turn(3)
            down(2)
            down(3)
            turn_y(2)
            turn_y(3)
            pe.wait_ge(o2_done, 1)
            o2 = o2T[:, :, :].rearrange("p b s -> p (b s)")
            nc.tensor.matmul(area0[:, 0:B * S], cw["k"][:, :], o2, start=True, stop=True)
            nc.tensor.matmul(area0[:, B * S:2 * B * S], cw["v"][:, :], o2, start=True, stop=True).then_inc(kcT_ready, 1)

            keep_clock(3)

            def c_scores(pair):
                b, half = divmod(pair, 2)
                pe.wait_ge(kheads_done, b + 1)
                if pair == 3:
                    pe.wait_ge(vo_copied, 2)
                if pair >= 4:
                    pe.wait_ge(c_shifted, pair - 3)
                for r in range(2):
                    t = 2 * half + r
                    mm = nc.tensor.matmul(c_banks[pair % 4][:, 256 * r:256 * (r + 1)], qcT[:, b, P * t:P * (t + 1)],
                                          kc_heads[:, b, :, :].rearrange("p h s -> p (h s)"), start=True, stop=True)
                mm.then_inc(c_scored, 1)

            def c_transpose(pair):
                pe.wait_ge(c_normed, pair + 1)
                if pair >= 2:
                    pe.wait_ge(c_copied, pair - 1)
                for c in range(4):
                    mm = nc.tensor.transpose(scoreT_bank[pair % 2][:, P * c:P * (c + 1)],
                                             c_prob[pair % 2][:, P * c:P * (c + 1)], ident[:, :])
                mm.then_inc(c_transposed, 1)

            def c_mix(pair):
                b, half = divmod(pair, 2)
                pe.wait_ge(c_copied, pair + 1)
                pe.wait_ge(vo_copied, 2)
                if pair >= 2:
                    pe.wait_ge(mix_copied, pair - 1)
                for r in range(2):
                    for c in range(2):
                        mm = nc.tensor.matmul((area0, area1)[pair % 2][:, D * r:D * (r + 1)],
                                              c_probT[pair % 2][:, P * (2 * r + c):P * (2 * r + c + 1)],
                                              vo[:, b, c, :], start=(c == 0), stop=(c == 1))
                mm.then_inc(c_mixed, 1)

            c_scores(0)
            c_scores(1)
            c_scores(2)
            pe.wait_ge(vheads_done, B)
            for b in range(B):
                for c in range(2):
                    mm = nc.tensor.matmul((area1, pv_bank)[b // 2][:, D * (2 * (b % 2) + c):D * (2 * (b % 2) + c + 1)],
                                          vc_heads[:, b, 8 * c:8 * c + 8, :].rearrange("p h s -> p (h s)"),
                                          cw["o"][:, :], start=True, stop=True)
                if b % 2:
                    mm.then_inc(vo_ready, 1)
            for pair in range(2 * B):
                if pair + 3 < 2 * B:
                    c_scores(pair + 3)
                c_transpose(pair)
                if pair:
                    c_mix(pair - 1)
            c_mix(2 * B - 1)

        @block.vector
        def _(dve):
            U32 = mybir.dt.uint32
            zeros = k0.bitcast(U32)
            nc.vector.memset(zeros[:, 0:zeros.shape[1] // 2], 0).then_inc(kzero_done, 1)
            nc.vector.memset(one_rows[:, :], 1.0).then_inc(consts, 1)

            def norm_stats(n, src, st, m, done, per_tile):
                for t in range(NT):
                    nc.vector.bn_stats(st[:, t, :], src[:, t, :]).then_inc(per_tile, 1)
                dve.wait_ge(per_tile, NT * (n + 1))
                for t in range(NT):
                    ins = nc.vector.bn_aggr(m[:, t, :], st[:, t, :])
                ins.then_inc(done, 1)

            def normalise(n, src, dst, m, r, s_r, done):
                dve.wait_ge(s_r, n + 1)
                for t in range(NT):
                    ins = nc.vector.tensor_scalar(dst[:, t, :], src[:, t, :], m[:, t, 0:1], r[:, t:t + 1],
                                                  ALU.subtract, ALU.mult)
                ins.then_inc(done, 1)

            def values_ones(n):
                nc.vector.memset(v_aug[n][:, NT, :, :], 0.0).then_inc(v_zero, 1)
                dve.wait_ge(v_zero, n + 1)
                nc.vector.memset(v_aug[n][P - MEM:P, NT, :, DH:DH + 1], 1.0)
                nc.vector.memset(v_aug[n][:, 0:NT, :, DH:DH + 1], 1.0).then_inc(consts, 1)

            def project(b, step):
                if step == A_STATS:
                    dve.wait_ge(x_in0 if b == 0 else x_in1, 16 if b == 0 else 16 * (B - 1))
                    norm_stats(b, x[:, b, :, :], stats, mv, stats_done, tile_stats)
                if step == A_NORM:
                    if b:
                        dve.wait_ge(area0_filled, AREA0[(b - 1, "xnT")] + 1)
                    normalise(b, x[:, b, :, :], xn, mv, rstd, rstd_done, norm_done)
                if step == A_Q + 2:
                    dve.wait_ge(q_first, b + 1)
                    if b:
                        dve.wait_ge(q_third, 2 * b - 1)
                    nc.vector.tensor_tensor(res[:, :], area0[:, :], qp[:, 0, :], ALU.subtract).then_inc(res_done, 1)
                    dve.wait_ge(res_done, 2 * b + 1)
                    dve.sem_inc(area0_drained, 1)
                if step == A_K + 2:
                    dve.wait_ge(k_first, b + 1)
                    if b:
                        dve.wait_ge(q_third, 2 * b)
                    nc.vector.tensor_tensor(resk[:, :], projection_bank(b, "k")[:, :], kp[:, 0, MEM:],
                                            ALU.subtract).then_inc(res_done, 1)
                    dve.wait_ge(res_done, 2 * b + 2)
                    dve.sem_inc(area0_drained, 1)
                if step == A_VLAST + READ:
                    dve.wait_ge(area0_filled, AREA0[(b, "vlast")] + 1)
                    dve.wait_ge(consts, (2, 4)[min(b, 1)])
                    if b >= 2:
                        dve.wait_ge(pv_done, NGB * (b - 1))
                    rows = slice(P - MEM, P)
                    nc.vector.tensor_copy(v_aug[b % 2][rows, NT, :, 0:DH],
                                          projection_bank(b, "vlast")[rows, 0:D].rearrange("p (h d) -> p h d", h=H))\
                        .then_inc(area0_drained, 1)

            def reduce_unit(group, k):
                n = TICKS * group + k
                tile, heads = unit_of_scores(group, k)
                dve.wait_ge(scores_ready, n + 1)
                bank = score_bank[n % 3]
                m, cols = rowmax[group % 2], scores_cols(tile)
                if tile == 0:
                    nc.vector.tensor_reduce(m[:, 0, :, heads[0] // 2], bank[:, 0:2 * cols].rearrange("p (a n) -> p a n", a=2),
                                            AX.X, ALU.max)
                    nc.vector.tensor_reduce(tailmax[group % 2][:, :, heads[0] // 2],
                                            bank[:, 2 * cols:2 * cols + 2 * MEM].rearrange("p (a n) -> p a n", a=2),
                                            AX.X, ALU.max).then_inc(scores_reduced, 1)
                else:
                    h = heads[0]
                    nc.vector.tensor_reduce(m[:, tile, h % 2, h // 2:h // 2 + 1], bank[:, 0:cols], AX.X,
                                            ALU.max).then_inc(scores_reduced, 1)

            def shift_of(group):
                m, sh = rowmax[group % 2], shift[group % 2]
                dve.wait_ge(scores_reduced, TICKS * (group + 1))
                if group >= 2:
                    dve.wait_ge(area0_filled, AREA0[("shift", group - 2)] + 1)
                last = m[:, NT - 1, :, :].rearrange("p g s -> p (g s)")
                nc.vector.tensor_tensor(last, last, tailmax[group % 2][:, :, :].rearrange("p g s -> p (g s)"),
                                        ALU.max).then_inc(max_chain, 1)
                dve.wait_ge(max_chain, 3 * group + 1)
                mm = m[:, :, :, :].rearrange("p t g s -> p (t g) s")
                hi = sh[:, :, :, 0, :].rearrange("p t g s -> p (t g) s")
                lo = sh[:, :, :, 1, :].rearrange("p t g s -> p (t g) s")
                nc.vector.tensor_scalar(hi, mm, -1.0, None, ALU.mult).then_inc(max_chain, 1)
                dve.wait_ge(max_chain, 3 * group + 2)
                nc.vector.scalar_tensor_tensor(out=lo, in0=mm, scalar=-1.0, in1=hi, op0=ALU.mult,
                                               op1=ALU.subtract).then_inc(max_chain, 1)

            def shift_copy(group):
                dve.wait_ge(area0_filled, AREA0[("shift", group)] + 1)
                if group >= 2:
                    dve.wait_ge(shift_in[group % 2], 16 * (group // 2))
                nc.vector.tensor_copy(shiftT[group % 2][:, :], area0[:, :].bitcast(BF16)[0:8, 0:T])\
                    .then_inc(area0_drained, 1)

            def finish(b, n):
                for name in finish_uses(b, n):
                    filled, bank = AREA1[name] + 1, bank_of[name]
                if n in P_TOK:
                    t = P_TOK.index(n)
                    if t == 0 and b:
                        dve.wait_ge(att_done, NT * b)
                    heads = bank[:, :].rearrange("p (h c) -> p h c", h=H)
                    dve.wait_ge(area1_filled, filled)
                    nc.vector.reciprocal(rden[:, t, :], heads[:, :, DH]).then_inc(rden_done, 1)
                    dve.wait_ge(rden_done, NT * b + t + 1)
                    nc.vector.tensor_tensor(att[:, t, :].rearrange("p (h d) -> p h d", h=H), heads[:, :, 0:DH],
                                            rden[:, t, :].unsqueeze(2).broadcast_to([P, H, DH]),
                                            ALU.mult).then_inc(att_done, 1)
                if n == P_OUT:
                    dve.wait_ge(area1_filled, filled)
                    dve.wait_ge(x_b, b + 1)
                    xb = x[:, b, :, :].rearrange("p t d -> p (t d)")
                    nc.vector.tensor_tensor(xb, bank[:, :], xb, ALU.add).then_inc(x_added, 1)
                if n == P_STATS:
                    dve.wait_ge(x_added, b + 1)
                    norm_stats(b, x[:, b, :, :], stats2, mv2, stats2_done, tile_stats2)
                if n == P_NORM:
                    normalise(b, x[:, b, :, :], xn2, mv2, rstd2, rstd2_done, norm2_done)
                if n in P_SD:
                    c = P_SD.index(n)
                    dve.wait_ge(area1_filled, filled)
                    nc.vector.tensor_reduce(sd_max[:, c:c + 1], bank[:, :], AX.X, ALU.max,
                                            negate=True).then_inc(sd_chain, 1)
                    dve.wait_ge(fold_copied, 1)
                    dve.wait_ge(sd_chain, 3 * (2 * b + c) + 1)
                    nc.vector.tensor_scalar(sd_max[:, c:c + 1], sd_max[:, c:c + 1], key_bias[:, c:c + 1], None,
                                            ALU.subtract).then_inc(sd_chain, 1)
                    dve.wait_ge(sd_chain, 3 * (2 * b + c) + 2)
                    nc.vector.tensor_scalar(sd_max[:, c:c + 1], sd_max[:, c:c + 1], key_bias[:, c:c + 1], SCALE,
                                            ALU.add, ALU.mult).then_inc(sd_chain, 1)
                if n in P_PV:
                    c = P_PV.index(n)
                    dve.wait_ge(area1_filled, filled)
                    dve.wait_ge(sd_exp, 2 * b + c + 1)
                    nc.vector.reciprocal(sd_r[:, c:c + 1], sd_sum[:, c:c + 1]).then_inc(sd_recip, 1)
                    dve.wait_ge(sd_recip, 2 * b + c + 1)
                    nc.vector.scalar_tensor_tensor(
                        out=od[:, c, :].rearrange("p (h d) -> p h d", h=H),
                        in0=bank[:, 0:D].rearrange("p (h d) -> p h d", h=H), scalar=sd_r[:, c:c + 1],
                        in1=slot_head[:, c, :].unsqueeze(2).broadcast_to([P, H, DH]),
                        op0=ALU.mult, op1=ALU.mult).then_inc(od_done, 1)
                if n == P_SUM:
                    dve.wait_ge(area1_filled, filled)
                    nc.vector.tensor_scalar(adT[:, b, :], bank[:, 0:S], db["v"][:, 0:1], None,
                                            ALU.add).then_inc(ad_done, 1)

            project(0, A_STATS)
            nc.vector.memset(pv_bank[:, :], 0.0).then_inc(pv_cleared, 1)
            project(0, A_NORM)
            dve.wait_ge(kmem_part, 1)
            nc.vector.tensor_tensor(resk[:, 0:P], area0[:, 0:P], kmem[:, 0, :], ALU.subtract).then_inc(kmem_part, 1)
            dve.wait_ge(kmem_part, 2)
            dve.sem_inc(area0_drained, 1)
            nc.vector.tensor_copy(kmem[:, 1, :], resk[:, 0:P]).then_inc(kmem_part, 1)
            dve.wait_ge(kmem_part, 3)
            nc.vector.tensor_tensor(kmem[:, 2, :], resk[:, 0:P], kmem[:, 1, :], ALU.subtract).then_inc(kmem_part, 1)
            nc.vector.memset(q0[SHIFT_ROW:P, :].bitcast(U32), 0).then_inc(q_zeroed, 1)
            values_ones(0)
            dve.wait_ge(kmem_part, 4)
            for step in range(A_NORM + 1, A_END):
                project(0, step)
            project(1, A_STATS)
            nc.vector.memset(zero_rows[:, :], 0.0).then_inc(consts, 1)
            for step in range(A_STATS + 1, A_NORM + 1):
                project(1, step)
            nc.vector.memset(q1[SHIFT_ROW:P, :].bitcast(U32), 0).then_inc(q_zeroed, 1)
            values_ones(1)
            for step in range(A_NORM + 1, A_K):
                project(1, step)
            for slot in range(-LEAD, SLOTS):
                for tick in range(TICKS):
                    if slot + LEAD < NGROUPS:
                        reduce_unit(slot + LEAD, tick)
                    if tick == MAX_TICK and slot > -LEAD and slot - 1 + LEAD < NGROUPS:
                        shift_of(slot - 1 + LEAD)
                    if tick == SHIFT_TICK + READ and slot > -LEAD and slot - 1 + LEAD < NGROUPS:
                        shift_copy(slot - 1 + LEAD)
                    b, n = projection_step(slot, tick)
                    if b is not None:
                        project(b, n)
                    b, n = finish_step(slot, tick - READ)
                    if b is not None:
                        finish(b, n)
            dve.wait_ge(pv_done, NGROUPS - 1)
            nc.vector.memset(hT, 0.0).then_inc(hT_zeroed, 1)
            for n in range(P_END):
                finish(B - 1, n)

            dve.wait_ge(oh_ready, 1)
            dve.wait_ge(o_pool, 1)
            nc.vector.tensor_tensor(o_rows[:, :], area0[0:B * S, 0:D], slot_rows[:, :], ALU.add).then_inc(o_chain, 1)
            dve.wait_ge(o_chain, 1)
            nc.vector.bn_stats(o_stats[:, :], o_rows[:, :]).then_inc(o_chain, 1)
            dve.wait_ge(o_chain, 2)
            nc.vector.bn_aggr(o_mv[:, :], o_stats[:, :]).then_inc(o_chain, 1)
            dve.wait_ge(o_pool, 3)
            nc.vector.tensor_scalar(h_rows[:, :], o_rows[:, :], o_mv[:, 0:1], rstd[0:B * S, 0:1], ALU.subtract,
                                    ALU.mult).then_inc(o_chain, 1)
            dve.wait_ge(o_chain, 4)
            nc.vector.tensor_tensor(h_rows[:, :], h_rows[:, :], ln_g[:, :], ALU.mult).then_inc(o_chain, 1)
            dve.wait_ge(o_chain, 5)
            nc.vector.tensor_tensor(h_rows[:, :], h_rows[:, :], ln_b[:, :], ALU.add).then_inc(o_chain, 1)
            nc.vector.tensor_tensor(o_rows[:, :], o_rows[:, :], b2_rows[:, :], ALU.add).then_inc(o_chain, 1)
            up_banks = [*score_bank, area0, area1]

            def add_bias(g, k):
                n = 2 * g + k
                if n == 0:
                    dve.wait_ge(b1_in, 16 * 2 * HG)
                dve.wait_ge(up_ready, n + 1)
                nc.vector.tensor_tensor((ub, gb)[k][g % 2], up_banks[n % len(up_banks)][:, :], (b1_rows, bg_rows)[k][:, g, :],
                                        ALU.add).then_inc(silu_in, 1)

            def times(g):
                dve.wait_ge(silu_done, 2 * g + 2)
                if g >= 2:
                    dve.wait_ge(uvT_ready, g - 1)
                nc.vector.tensor_tensor(uv[g % 2], ub[g % 2], gb[g % 2], ALU.mult).then_inc(uv_done, 1)

            for g in range(NGB):
                if g >= 2:
                    dve.wait_ge(uv_done, g - 1)
                add_bias(g, 0)
                if g:
                    times(g - 1)
                add_bias(g, 1)
            times(NGB - 1)
            for g in range(NGB):
                dve.wait_ge(y_ready, g + 1)
                nc.vector.tensor_copy(ysb[:, P * g:P * (g + 1)], (pv_bank, area0)[g % 2][:, 0:P]).then_inc(y_copied, 1)
            dve.wait_ge(yT_ready, NGB)
            nc.vector.tensor_tensor(o2T[:, :, :].rearrange("p b (g j) -> p b g j", g=NGB),
                                    area1[:, :].rearrange("p (g j r) -> p r g j", g=NGB, j=HG)[:, 0:B, :, :],
                                    o_T[:, :].rearrange("p (b g j) -> p b g j", b=B, g=NGB), ALU.add).then_inc(o2_done, 1)

            dve.wait_ge(kcT_copied, 1)
            def key_heads(b):
                nc.vector.tensor_tensor(kc_heads[:, b, :, :], kcT[:, b, :].unsqueeze(1).broadcast_to([P, H, S]),
                                        head_of[:, :].unsqueeze(2).broadcast_to([P, H, S]),
                                        ALU.mult).then_inc(kheads_done, 1)

            def c_shift(pair):
                bank = c_banks[pair % 4][:, :].rearrange("p (a s) -> p a s", s=S)
                m = c_max[pair % 2]
                dve.wait_ge(c_scored, pair + 1)
                nc.vector.tensor_reduce(m[:, :], bank, AX.X, ALU.max).then_inc(c_reduced, 1)
                dve.wait_ge(c_reduced, pair + 1)
                if pair >= 3:
                    dve.wait_ge(c_normed, pair - 2)
                nc.vector.tensor_tensor(c_exp[pair % 3].rearrange("p (a s) -> p a s", s=S), bank,
                                        m[:, :].unsqueeze(2).broadcast_to([P, 2 * H, S]),
                                        ALU.subtract).then_inc(c_shifted, 1)

            def c_sums(pair):
                dve.wait_ge(c_exped, pair + 1)
                if pair >= 2:
                    dve.wait_ge(c_normed, pair - 1)
                nc.vector.tensor_reduce(c_sum[pair % 2][:, :], c_exp[pair % 3].rearrange("p (a s) -> p a s", s=S),
                                        AX.X, ALU.add).then_inc(c_summing, 1)
                dve.wait_ge(c_summing, pair + 1)
                nc.vector.reciprocal(c_sum[pair % 2][:, :], c_sum[pair % 2][:, :]).then_inc(c_summed, 1)

            def c_result(pair):
                b, half = divmod(pair, 2)
                dve.wait_ge(c_mixed, pair + 1)
                dve.wait_ge(x_plus, b + 1)
                dve.wait_ge(out_sent[pair % 2], 16 * (pair // 2))
                nc.vector.tensor_tensor(y[:, pair % 2, :, :].rearrange("p t d -> p (t d)"),
                                        (area0, area1)[pair % 2][:, 0:2 * D],
                                        x[:, b, 2 * half:2 * half + 2, :].rearrange("p t d -> p (t d)"),
                                        ALU.add).then_inc(last_y_done, 1)

            key_heads(0)
            key_heads(1)
            c_shift(0)
            key_heads(2)
            key_heads(3)
            for pair in range(2 * B):
                if pair + 1 < 2 * B:
                    c_shift(pair + 1)
                c_sums(pair)
            for pair in range(POOL_PAIRS, 2 * B):
                c_result(pair)


INS = ["x", "ctx_1024", "L0_xattn_Wq", "L0_xattn_Wkv", "L0_xattn_Wout", "L0_xattn_bout", "L0_ffn_slot_query",
       "L0_ffn_d_Wq", "L0_ffn_d_Wk", "L0_ffn_d_Wv", "L0_ffn_d_Wo", "L0_ffn_d_bq", "L0_ffn_d_bk", "L0_ffn_d_bv",
       "L0_ffn_d_bo", "L0_ffn_c_Wq", "L0_ffn_c_Wk", "L0_ffn_c_Wv", "L0_ffn_c_Wo", "L0_ffn_c_bq", "L0_ffn_c_bk",
       "L0_ffn_c_bv", "L0_ffn_c_bo", "L0_ffn_e_ln_g", "L0_ffn_e_ln_b", "L0_ffn_e_W1", "L0_ffn_e_b1", "L0_ffn_e_Wg",
       "L0_ffn_e_bg", "L0_ffn_e_W2", "L0_ffn_e_b2"]


def kernel(**inputs):
    import numpy as np
    import concourse.bacc as bacc
    from concourse.bass_utils import run_bass_kernel_spmd

    nc = bacc.Bacc("TRN2", target_bir_lowering=False, num_devices=1)
    arrays, args = {}, {}
    for name in INS:
        a = np.ascontiguousarray(inputs[name])
        arrays[f"in_{name}"] = a
        args[name] = nc.dram_tensor(f"in_{name}", a.shape, mybir.dt.from_np(a.dtype), kind="ExternalInput").ap()
    out = nc.dram_tensor("out", (B, T, D), F32, kind="ExternalOutput").ap()
    program(nc, args, out)
    r = run_bass_kernel_spmd(nc, [arrays], core_ids=[0])
    return r.results[0]["out"]
```
